# Optimizing a Trainium2 kernel written in Bass

```python
import numpy as np
import jax
import jax.numpy as jnp

def _softmax(x, axis=-1):
    return jax.nn.softmax(x, axis=axis)

def _gelu(x):
    return jax.nn.gelu(x, approximate=True)

def _silu(x):
    return jax.nn.silu(x)

def _sigmoid(x):
    return jax.nn.sigmoid(x)

def _layernorm(x, axis=-1, eps=1e-05):
    m = jnp.mean(x, axis=axis, keepdims=True)
    v = jnp.var(x, axis=axis, keepdims=True)
    return (x - m) / jnp.sqrt(v + eps)

def _scatter_add(tgt, idx, src, axis=0):
    return tgt.at[idx].add(src)

def _segment_sum(src, seg, n):
    return jax.ops.segment_sum(src, seg, n)
kernel_name = 'mk_conv_attn_hybrid_d4_conv_nchw1024_r2_6c6211'

def setup_inputs(seed: int=0):
    np.random.seed(seed)
    _w = jnp.asarray

    def _rec_inputs():
        import jax
        import jax.numpy as jnp
        _gk = jax.random.key(seed)
        x = -0.0002928 + 1 * jax.random.normal(jax.random.fold_in(_gk, 1), (1, 512, 32, 32), jnp.float32)
        return x
    x = _rec_inputs()

    def _L0_conv_setup():
        import jax, jax.numpy as jnp
        import numpy as np
        EPS = 1e-05

        def _layernorm2d(x, w, b):
            mean = jnp.mean(x, axis=(-2, -1), keepdims=True)
            var = jnp.mean(jnp.square(x - mean), axis=(-2, -1), keepdims=True)
            return (x - mean) / jnp.sqrt(var + EPS) * w + b
        key = jax.random.key(seed)
        ks = jax.random.split(key, 6)
        b, seq, d = (1, 512, 32)
        x = jax.random.normal(ks[0], (b, seq, d, d), dtype=jnp.float32)
        log_A = jax.random.normal(ks[1], (d,), dtype=jnp.float32) * 0.02
        dt_w = jax.random.normal(ks[2], (1, d), dtype=jnp.float32) / np.sqrt(d)
        dt_b = jax.random.normal(ks[3], (1,), dtype=jnp.float32) * 0.01
        ln_w = jnp.ones((d, d), dtype=jnp.float32)
        ln_b = jnp.zeros((d, d), dtype=jnp.float32)
        return {'x': x, 'log_A': log_A, 'dt_w': dt_w, 'dt_b': dt_b, 'ln_w': ln_w, 'ln_b': ln_b}
    _L0_conv_all = _L0_conv_setup()
    _L0_conv_in = {k: v for k, v in _L0_conv_all.items() if k in ('log_A', 'dt_w', 'dt_b', 'ln_w', 'ln_b')}
    del _L0_conv_all

    def _L1_conv_setup():
        import jax, jax.numpy as jnp
        import numpy as np
        B, SEQ, D = (2, 512, 32)
        key = jax.random.key(seed)
        k1, k2, k3 = jax.random.split(key, 3)
        x = jax.random.normal(k1, (B, SEQ, D, D), dtype=jnp.float32)
        log_A = jax.random.normal(k2, (D,), dtype=jnp.float32) * 0.02
        w_dt = jax.random.normal(k3, (1, D), dtype=jnp.float32) * (1.0 / np.sqrt(D))
        b_dt = jnp.zeros((1,), dtype=jnp.float32)
        return {'x': x, 'log_A': log_A, 'w_dt': w_dt, 'b_dt': b_dt}
    _L1_conv_all = _L1_conv_setup()
    _L1_conv_in = {k: v for k, v in _L1_conv_all.items() if k in ('log_A', 'w_dt', 'b_dt')}
    del _L1_conv_all

    def _L2_attn_setup():
        import jax, jax.numpy as jnp
        import numpy as np
        D_MODEL = 512
        N_LAYERS = 2
        D_STATE = 32
        D_CONV = 4
        EXPAND = 2
        D_INNER = EXPAND * D_MODEL
        HEADDIM = D_STATE
        NHEADS = D_INNER // HEADDIM
        CONV_DIM = D_INNER + 2 * D_STATE
        D_IN_PROJ = 2 * D_INNER + 2 * D_STATE + NHEADS
        EPS = 1e-05

        def _layernorm(x, w, b):
            m = x.mean(-1, keepdims=True)
            v = ((x - m) ** 2).mean(-1, keepdims=True)
            return (x - m) * jax.lax.rsqrt(v + EPS) * w + b

        def _mamba2(u, in_w, conv_w, conv_b, dt_bias, A_log, Dp, rms_w, out_w):
            b, l, _ = u.shape
            zxbcdt = u @ in_w.T
            z, xBC, dt = jnp.split(zxbcdt, [D_INNER, D_INNER + CONV_DIM], axis=-1)
            dt = jax.nn.softplus(dt + dt_bias)
            xBC = jnp.transpose(xBC, (0, 2, 1))
            xBC = jax.lax.conv_general_dilated(xBC, conv_w[:, None, :], (1,), [(D_CONV - 1, 0)], dimension_numbers=('NCH', 'OIH', 'NCH'), feature_group_count=CONV_DIM)
            xBC = jnp.transpose(xBC, (0, 2, 1)) + conv_b
            xBC = jax.nn.silu(xBC)
            xh, Bm, Cm = jnp.split(xBC, [D_INNER, D_INNER + D_STATE], axis=-1)
            xh = xh.reshape(b, l, NHEADS, HEADDIM)
            A = -jnp.exp(A_log)
            dA = jnp.exp(dt * A)

            def step(state, inputs):
                dA_t, dt_t, x_t, B_t, C_t = inputs
                state = dA_t[:, :, None, None] * state + (dt_t[:, :, None] * x_t)[..., None] * B_t[:, None, None, :]
                y_t = jnp.einsum('bhpn,bn->bhp', state, C_t)
                return (state, y_t)
            xs = (jnp.moveaxis(dA, 1, 0), jnp.moveaxis(dt, 1, 0), jnp.moveaxis(xh, 1, 0), jnp.moveaxis(Bm, 1, 0), jnp.moveaxis(Cm, 1, 0))
            init = jnp.zeros((b, NHEADS, HEADDIM, D_STATE), u.dtype)
            _, ys = jax.lax.scan(step, init, xs)
            y = jnp.moveaxis(ys, 0, 1) + Dp[None, None, :, None] * xh
            y = y.reshape(b, l, D_INNER)
            y = y * jax.nn.silu(z)
            y = y * jax.lax.rsqrt(jnp.mean(y * y, -1, keepdims=True) + EPS) * rms_w
            return y @ out_w.T
        key = jax.random.key(seed)
        ks = jax.random.split(key, 8)
        B, L = (2, 2048)
        return {'x': jax.random.normal(ks[0], (B, L, D_MODEL), jnp.float32), 'ln_w': jnp.ones((N_LAYERS, D_MODEL), jnp.float32), 'ln_b': jnp.zeros((N_LAYERS, D_MODEL), jnp.float32), 'in_proj_w': jax.random.normal(ks[1], (N_LAYERS, D_IN_PROJ, D_MODEL), jnp.float32) * D_MODEL ** (-0.5), 'conv_w': jax.random.normal(ks[2], (N_LAYERS, CONV_DIM, D_CONV), jnp.float32) * D_CONV ** (-0.5), 'conv_b': jnp.zeros((N_LAYERS, CONV_DIM), jnp.float32), 'dt_bias': jax.random.normal(ks[3], (N_LAYERS, NHEADS), jnp.float32) * 0.5, 'A_log': jnp.log(jax.random.uniform(ks[4], (N_LAYERS, NHEADS), jnp.float32, 1.0, 16.0)), 'D': jnp.ones((N_LAYERS, NHEADS), jnp.float32), 'rms_w': jnp.ones((N_LAYERS, D_INNER), jnp.float32), 'out_proj_w': jax.random.normal(ks[5], (N_LAYERS, D_MODEL, D_INNER), jnp.float32) * D_INNER ** (-0.5)}
    _L2_attn_all = _L2_attn_setup()
    _L2_attn_in = {k: v for k, v in _L2_attn_all.items() if k in ('ln_w', 'ln_b', 'in_proj_w', 'conv_w', 'conv_b', 'dt_bias', 'A_log', 'D', 'rms_w', 'out_proj_w')}
    del _L2_attn_all

    def _L2_ffn_setup():
        import jax, jax.numpy as jnp
        import numpy as np
        IN_FEATURES = 512
        ACT_BITS = 4

        def _hadamard(size: int) -> np.ndarray:
            h = np.array([[1.0]], dtype=np.float64)
            while h.shape[0] < size:
                h = np.block([[h, h], [h, -h]])
            return (h / np.sqrt(size)).astype(np.float32)

        def _quantize_activations(x, bits=ACT_BITS):
            pos = 2 ** (bits - 1) - 1
            neg = 2 ** (bits - 1)
            scale = jnp.clip(jnp.max(jnp.abs(jax.lax.stop_gradient(x)), axis=-1, keepdims=True), 1e-05) / pos
            q = jnp.clip(jnp.round(x / scale), -neg, pos) * scale
            return x + jax.lax.stop_gradient(q - x)

        def _ternary_quantize_ste(w):
            scale = jnp.clip(jnp.mean(jnp.abs(jax.lax.stop_gradient(w)), axis=1, keepdims=True), 1e-05)
            n = w / scale
            tern = jnp.where(n > 0.5, 1.0, jnp.where(n < -0.5, -1.0, 0.0))
            q = tern * scale
            return w + jax.lax.stop_gradient(q - w)
        key = jax.random.key(seed)
        k1, k2 = jax.random.split(key)
        x = jax.random.normal(k1, (8, 4096, IN_FEATURES), dtype=jnp.float32)
        bound = 1.0 / np.sqrt(IN_FEATURES)
        weight = jax.random.uniform(k2, (512, IN_FEATURES), dtype=jnp.float32, minval=-bound, maxval=bound)
        return {'x': x, 'weight': weight}
    _L2_ffn_all = _L2_ffn_setup()
    _L2_ffn_in = {k: v for k, v in _L2_ffn_all.items() if k in ('weight',)}
    del _L2_ffn_all

    def _L3_attn_setup():
        import jax, jax.numpy as jnp
        import numpy as np
        D_MODEL = 512
        D_STATE = 32
        EXPAND = 2
        N_HEADS = 4
        D_INNER = EXPAND * D_MODEL
        HEAD_DIM = D_INNER // N_HEADS
        D_PROJ_OUT = 2 * D_INNER + 2 * N_HEADS * D_STATE + N_HEADS
        RMS_EPS = 1.1920929e-07
        key = jax.random.key(seed)
        ks = jax.random.split(key, 8)
        s_in = 1.0 / np.sqrt(D_MODEL)
        s_out = 1.0 / np.sqrt(D_INNER)
        return {'u': jax.random.normal(ks[0], (2, 1024, D_MODEL), jnp.float32), 'norm_w': jnp.ones((D_MODEL,), jnp.float32), 'in_proj_w': jax.random.normal(ks[1], (D_PROJ_OUT, D_MODEL), jnp.float32) * s_in, 'in_proj_b': jax.random.normal(ks[2], (D_PROJ_OUT,), jnp.float32) * s_in, 'A_log': jnp.full((N_HEADS,), -4.0, jnp.float32), 'D': jnp.ones((N_HEADS,), jnp.float32), 'dt_bias': jax.random.uniform(ks[3], (N_HEADS,), jnp.float32) - 4.0, 'out_proj_w': jax.random.normal(ks[4], (D_MODEL, D_INNER), jnp.float32) * s_out, 'out_proj_b': jax.random.normal(ks[5], (D_MODEL,), jnp.float32) * s_out}
    _L3_attn_all = _L3_attn_setup()
    _L3_attn_in = {k: v for k, v in _L3_attn_all.items() if k in ('norm_w', 'in_proj_w', 'in_proj_b', 'A_log', 'D', 'dt_bias', 'out_proj_w', 'out_proj_b')}
    del _L3_attn_all

    def _L3_ffn_setup():
        import jax, jax.numpy as jnp
        import numpy as np
        TOP_K = 2
        key = jax.random.key(seed)
        ks = jax.random.split(key, 6)
        B, S, H, F, E = (4, 1024, 512, 2048, 8)
        scale = 0.02
        x = jax.random.normal(ks[0], (B, S, H), dtype=jnp.float32)
        gate_w = jax.random.normal(ks[1], (E, H), dtype=jnp.float32) * scale
        w1 = jax.random.normal(ks[2], (E, H, F), dtype=jnp.float32) * scale
        b1 = jnp.zeros((E, F), dtype=jnp.float32)
        w2 = jax.random.normal(ks[3], (E, F, H), dtype=jnp.float32) * scale
        b2 = jnp.zeros((E, H), dtype=jnp.float32)
        return {'x': x, 'gate_w': gate_w, 'w1': w1, 'b1': b1, 'w2': w2, 'b2': b2}
    _L3_ffn_all = _L3_ffn_setup()
    _L3_ffn_in = {k: v for k, v in _L3_ffn_all.items() if k in ('gate_w', 'w1', 'b1', 'w2', 'b2')}
    del _L3_ffn_all
    return {'x': x, 'L0_conv_log_A': _L0_conv_in['log_A'], 'L0_conv_dt_w': _L0_conv_in['dt_w'], 'L0_conv_dt_b': _L0_conv_in['dt_b'], 'L0_conv_ln_w': _L0_conv_in['ln_w'], 'L0_conv_ln_b': _L0_conv_in['ln_b'], 'L1_conv_log_A': _L1_conv_in['log_A'], 'L1_conv_w_dt': _L1_conv_in['w_dt'], 'L1_conv_b_dt': _L1_conv_in['b_dt'], 'L2_attn_ln_w': _L2_attn_in['ln_w'], 'L2_attn_ln_b': _L2_attn_in['ln_b'], 'L2_attn_in_proj_w': _L2_attn_in['in_proj_w'], 'L2_attn_conv_w': _L2_attn_in['conv_w'], 'L2_attn_conv_b': _L2_attn_in['conv_b'], 'L2_attn_dt_bias': _L2_attn_in['dt_bias'], 'L2_attn_A_log': _L2_attn_in['A_log'], 'L2_attn_D': _L2_attn_in['D'], 'L2_attn_rms_w': _L2_attn_in['rms_w'], 'L2_attn_out_proj_w': _L2_attn_in['out_proj_w'], 'L2_ffn_weight': _L2_ffn_in['weight'], 'L3_attn_norm_w': _L3_attn_in['norm_w'], 'L3_attn_in_proj_w': _L3_attn_in['in_proj_w'], 'L3_attn_in_proj_b': _L3_attn_in['in_proj_b'], 'L3_attn_A_log': _L3_attn_in['A_log'], 'L3_attn_D': _L3_attn_in['D'], 'L3_attn_dt_bias': _L3_attn_in['dt_bias'], 'L3_attn_out_proj_w': _L3_attn_in['out_proj_w'], 'L3_attn_out_proj_b': _L3_attn_in['out_proj_b'], 'L3_ffn_gate_w': _L3_ffn_in['gate_w'], 'L3_ffn_w1': _L3_ffn_in['w1'], 'L3_ffn_b1': _L3_ffn_in['b1'], 'L3_ffn_w2': _L3_ffn_in['w2'], 'L3_ffn_b2': _L3_ffn_in['b2']}

def reference(x, L0_conv_log_A, L0_conv_dt_w, L0_conv_dt_b, L0_conv_ln_w, L0_conv_ln_b, L1_conv_log_A, L1_conv_w_dt, L1_conv_b_dt, L2_attn_ln_w, L2_attn_ln_b, L2_attn_in_proj_w, L2_attn_conv_w, L2_attn_conv_b, L2_attn_dt_bias, L2_attn_A_log, L2_attn_D, L2_attn_rms_w, L2_attn_out_proj_w, L2_ffn_weight, L3_attn_norm_w, L3_attn_in_proj_w, L3_attn_in_proj_b, L3_attn_A_log, L3_attn_D, L3_attn_dt_bias, L3_attn_out_proj_w, L3_attn_out_proj_b, L3_ffn_gate_w, L3_ffn_w1, L3_ffn_b1, L3_ffn_w2, L3_ffn_b2):
    import jax
    import jax.numpy as jnp

    def _L0_conv_ref(x, log_A, dt_w, dt_b, ln_w, ln_b):
        import jax, jax.numpy as jnp
        import numpy as np
        EPS = 1e-05

        def _layernorm2d(x, w, b):
            mean = jnp.mean(x, axis=(-2, -1), keepdims=True)
            var = jnp.mean(jnp.square(x - mean), axis=(-2, -1), keepdims=True)
            return (x - mean) / jnp.sqrt(var + EPS) * w + b
        x_norm = _layernorm2d(x, ln_w, ln_b)
        b, seq, d, _ = x_norm.shape
        A_cont = -jnp.exp(log_A)
        dt = jax.nn.softplus(jnp.einsum('bsdc,c->bsd', x_norm, dt_w[0]) + dt_b[0])
        log_a = dt * A_cont
        cums = jnp.cumsum(log_a, axis=1)
        log_M = cums[:, :, None, :] - cums[:, None, :, :]
        idx = jnp.arange(seq)
        mask = idx[:, None] >= idx[None, :]
        log_M = jnp.where(mask[None, :, :, None], log_M, -jnp.inf)
        M = jnp.exp(log_M)
        out = jnp.einsum('btjr,bjrc->btrc', M, x_norm)
        return out

    def _L1_conv_ref(x, log_A, w_dt, b_dt):
        import jax, jax.numpy as jnp
        import numpy as np
        B, SEQ, D = (2, 512, 32)
        A_continuous = -jnp.exp(log_A)
        dt = jax.nn.softplus(jnp.einsum('bsrc,oc->bsro', x, w_dt) + b_dt)[..., 0]
        log_A_dt = dt * A_continuous
        cumsum_A = jnp.cumsum(log_A_dt, axis=1)
        log_M = cumsum_A[:, :, None, :] - cumsum_A[:, None, :, :]
        idx = jnp.arange(SEQ)
        mask = idx[:, None] >= idx[None, :]
        log_M = jnp.where(mask[None, :, :, None], log_M, -jnp.inf)
        M = jnp.exp(log_M)
        out = jnp.einsum('btjr,bjrc->btrc', M, x)
        return out

    def _L2_attn_ref(x, ln_w, ln_b, in_proj_w, conv_w, conv_b, dt_bias, A_log, D, rms_w, out_proj_w):
        import jax, jax.numpy as jnp
        import numpy as np
        D_MODEL = 512
        N_LAYERS = 2
        D_STATE = 32
        D_CONV = 4
        EXPAND = 2
        D_INNER = EXPAND * D_MODEL
        HEADDIM = D_STATE
        NHEADS = D_INNER // HEADDIM
        CONV_DIM = D_INNER + 2 * D_STATE
        D_IN_PROJ = 2 * D_INNER + 2 * D_STATE + NHEADS
        EPS = 1e-05

        def _layernorm(x, w, b):
            m = x.mean(-1, keepdims=True)
            v = ((x - m) ** 2).mean(-1, keepdims=True)
            return (x - m) * jax.lax.rsqrt(v + EPS) * w + b

        def _mamba2(u, in_w, conv_w, conv_b, dt_bias, A_log, Dp, rms_w, out_w):
            b, l, _ = u.shape
            zxbcdt = u @ in_w.T
            z, xBC, dt = jnp.split(zxbcdt, [D_INNER, D_INNER + CONV_DIM], axis=-1)
            dt = jax.nn.softplus(dt + dt_bias)
            xBC = jnp.transpose(xBC, (0, 2, 1))
            xBC = jax.lax.conv_general_dilated(xBC, conv_w[:, None, :], (1,), [(D_CONV - 1, 0)], dimension_numbers=('NCH', 'OIH', 'NCH'), feature_group_count=CONV_DIM)
            xBC = jnp.transpose(xBC, (0, 2, 1)) + conv_b
            xBC = jax.nn.silu(xBC)
            xh, Bm, Cm = jnp.split(xBC, [D_INNER, D_INNER + D_STATE], axis=-1)
            xh = xh.reshape(b, l, NHEADS, HEADDIM)
            A = -jnp.exp(A_log)
            dA = jnp.exp(dt * A)

            def step(state, inputs):
                dA_t, dt_t, x_t, B_t, C_t = inputs
                state = dA_t[:, :, None, None] * state + (dt_t[:, :, None] * x_t)[..., None] * B_t[:, None, None, :]
                y_t = jnp.einsum('bhpn,bn->bhp', state, C_t)
                return (state, y_t)
            xs = (jnp.moveaxis(dA, 1, 0), jnp.moveaxis(dt, 1, 0), jnp.moveaxis(xh, 1, 0), jnp.moveaxis(Bm, 1, 0), jnp.moveaxis(Cm, 1, 0))
            init = jnp.zeros((b, NHEADS, HEADDIM, D_STATE), u.dtype)
            _, ys = jax.lax.scan(step, init, xs)
            y = jnp.moveaxis(ys, 0, 1) + Dp[None, None, :, None] * xh
            y = y.reshape(b, l, D_INNER)
            y = y * jax.nn.silu(z)
            y = y * jax.lax.rsqrt(jnp.mean(y * y, -1, keepdims=True) + EPS) * rms_w
            return y @ out_w.T
        h = x
        for i in range(N_LAYERS):
            res = h
            h = _layernorm(h, ln_w[i], ln_b[i])
            h = _mamba2(h, in_proj_w[i], conv_w[i], conv_b[i], dt_bias[i], A_log[i], D[i], rms_w[i], out_proj_w[i])
            h = h + res
        return h

    def _L2_ffn_ref(x, weight):
        import jax, jax.numpy as jnp
        import numpy as np
        IN_FEATURES = 512
        ACT_BITS = 4

        def _hadamard(size: int) -> np.ndarray:
            h = np.array([[1.0]], dtype=np.float64)
            while h.shape[0] < size:
                h = np.block([[h, h], [h, -h]])
            return (h / np.sqrt(size)).astype(np.float32)

        def _quantize_activations(x, bits=ACT_BITS):
            pos = 2 ** (bits - 1) - 1
            neg = 2 ** (bits - 1)
            scale = jnp.clip(jnp.max(jnp.abs(jax.lax.stop_gradient(x)), axis=-1, keepdims=True), 1e-05) / pos
            q = jnp.clip(jnp.round(x / scale), -neg, pos) * scale
            return x + jax.lax.stop_gradient(q - x)

        def _ternary_quantize_ste(w):
            scale = jnp.clip(jnp.mean(jnp.abs(jax.lax.stop_gradient(w)), axis=1, keepdims=True), 1e-05)
            n = w / scale
            tern = jnp.where(n > 0.5, 1.0, jnp.where(n < -0.5, -1.0, 0.0))
            q = tern * scale
            return w + jax.lax.stop_gradient(q - w)
        H = jnp.asarray(_hadamard(IN_FEATURES))
        xh = x @ H
        xq = _quantize_activations(xh)
        wq = _ternary_quantize_ste(weight)
        return jnp.einsum('bsi,oi->bso', xq, wq)

    def _L3_attn_ref(u, norm_w, in_proj_w, in_proj_b, A_log, D, dt_bias, out_proj_w, out_proj_b):
        import jax, jax.numpy as jnp
        import numpy as np
        D_MODEL = 512
        D_STATE = 32
        EXPAND = 2
        N_HEADS = 4
        D_INNER = EXPAND * D_MODEL
        HEAD_DIM = D_INNER // N_HEADS
        D_PROJ_OUT = 2 * D_INNER + 2 * N_HEADS * D_STATE + N_HEADS
        RMS_EPS = 1.1920929e-07
        B, L, _ = u.shape
        u_norm = u * jax.lax.rsqrt(jnp.mean(u * u, axis=-1, keepdims=True) + RMS_EPS) * norm_w
        zxbcdt = u_norm @ in_proj_w.T + in_proj_b
        z = zxbcdt[..., :D_INNER]
        x = zxbcdt[..., D_INNER:2 * D_INNER].reshape(B, L, N_HEADS, HEAD_DIM)
        dt = zxbcdt[..., 2 * D_INNER:2 * D_INNER + N_HEADS]
        BC = zxbcdt[..., 2 * D_INNER + N_HEADS:].reshape(B, L, N_HEADS, 2, D_STATE)
        B_mat, C_mat = (BC[..., 0, :], BC[..., 1, :])
        dt = jax.nn.softplus(dt + dt_bias)
        A = -jnp.exp(A_log)
        dtA = jnp.exp(dt * A)
        dtB = dt[..., None] * B_mat

        def step(h, inp):
            dtA_t, dtB_t, x_t, C_t = inp
            h = h * dtA_t[:, :, None, None] + dtB_t[..., None] * x_t[:, :, None, :]
            y_t = jnp.einsum('bhn,bhnp->bhp', C_t, h)
            return (h, y_t)
        h0 = jnp.zeros((B, N_HEADS, D_STATE, HEAD_DIM), u.dtype)
        xs = (jnp.moveaxis(dtA, 1, 0), jnp.moveaxis(dtB, 1, 0), jnp.moveaxis(x, 1, 0), jnp.moveaxis(C_mat, 1, 0))
        _, ys = jax.lax.scan(step, h0, xs)
        y = jnp.moveaxis(ys, 0, 1)
        y = y + x * D[None, None, :, None]
        y = y.reshape(B, L, D_INNER)
        y = y * jax.nn.silu(z)
        return y @ out_proj_w.T + out_proj_b

    def _L3_ffn_ref(x, gate_w, w1, b1, w2, b2):
        import jax, jax.numpy as jnp
        import numpy as np
        TOP_K = 2
        E = gate_w.shape[0]
        gate_logits = jnp.einsum('bsh,eh->bse', x, gate_w)
        gate_probs = jax.nn.softmax(gate_logits, axis=-1)
        top_v, top_i = jax.lax.top_k(gate_probs, TOP_K)
        onehot = jax.nn.one_hot(top_i, E, dtype=x.dtype)
        comb_w = jnp.einsum('bsk,bske->bse', top_v, onehot)
        out = jnp.zeros_like(x)
        for e in range(E):
            h = jax.nn.silu(jnp.einsum('bsh,hf->bsf', x, w1[e]) + b1[e])
            y = jnp.einsum('bsf,fh->bsh', h, w2[e]) + b2[e]
            out = out + y * comb_w[..., e:e + 1]
        return out

    def _gn(v, G=32, eps=1e-05):
        B_, C_, H_, W_ = v.shape
        g = v.reshape(B_, G, C_ // G, H_, W_)
        m = jnp.mean(g, axis=(2, 3, 4), keepdims=True)
        s = jnp.var(g, axis=(2, 3, 4), keepdims=True)
        return ((g - m) / jnp.sqrt(s + eps)).reshape(v.shape)

    def _ln_c(v, eps=1e-06):
        m = jnp.mean(v, axis=1, keepdims=True)
        s = jnp.var(v, axis=1, keepdims=True)
        return (v - m) / jnp.sqrt(s + eps)

    def _ln_t(v, eps=1e-05):
        m = jnp.mean(v, axis=-1, keepdims=True)
        s = jnp.var(v, axis=-1, keepdims=True)
        return (v - m) / jnp.sqrt(s + eps)

    def _to_tokens(v):
        B_, C_, H_, W_ = v.shape
        return v.reshape(B_, C_, H_ * W_).transpose(0, 2, 1)

    def _from_tokens(t, like):
        B_, C_, H_, W_ = like.shape
        return t.transpose(0, 2, 1).reshape(B_, C_, H_, W_)
    x = x + _L0_conv_ref(_gn(x), L0_conv_log_A, L0_conv_dt_w, L0_conv_dt_b, L0_conv_ln_w, L0_conv_ln_b)
    x = x + _L1_conv_ref(_gn(x), L1_conv_log_A, L1_conv_w_dt, L1_conv_b_dt)
    t = _to_tokens(x)
    t = t + _L2_attn_ref(_ln_t(t), L2_attn_ln_w, L2_attn_ln_b, L2_attn_in_proj_w, L2_attn_conv_w, L2_attn_conv_b, L2_attn_dt_bias, L2_attn_A_log, L2_attn_D, L2_attn_rms_w, L2_attn_out_proj_w)
    t = t + _L2_ffn_ref(_ln_t(t), L2_ffn_weight)
    t = t + _L3_attn_ref(_ln_t(t), L3_attn_norm_w, L3_attn_in_proj_w, L3_attn_in_proj_b, L3_attn_A_log, L3_attn_D, L3_attn_dt_bias, L3_attn_out_proj_w, L3_attn_out_proj_b)
    t = t + _L3_ffn_ref(_ln_t(t), L3_ffn_gate_w, L3_ffn_w1, L3_ffn_b1, L3_ffn_w2, L3_ffn_b2)
    x = _from_tokens(t, x)
    return x

_drawn_inputs = setup_inputs


def setup_inputs(seed=0):
    import zlib

    import numpy as np

    out = dict(_drawn_inputs(seed))
    spreads = {'L0_conv_ln_w': (1.0, 0.2),
     'L0_conv_ln_b': (0.0, 0.1),
     'L2_attn_ln_w': (1.0, 0.2),
     'L2_attn_ln_b': (0.0, 0.1),
     'L2_attn_conv_b': (0.0, 0.1),
     'L2_attn_D': (1.0, 0.2),
     'L2_attn_rms_w': (1.0, 0.2),
     'L3_attn_norm_w': (1.0, 0.2),
     'L3_attn_A_log': (-4.0, 0.2),
     'L3_attn_D': (1.0, 0.6),
     'L3_ffn_b1': (0.0, 0.8),
     'L3_ffn_b2': (0.0, 0.8)}
    factors = {'L0_conv_log_A': 3.42,
     'L1_conv_log_A': 4.818,
     'L3_attn_out_proj_b': 8.0,
     'L3_ffn_gate_w': 8.0,
     'L3_ffn_w1': 8.0,
     'L3_ffn_w2': 7.825}
    for name, (base, spread) in spreads.items():
        noise = np.random.default_rng([zlib.crc32(name.encode()), seed]).standard_normal(out[name].shape)
        drawn = base * np.exp(spread * noise) if base else spread * noise
        out[name] = jnp.asarray(drawn.astype(out[name].dtype))
    for name, factor in factors.items():
        out[name] = (out[name] * factor).astype(out[name].dtype)
    return out
```

```python
from contextlib import ExitStack

import numpy as np
import concourse.bass as bass
from concourse import mybir

P = 128
F32 = mybir.dt.float32
F16 = mybir.dt.float16
U32 = mybir.dt.uint32
ACT = mybir.ActivationFunctionType
ALU = mybir.AluOpType
AX = mybir.AxisListType
ds = bass.ds

SEQ, SIDE = 512, 32
TOK = SIDE * SIDE
TT = TOK // P
D = 512
KD = D // P
GROUPS = 32
DI = 1024
JD = DI // P
NS = 32
H2 = 32
LAYERS = 2
TAPS = 4


class Core:

    def __init__(self, nc, ctx, ins):
        self.nc, self.ctx, self.ins = nc, ctx, ins
        self.stages = 0
        self.stage_end = self.sem("stage_end")
        self.cleared = self.sem("cleared")
        self.t = self.sb("t_res", [P, TT, D])
        self.ident = self.sb("ident", [P, P])
        self.tri = self.sb("tri", [P, P])
        self.after = self.sb("after", [P, P])
        self.after16 = self.sb("after16", [P, P], F16)
        self.tri16 = self.sb("tri16", [P, P], F16)
        self.ones = self.sb("ones", [P, P])
        self.sel = self.sb("sel", [H2, JD, P])
        self.passed = self.sem("passed")
        self.consts_in = self.sem("consts_in")

    def sb(self, name, shape, dt=F32, ctx=None):
        return (ctx or self.ctx).enter_context(self.nc.sbuf_tensor(name, shape, dt))

    def sem(self, name, ctx=None):
        return (ctx or self.ctx).enter_context(self.nc.semaphore(name))

    def stage_sem(self, name, ctx, used):
        used.append(self.sem(name, ctx))
        return used[-1]

    def load_consts(self, sp):
        for dst, name in ((self.ident, "c_ident"), (self.tri, "c_tri"), (self.after, "c_after"),
                          (self.after16, "c_after16"), (self.tri16, "c_tri16"), (self.ones, "c_ones"), (self.sel, "c_sel")):
            sp.dma_start(dst[:], self.ins[name]).then_inc(self.consts_in, 16)

    CONSTS = 7 * 16

    def apart(self, e):
        e.sem_inc(self.passed, 1)


class Chain:

    def __init__(self, eng, sem):
        self.eng, self.sem, self.n = eng, sem, 0

    def __call__(self, instruction):
        instruction.then_inc(self.sem, 1)
        self.n = self.n + 1
        self.eng.wait_ge(self.sem, self.n)


L01_EPS_GN = 1e-5
L01_EPS_LN2 = 1e-5


def stage_l01(core, ps):
    nc, ins, t = core.nc, core.ins, core.t
    cx = ExitStack()
    sb = lambda n, s, d=F32: core.sb(n, s, d, cx)
    used = []
    sem = lambda n: core.stage_sem("c_" + n, cx, used)
    xcm = sb("xcm", [P, KD, TOK])
    xn = sb("xn", [P, TT, D])
    sq = sb("sq", [P, TT, D])
    selT = sb("selT", [P, TT, H2])
    wsel = sb("wsel", [P, 2, TT, H2])
    g16 = sb("g16", [P, P])
    lnw = sb("lnw2d", [P, TT])
    lnb = sb("lnb2d", [P, TT])
    dtw = sb("dtw", [P, 2])
    dtb = sb("dtb", [H2, 2])
    loga = sb("loga", [H2, 2])
    nega = sb("nega", [H2, 2])
    stats = sb("stats0", [P, KD, 2, 6])
    mv = sb("mv0", [P, KD, 2])
    dev = sb("dev0", [P, KD])
    q = sb("q0", [P, KD])
    rg = sb("rg0", [P, KD])
    rc = sb("rc0", [P, KD])
    sh = sb("sh0", [P, KD])
    xb = sb("xb01", [H2, D])
    ab = sb("ab01", [H2, D])
    ex = sb("ex01", [H2, D])
    lg = sb("lg01", [H2, D])
    dtt = sb("dtt01", [H2, D])
    dec = sb("dec01", [H2, D])
    s1 = sb("s1", [P, GROUPS])
    mg = sb("mg", [P, GROUPS])
    rgr = sb("rgr", [P, GROUPS])

    onesn = sb("onesn", [P, P])
    x_cm_in = sem("x_cm_in")
    x_tm_in = sem("x_tm_in")
    par_in = sem("par01_in")
    dve_own = sem("dve_own01")
    act_own = sem("act_own01")
    ch_mean = sem("ch_mean")
    g_mean = sem("g_mean")
    ch_spread = sem("ch_spread")
    g_var = sem("g_var")
    sq_in = sem("sq_in")
    sq_out = sem("sq_out")
    x_hat = sem("x_hat")
    turned = sem("turned")
    affine = sem("affine")
    weights = sem("weights01")
    dt_raw = sem("dt_raw01")
    pre = sem("pre01")
    negabs = sem("negabs01")
    log1p = sem("log1p01")
    dt_done = sem("dt_done01")
    decayed = sem("decayed01")
    spread_d = sem("spread_d01")
    scanned = sem("scanned")
    added = sem("added01")
    sums = sem("sums01")
    tot = sem("tot01")
    centred = sem("centred")
    squared = sem("squared")
    scaled = sem("scaled01")
    PAR = 8 * 16

    def sp(e):
        for j in range(KD):
            e.dma_start(xcm[:, j, :], ins["x_cm"][j * P:(j + 1) * P, :]).then_inc(x_cm_in, 16)
        for dst, name in ((selT, "c_selT"), (g16, "c_g16"), (onesn, "c_onesn"), (lnw, "ln2d_w"), (lnb, "ln2d_b"),
                          (dtw, "dt_w01"), (dtb, "dt_b01"), (loga, "log_A01")):
            e.dma_start(dst[:], ins[name]).then_inc(par_in, 16)
        core.load_consts(e)
        e.dma_start(t[:], ins["x_tm"].rearrange("(i p) f -> p i f", p=P)).then_inc(x_tm_in, 16)

    def dve(e):
        own = Chain(e, dve_own)
        e.wait_ge(x_cm_in, 16 * KD)
        for j in range(KD):
            e.bn_stats(stats[:, j, 0, :], xcm[:, j, 0:512])
            own(e.bn_stats(stats[:, j, 1, :], xcm[:, j, 512:1024]))
        for j in range(KD):
            own(e.bn_aggr(mv[:, j, :], stats[:, j, :, :].rearrange("p a b -> p (a b)")))
        e.tensor_copy(dev[:], mv[:, :, 0]).then_inc(ch_mean, 1)
        e.wait_ge(g_mean, 1)
        own(e.tensor_tensor(dev[:], mv[:, :, 0], ps[:, 0, 0:KD], ALU.subtract))
        own(e.tensor_tensor(q[:], dev[:], dev[:], ALU.mult))
        e.tensor_tensor(q[:], q[:], mv[:, :, 1], ALU.add).then_inc(ch_spread, 1)
        e.wait_ge(g_var, 1)
        e.tensor_scalar(rg[:], ps[:, 1, 0:KD], L01_EPS_GN, None, ALU.add).then_inc(sq_in, 1)
        e.wait_ge(sq_out, 1)
        own(e.reciprocal(rg[:], rg[:]))
        own(e.tensor_tensor(q[:], rg[:], rg[:], ALU.mult))
        own(e.tensor_tensor(q[:], q[:], mv[:, :, 1], ALU.mult))
        e.tensor_scalar(rc[:], q[:], L01_EPS_LN2, None, ALU.add).then_inc(sq_in, 1)
        e.wait_ge(sq_out, 2)
        own(e.reciprocal(rc[:], rc[:]))
        own(e.tensor_tensor(rc[:], rc[:], rg[:], ALU.mult))
        own(e.scalar_tensor_tensor(out=sh[:], in0=mv[:, :, 0], scalar=-1.0, in1=rc[:], op0=ALU.mult, op1=ALU.mult))
        for j in range(KD):
            e.tensor_scalar(xcm[:, j, :], xcm[:, j, :], rc[:, j:j + 1], sh[:, j:j + 1], ALU.mult, ALU.add).then_inc(x_hat, 1)
        e.wait_ge(par_in, PAR)
        for l in range(2):
            e.tensor_scalar(wsel[:, l, :, :], selT[:], dtw[:, l:l + 1], None, ALU.mult).then_inc(weights, 1)
        scans(e, 0)
        e.wait_ge(added, TT)
        e.tensor_reduce(s1[:], t[:].rearrange("p i (g c) -> p g i c", g=GROUPS), AX.XY, ALU.add).then_inc(sums, 1)
        e.wait_ge(tot, 1)
        own(e.tensor_copy(mg[:], ps[:, 0, 0:GROUPS]))
        for i in range(TT):
            e.tensor_tensor(grp(xn[:, i, :]), grp(t[:, i, :]), per_group(mg), ALU.subtract).then_inc(centred, 1)
        e.wait_ge(squared, TT)
        e.tensor_reduce(s1[:], sq[:].rearrange("p i (g c) -> p g i c", g=GROUPS), AX.XY, ALU.add).then_inc(sums, 1)
        e.wait_ge(tot, 2)
        e.tensor_scalar(rgr[:], ps[:, 1, 0:GROUPS], L01_EPS_GN, None, ALU.add).then_inc(sq_in, 1)
        e.wait_ge(sq_out, 3)
        own(e.reciprocal(rgr[:], rgr[:]))
        for i in range(TT):
            e.tensor_tensor(grp(xn[:, i, :]), grp(xn[:, i, :]), per_group(rgr), ALU.mult).then_inc(scaled, 1)
        scans(e, 1)

    def grp(x):
        return x.rearrange("p (g c) -> p g c", g=GROUPS)

    def per_group(x):
        return x[:].unsqueeze(2).to_broadcast([P, GROUPS, SEQ // GROUPS])

    def scans(e, l):
        e.wait_ge(pre, l + 1)
        e.scalar_tensor_tensor(out=ab[:], in0=xb[:], scalar=-1.0, in1=xb[:], op0=ALU.mult, op1=ALU.min).then_inc(negabs, 1)
        e.wait_ge(log1p, 2 * l + 2)
        e.scalar_tensor_tensor(out=dtt[:], in0=xb[:], scalar=0.0, in1=lg[:], op0=ALU.max, op1=ALU.add).then_inc(dt_done, 1)
        for i in range(TT):
            e.wait_ge(spread_d, l * TT + i + 1)
            e.tensor_tensor_scan(sq[:, i, :], ps[:, i % 4, :], xn[:, i, :], 0.0, ALU.mult, ALU.add).then_inc(scanned, 1)

    def pool(e):
        e.wait_ge(x_tm_in, 16)
        for l in range(2):
            for i in range(TT):
                e.wait_ge(scanned, l * TT + i + 1)
                e.tensor_tensor(t[:, i, :], t[:, i, :], sq[:, i, :], ALU.add).then_inc(added, 1)
        e.wait_ge(added, 2 * TT)

    def act(e):
        own = Chain(e, act_own)
        for k, s in enumerate((rg, rc)):
            e.wait_ge(sq_in, k + 1)
            e.activation(s[:], s[:], ACT.Sqrt).then_inc(sq_out, 1)
        e.wait_ge(par_in, PAR)
        own(e.activation(nega[:], loga[:], ACT.Exp))
        own(e.mul(nega[:], nega[:], -1.0))
        for i in range(TT):
            e.wait_ge(turned, i + 1)
            e.activation(xn[:, i, :], ps[:, 2 + i % 4, :], ACT.Identity, scale=lnw[:, i:i + 1], bias=lnb[:, i:i + 1])\
                .then_inc(affine, 1)
        decay(e, 0)
        for i in range(TT):
            e.wait_ge(centred, i + 1)
            e.activation(sq[:, i, :], xn[:, i, :], ACT.Square).then_inc(squared, 1)
        e.wait_ge(sq_in, 3)
        e.activation(rgr[:], rgr[:], ACT.Sqrt).then_inc(sq_out, 1)
        decay(e, 1)

    def decay(e, l):
        e.wait_ge(dt_raw, l + 1)
        e.activation(xb[:], ps[0:H2, 6, :], ACT.Identity, bias=dtb[:, l:l + 1]).then_inc(pre, 1)
        e.wait_ge(negabs, l + 1)
        e.activation(ex[:], ab[:], ACT.Exp).then_inc(log1p, 1)
        e.wait_ge(log1p, 2 * l + 1)
        e.activation(lg[:], ex[:], ACT.Ln, bias=1.0).then_inc(log1p, 1)
        e.wait_ge(dt_done, l + 1)
        e.activation(dec[:], dtt[:], ACT.Exp, scale=nega[:, l:l + 1]).then_inc(decayed, 1)

    def pe(e):
        e.wait_ge(par_in, PAR)
        e.wait_ge(core.consts_in, core.CONSTS)
        e.wait_ge(ch_mean, 1)
        e.matmul(ps[:, 0, 0:KD], g16[:], dev[:], start=True, stop=True).then_inc(g_mean, 1)
        e.wait_ge(ch_spread, 1)
        e.matmul(ps[:, 1, 0:KD], g16[:], q[:], start=True, stop=True).then_inc(g_var, 1)
        for i in range(TT):
            if i >= 4:
                e.wait_ge(affine, i - 3)
            for j in range(KD):
                if i == 0:
                    e.wait_ge(x_hat, j + 1)
                x = e.transpose(ps[:, 2 + i % 4, j * P:(j + 1) * P], xcm[:, j, i * P:(i + 1) * P], core.ident[:])
            x.then_inc(turned, 1)
        decays(e, 0)
        e.wait_ge(sums, 1)
        e.matmul(ps[:, 0, 0:GROUPS], onesn[:], s1[:], start=True, stop=True).then_inc(tot, 1)
        e.wait_ge(sums, 2)
        e.matmul(ps[:, 1, 0:GROUPS], onesn[:], s1[:], start=True, stop=True).then_inc(tot, 1)
        decays(e, 1)

    def decays(e, l):
        e.wait_ge(weights, l + 1)
        for i in range(TT):
            e.wait_ge(scaled if l else affine, i + 1)
            x = e.matmul(ps[0:H2, 6, :], wsel[:, l, i, :], xn[:, i, :], start=(i == 0), stop=(i == TT - 1))
        x.then_inc(dt_raw, 1)
        e.wait_ge(decayed, l + 1)
        for i in range(TT):
            if i >= 4:
                e.wait_ge(scanned, l * TT + i - 3)
            e.matmul(ps[:, i % 4, :], core.sel[:, i, :], dec[:], start=True, stop=True).then_inc(spread_d, 1)

    return dict(sp=sp, dve=dve, act=act, pe=pe, pool=pool, cx=cx, used=used)


MB_EPS = 1e-5
MB_DPROJ = 2 * DI + 2 * NS + H2
MB_CX, MB_CB, MB_CC, MB_CDT = DI, 2 * DI, 2 * DI + NS, 2 * DI + 2 * NS
MB_PIECES = 6
MB_ER = 2
MB_EG = 8
MB_LNW, MB_LNB, MB_CVW, MB_CVB, MB_BCW, MB_BCB, MB_DCOL, MB_RMSW, MB_DTB, MB_ALOG = 0, 4, 8, 40, 48, 56, 58, 66, 74, 106
MB_NPAR = 138


def stage_mamba(core, ps):
    nc, ins, t = core.nc, core.ins, core.t
    cx = ExitStack()
    sb = lambda n, s, d=F32: core.sb("mb_" + n, s, d, cx)
    used = []
    sem = lambda n: core.stage_sem("m_" + n, cx, used)
    h = t
    kept = nc.dram_tensor("t_kept", [TOK, D], F32).ap().rearrange("(i p) f -> p i f", p=P)
    par = sb("par", [P, MB_NPAR])
    wi_hi, wi_lo = sb("wi_hi", [P, KD, MB_DPROJ], F16), sb("wi_lo", [P, KD, MB_DPROJ], F16)
    wo_hi, wo_lo = sb("wo_hi", [P, JD, D], F16), sb("wo_lo", [P, JD, D], F16)
    ring = sb("ring", [P, 2 * MB_DPROJ])
    raw = [ring[:, b * MB_DPROJ:(b + 1) * MB_DPROJ] for b in range(2)]
    u_hi, u_lo = sb("u_hi", [P, KD, TOK], F16), sb("u_lo", [P, KD, TOK], F16)
    stats, mv = sb("stats", [P, TT, 6]), sb("mv", [P, TT, 2])
    rstd = sb("rstd", [P, TT])
    nega = sb("nega", [P, H2])
    dtx, dtn, dte_ = sb("dtx", [P, TT, H2]), sb("dtn", [P, TT, H2]), sb("dte_", [P, TT, H2])
    dt, la, dend = sb("dt", [P, TT, H2]), sb("la", [P, TT, H2]), sb("dend", [P, TT, H2])
    edec, dte = sb("edec", [P, TT, H2]), sb("dte", [P, TT, H2])
    la_hi, la_lo = sb("la_hi", [P, TT, H2], F16), sb("la_lo", [P, TT, H2], F16)
    cumT = sb("cumT", [H2, TOK])
    tri_th = sb("tri_th", [P, P, H2], F16)
    r_hi, r_lo = (ring[:, b * 2048:(b + 1) * 2048].bitcast(F16).rearrange("p (t h) -> p t h", h=H2) for b in range(2))
    E = sb("E", [P, MB_ER * 512])
    M = sb("M", [P, H2, P])
    uf = M[:].rearrange("p h t -> p (h t)").rearrange("p (i f) -> p i f", i=TT)
    xp, bcp = sb("xp", [P, JD, P + 3]), sb("bcp", [NS, 2, P + 3])
    ca, cbc = sb("ca", [P, JD, P]), sb("cbc", [NS, 2, P])
    th, thbc = sb("th", [P, JD, P]), sb("thbc", [NS, 2, P])
    xc, bcc = sb("xc", [P, JD, P]), sb("bcc", [NS, 2, P])
    thz, sz = th, sb("sz", [P, JD, P])
    xdt, xe = sb("xdt", [P, DI]), sb("xe", [P, DI])
    btok = sb("btok", [P, NS])
    gm = sb("gm", [P, P])
    S = sb("S", [NS, DI])
    quad = sb("quad", [P, 4, DI])
    un = quad[:].rearrange("p a b -> p (a b)").rearrange("p (i f) -> p i f", i=TT)
    ec, yi, dx, y = (quad[:, a, :].rearrange("p (j t) -> p j t", j=JD) for a in range(4))
    ysq = sb("ysq", [P, JD, P])
    y_hi, y_lo = sb("y_hi", [P, JD, P], F16), sb("y_lo", [P, JD, P], F16)
    rv, rs, mhalf = sb("rv", [P, 1]), sb("rs", [P, 1]), sb("mhalf", [P, 1])

    dve_own, act_own, pool_own = sem("dve_own"), sem("act_own"), sem("pool_own")
    layer_open = sem("layer_open")
    par_in = sem("par_in")
    raw_in = [sem(f"raw_in{b}") for b in range(2)]
    w_hi, w_lo = sem("w_hi"), sem("w_lo")
    var_done, sd_done = sem("var_done"), sem("sd_done")
    un_done, turned, uf_done, uhi_done, ulo_done = (sem(n) for n in ("un_done", "turned", "uf_done", "uhi_done", "ulo_done"))
    dt_mm, dtn_done, dt_log, la_done, sums_mm, sums_exp, cum_ev, prep = (
        sem(n) for n in ("dt_mm", "dtn_done", "dt_log", "la_done", "sums_mm", "sums_exp", "cum_ev", "prep"))
    nega_done = sem("nega_done")
    zeroed = sem("zeroed")
    x_mm, bc_mm, z_mm = sem("x_mm"), sem("bc_mm"), sem("z_mm")
    x_ev, bc_ev = sem("x_ev"), sem("bc_ev")
    halo = sem("halo")
    acc, tanh, xc_done, bcc_done = sem("acc"), sem("tanh"), sem("xc_done"), sem("bcc_done")
    thz_done, sz_done = sem("thz_done"), sem("sz_done")
    rhi_done, rlo_done = sem("rhi_done"), sem("rlo_done")
    xtr, x_scaled, g_mm, gm_done, bt_done = (sem(n) for n in ("xtr", "x_scaled", "g_mm", "gm_done", "bt_done"))
    diff, exped, m_done = sem("diff"), sem("exped"), sem("m_done")
    ecum_mm, ec_done, inter_mm, yi_done, yid_done, dx_done = (
        sem(n) for n in ("ecum_mm", "ec_done", "inter_mm", "yi_done", "yid_done", "dx_done"))
    ds_mm, smul, s_done = sem("ds_mm"), sem("smul"), sem("s_done")
    intra_mm, ya_done, y_done, yhi_done, ylo_done, ysq_done = (
        sem(n) for n in ("intra_mm", "ya_done", "y_done", "yhi_done", "ylo_done", "ysq_done"))
    rms_mm, rv_done, pow_done, out_mm, h_done = (sem(n) for n in ("rms_mm", "rv_done", "pow_done", "out_mm", "h_done"))

    W_IN = ins["m_in_w"]
    W_OUT = ins["m_out_w"]

    def chunks(e, l, body):
        body(0, l * TT, True, False)
        with e.Fori(1, TT - 1) as i:
            body(i, l * TT + i, False, False)
        body(TT - 1, l * TT + TT - 1, False, True)

    def heads(x):
        return x.rearrange("p (h q) -> p h q", h=H2)

    def sp(e):
        e.dma_start(kept, t[:]).then_inc(t_kept, 16)
        with e.Fori(0, LAYERS) as l:
            e.wait_ge(layer_open, l + 1)
            e.dma_start(par[:], ins["m_par"][l, :, :]).then_inc(par_in, 16)
            for n in range(MB_PIECES):
                if n >= 2:
                    e.wait_ge(w_hi, l * MB_PIECES + n - 1)
                    e.wait_ge(w_lo, l * MB_PIECES + n - 1)
                if n < KD:
                    e.dma_start(raw[n % 2], W_IN[l, n * P:(n + 1) * P, :]).then_inc(raw_in[n % 2], 16)
                else:
                    e.dma_start(raw[n % 2][:, 0:4 * D].rearrange("p (j f) -> p j f", j=4),
                                W_OUT[l, (n - KD) * 512:(n - KD + 1) * 512, :].rearrange("(j p) f -> p j f", p=P))\
                        .then_inc(raw_in[n % 2], 16)

        e.wait_ge(layer_open, LAYERS + 1)
        e.dma_start(uf, kept).then_inc(t_back, 16)

    def dve(e):
        own = Chain(e, dve_own)

        def loop8(body):
            base = own.n
            with e.Fori(0, TT) as i:
                own.n = base + i
                body(i).then_inc(dve_own, 1)
            own.n = base + TT
            e.wait_ge(dve_own, own.n)
            core.apart(e)

        def layernorm(src, n):
            loop8(lambda i: e.bn_stats(stats[:, i, :], src[:, i, :]))
            for i in range(TT):
                x = e.bn_aggr(mv[:, i, :], stats[:, i, :])
            own(x)
            e.tensor_scalar(rstd[:], mv[:, :, 1], MB_EPS, None, ALU.add).then_inc(var_done, 1)
            e.wait_ge(sd_done, n)
            own(e.reciprocal(rstd[:], rstd[:]))

        e.wait_ge(t_kept, 16)
        e.tensor_copy(tri_th[:], core.tri16[:].unsqueeze(2).to_broadcast([P, P, H2]))
        layernorm(t, 1)
        loop8(lambda i: e.tensor_scalar(h[:, i, :], t[:, i, :], mv[:, i, 0:1], rstd[:, ds(i, 1)],
                                        ALU.subtract, ALU.mult))
        e.tensor_copy(rv[:], rstd[:, 0:1]).then_inc(layer_open, 1)

        start = own.n
        with e.Fori(0, LAYERS) as l:
            own.n = start + l * OWN_PER_LAYER
            e.wait_ge(layer_open, l + 1)
            core.apart(e)
            layernorm(h, l + 2)
            core.apart(e)
            with e.Fori(0, TT) as i:
                e.tensor_scalar(un[:, i, :], h[:, i, :], mv[:, i, 0:1], rstd[:, ds(i, 1)],
                                ALU.subtract, ALU.mult).then_inc(un_done, 1)
            e.wait_ge(par_in, (l + 1) * 16)
            core.apart(e)
            own(e.tensor_scalar(par[:, MB_CVW:MB_DCOL], par[:, MB_CVW:MB_DCOL], 0.5, None, ALU.mult))
            for n in range(MB_PIECES):
                e.wait_ge(w_hi, l * MB_PIECES + n + 1)
                if n < KD:
                    e.tensor_tensor(wi_lo[:, n, :], raw[n % 2], wi_hi[:, n, :], ALU.subtract).then_inc(w_lo, 1)
                else:
                    for q in range(4):
                        j = 4 * (n - KD) + q
                        x = e.scalar_tensor_tensor(out=wo_lo[:, j, :], in0=raw[n % 2][:, q * D:(q + 1) * D],
                                                   scalar=par[:, MB_RMSW + j:MB_RMSW + j + 1], in1=wo_hi[:, j, :],
                                                   op0=ALU.mult, op1=ALU.subtract)
                    x.then_inc(w_lo, 1)
            core.apart(e)
            with e.Fori(0, TT) as i:
                e.wait_ge(uhi_done, l * TT + i + 1)
                e.tensor_tensor(u_lo[:, :, ds(i * P, P)], uf[:, i, :].rearrange("p (k c) -> p k c", k=KD),
                                u_hi[:, :, ds(i * P, P)], ALU.subtract).then_inc(ulo_done, 1)
            e.wait_ge(dt_mm, l + 1)
            own(e.tensor_tensor(dtx[:], ps[:, 2, 0:TT * H2].rearrange("p (i h) -> p i h", i=TT),
                                par[:, MB_DTB:MB_DTB + H2].unsqueeze(1).to_broadcast([P, TT, H2]), ALU.add))
            e.scalar_tensor_tensor(out=dtn[:], in0=dtx[:], scalar=-1.0, in1=dtx[:], op0=ALU.mult, op1=ALU.min)\
                .then_inc(dtn_done, 1)
            e.wait_ge(dt_log, l + 1)
            own(e.scalar_tensor_tensor(out=dt[:], in0=dtx[:], scalar=0.0, in1=dte_[:], op0=ALU.max, op1=ALU.add))
            e.wait_ge(nega_done, l + 1)
            e.tensor_tensor(la[:], dt[:], nega[:].unsqueeze(1).to_broadcast([P, TT, H2]), ALU.mult).then_inc(la_done, 1)
            e.wait_ge(la_done, l + 1)
            own(e.tensor_copy(la_hi[:], la[:]))
            own(e.tensor_tensor(la_lo[:], la[:], la_hi[:], ALU.subtract))
            e.wait_ge(sums_exp, l + 1)
            e.tensor_tensor(dte[:], dend[:], dt[:], ALU.mult).then_inc(prep, 1)
            e.wait_ge(prep, l + 1)

            def r_build(i):
                e.tensor_tensor(r_lo, la_lo[:, i, :].unsqueeze(1).to_broadcast([P, P, H2]), tri_th[:], ALU.mult)\
                    .then_inc(rlo_done, 1)

            def conv(g):
                for q in range(2):
                    e.wait_ge(x_ev, 2 * g + q + 1)
                    for k in range(TAPS):
                        for j in range(4 * q, 4 * q + 4):
                            w = par[:, MB_CVW + 4 * j + k:MB_CVW + 4 * j + k + 1]
                            if k == 0:
                                x = e.tensor_scalar(ca[:, j, :], xp[:, j, 0:P], w, par[:, MB_CVB + j:MB_CVB + j + 1],
                                                    ALU.mult, ALU.add)
                            else:
                                x = e.scalar_tensor_tensor(out=ca[:, j, :], in0=xp[:, j, k:k + P], scalar=w,
                                                           in1=ca[:, j, :], op0=ALU.mult, op1=ALU.add)
                        if k < TAPS - 1:
                            own(x)
                    x.then_inc(acc, 1)
                e.wait_ge(bc_ev, g + 1)
                for k in range(TAPS):
                    for c in range(2):
                        w = par[0:NS, MB_BCW + 4 * c + k:MB_BCW + 4 * c + k + 1]
                        if k == 0:
                            x = e.tensor_scalar(cbc[:, c, :], bcp[:, c, 0:P], w, par[0:NS, MB_BCB + c:MB_BCB + c + 1],
                                                ALU.mult, ALU.add)
                        else:
                            x = e.scalar_tensor_tensor(out=cbc[:, c, :], in0=bcp[:, c, k:k + P], scalar=w,
                                                       in1=cbc[:, c, :], op0=ALU.mult, op1=ALU.add)
                    if k < TAPS - 1:
                        own(x)
                x.then_inc(acc, 1)
                for q in range(2):
                    e.wait_ge(tanh, 3 * g + q + 1)
                    e.scalar_tensor_tensor(out=xc[:, 4 * q:4 * q + 4, :], in0=th[:, 4 * q:4 * q + 4, :], scalar=1.0,
                                           in1=ca[:, 4 * q:4 * q + 4, :], op0=ALU.add, op1=ALU.mult).then_inc(xc_done, 1)
                e.wait_ge(tanh, 3 * g + 3)
                e.scalar_tensor_tensor(out=bcc[:], in0=thbc[:], scalar=1.0, in1=cbc[:], op0=ALU.add, op1=ALU.mult)\
                    .then_inc(bcc_done, 1)

            def gate(g):
                for q in range(2):
                    e.wait_ge(thz_done, 2 * g + q + 1)
                    e.scalar_tensor_tensor(out=sz[:, 4 * q:4 * q + 4, :], in0=thz[:, 4 * q:4 * q + 4, :], scalar=1.0,
                                           in1=ps[:, 1 - q, :].rearrange("p (j t) -> p j t", j=4),
                                           op0=ALU.add, op1=ALU.mult).then_inc(sz_done, 1)

            def finish(i, g):
                e.wait_ge(rms_mm, g + 1)
                e.tensor_scalar(rv[:], ps[:, 2, 384:385], 1.0 / DI, 4 * MB_EPS, ALU.mult, ALU.add).then_inc(rv_done, 1)
                e.wait_ge(pow_done, g + 1)
                e.wait_ge(out_mm, g + 1)
                e.scalar_tensor_tensor(out=h[:, i, :], in0=ps[:, 7, :], scalar=rs[:], in1=h[:, i, :],
                                       op0=ALU.mult, op1=ALU.add).then_inc(h_done, 1)

            def split_y(g):
                e.wait_ge(yhi_done, g + 1)
                e.tensor_tensor(y_lo[:], y, y_hi[:], ALU.subtract).then_inc(ylo_done, 1)

            r_build(0)
            conv(l * TT)
            gate(l * TT)

            def body(i, g, is_first, is_last):
                if not is_first:
                    split_y(g - 1)
                e.wait_ge(g_mm, g + 1)
                e.tensor_tensor(gm[:], ps[:, 2, P:2 * P], core.tri[:], ALU.mult).then_inc(gm_done, 1)
                e.wait_ge(xtr, g + 1)
                xt = heads(ps[:, 5:7, :].rearrange("p b n -> p (b n)"))
                e.tensor_tensor(heads(xdt[:]), xt, dt[:, i, :].unsqueeze(2).to_broadcast([P, H2, 32]), ALU.mult)
                e.tensor_tensor(heads(xe[:]), xt, dte[:, i, :].unsqueeze(2).to_broadcast([P, H2, 32]), ALU.mult)\
                    .then_inc(x_scaled, 1)
                e.wait_ge(gm_done, g + 1)
                for k in range(MB_EG):
                    e.wait_ge(exped, g * MB_EG + k + 1)
                    e.tensor_tensor(M[:].rearrange("p h t -> p t h")[:, 16 * k:16 * k + 16, :],
                                    E[:, 512 * (k % MB_ER):512 * (k % MB_ER + 1)].rearrange("p (t h) -> p t h", h=H2),
                                    gm[:, 16 * k:16 * k + 16].unsqueeze(2).to_broadcast([P, 16, H2]), ALU.mult)\
                        .then_inc(m_done, 1)
                if not is_first:
                    finish(i - 1, g - 1)
                e.wait_ge(inter_mm, g + 1)
                e.wait_ge(ec_done, g + 1)
                e.tensor_tensor(yi.rearrange("p j t -> p (j t)"), ps[:, 5:7, :].rearrange("p b n -> p (b n)"),
                                ec.rearrange("p j t -> p (j t)"), ALU.mult).then_inc(yi_done, 1)
                e.wait_ge(ds_mm, g + 1)
                e.wait_ge(smul, g + 1)
                e.tensor_tensor(S[:], S[:], ps[0:NS, 3:5, :].rearrange("p b n -> p (b n)"), ALU.add).then_inc(s_done, 1)
                if not is_last:
                    e.wait_ge(diff, MB_EG * (g + 1))
                    r_build(i + 1)
                    e.wait_ge(dx_done, g + 1)
                    conv(g + 1)
                e.wait_ge(intra_mm, g + 1)
                e.wait_ge(yid_done, g + 1)
                e.tensor_tensor(y[:, 0:4, :], ps[:, 7, :].rearrange("p (j t) -> p j t", j=4), yi[:, 0:4, :], ALU.add)
                e.tensor_tensor(y[:, 4:8, :], ps[:, 2, :].rearrange("p (j t) -> p j t", j=4), yi[:, 4:8, :], ALU.add)\
                    .then_inc(ya_done, 1)
                e.wait_ge(ya_done, g + 1)
                e.tensor_tensor(y, y, sz[:], ALU.mult).then_inc(y_done, 1)
                if not is_last:
                    e.wait_ge(y_done, g + 1)
                    gate(g + 1)

            own_before = own.n
            body(0, l * TT, True, False)
            per_chunk = OWN_PER_CONV
            own.n = own_before + per_chunk
            with e.Fori(1, TT - 1) as i:
                own.n = own_before + i * per_chunk
                body(i, l * TT + i, False, False)
            own.n = own_before + (TT - 1) * per_chunk
            body(TT - 1, l * TT + TT - 1, False, True)
            split_y(l * TT + TT - 1)
            finish(TT - 1, l * TT + TT - 1)
            e.wait_ge(h_done, (l + 1) * TT)
            e.tensor_copy(rv[:], rstd[:, 0:1]).then_inc(layer_open, 1)
        e.wait_ge(layer_open, LAYERS + 1)
        e.wait_ge(t_back, 16)
        e.tensor_tensor(t[:], h[:], uf, ALU.add)

    OWN_PER_CONV = 2 * (TAPS - 1) + TAPS - 1
    OWN_PER_LAYER = TT + 1 + 1 + 1 + 1 + 1 + 1 + 1 + TT * OWN_PER_CONV

    def act(e):
        own = Chain(e, act_own)
        e.wait_ge(var_done, 1)
        e.activation(rstd[:], rstd[:], ACT.Sqrt).then_inc(sd_done, 1)
        with e.Fori(0, LAYERS) as l:
            e.wait_ge(layer_open, l + 1)
            e.wait_ge(var_done, l + 2)
            e.activation(rstd[:], rstd[:], ACT.Sqrt).then_inc(sd_done, 1)
            e.wait_ge(par_in, (l + 1) * 16)
            with e.Fori(0, TT) as i:
                e.wait_ge(turned, l * TT + i + 1)
                for k in range(KD):
                    x = e.activation(uf[:, i, k * P:(k + 1) * P], ps[:, i, k * P:(k + 1) * P], ACT.Identity,
                                     scale=par[:, MB_LNW + k:MB_LNW + k + 1], bias=par[:, MB_LNB + k:MB_LNB + k + 1])
                x.then_inc(uf_done, 1)
            for n in range(MB_PIECES):
                e.wait_ge(raw_in[n % 2], (l * (MB_PIECES // 2) + n // 2 + 1) * 16)
                if n < KD:
                    e.activation(wi_hi[:, n, :], raw[n % 2], ACT.Copy).then_inc(w_hi, 1)
                else:
                    for q in range(4):
                        j = 4 * (n - KD) + q
                        x = e.activation(wo_hi[:, j, :], raw[n % 2][:, q * D:(q + 1) * D], ACT.Copy,
                                         scale=par[:, MB_RMSW + j:MB_RMSW + j + 1])
                    x.then_inc(w_hi, 1)
            own.n = l * 4
            own(e.activation(nega[:], par[:, MB_ALOG:MB_ALOG + H2], ACT.Exp))
            e.mul(nega[:], nega[:], -1.0).then_inc(nega_done, 1)
            e.wait_ge(dtn_done, l + 1)
            own(e.activation(dte_[:], dtn[:], ACT.Exp))
            e.activation(dte_[:], dte_[:], ACT.Ln, bias=1.0).then_inc(dt_log, 1)
            e.wait_ge(sums_mm, l + 1)
            own(e.activation(dend[:], ps[:, 3, 0:TT * H2].rearrange("p (i h) -> p i h", i=TT), ACT.Exp))
            own(e.activation(edec[:], ps[:, 3, TT * H2:2 * TT * H2].rearrange("p (i h) -> p i h", i=TT), ACT.Exp))
            e.activation(cumT[:], ps[0:H2, 4:6, :].rearrange("p b n -> p (b n)"), ACT.Copy).then_inc(sums_exp, 1)

            def project_x(g, is_first):
                if not is_first:
                    e.wait_ge(halo, g)
                for q in range(2):
                    e.wait_ge(x_mm, 2 * g + q + 1)
                    e.activation(xp[:, 4 * q:4 * q + 4, 3:P + 3], ps[:, q, :].rearrange("p (j t) -> p j t", j=4),
                                 ACT.Copy).then_inc(x_ev, 1)
                e.wait_ge(bc_mm, g + 1)
                e.activation(bcp[:, :, 3:P + 3], ps[0:NS, 0, 0:2 * P].rearrange("p (c t) -> p c t", c=2), ACT.Copy)\
                    .then_inc(bc_ev, 1)
                for q in range(2):
                    e.wait_ge(acc, 3 * g + q + 1)
                    e.activation(th[:, 4 * q:4 * q + 4, :], ca[:, 4 * q:4 * q + 4, :], ACT.Tanh).then_inc(tanh, 1)
                e.wait_ge(acc, 3 * g + 3)
                e.activation(thbc[:], cbc[:], ACT.Tanh).then_inc(tanh, 1)

            def project_z(g):
                e.wait_ge(xc_done, 2 * g + 2)
                for q in range(2):
                    e.wait_ge(z_mm, 2 * g + q + 1)
                    e.activation(thz[:, 4 * q:4 * q + 4, :], ps[:, 1 - q, :].rearrange("p (j t) -> p j t", j=4),
                                 ACT.Tanh, scale=0.5).then_inc(thz_done, 1)

            def split_y(g):
                e.wait_ge(y_done, g + 1)
                e.activation(y_hi[:], y, ACT.Copy).then_inc(yhi_done, 1)
                e.activation(ysq[:], y, ACT.Square).then_inc(ysq_done, 1)

            e.wait_ge(zeroed, l + 1)
            project_x(l * TT, True)
            project_z(l * TT)

            def body(i, g, is_first, is_last):
                if not is_first:
                    split_y(g - 1)
                e.wait_ge(gm_done, g + 1)
                e.activation(btok[:], ps[:, 2, 0:NS], ACT.Copy).then_inc(bt_done, 1)
                for k in range(MB_EG):
                    e.wait_ge(diff, MB_EG * g + k + 1)
                    if k >= MB_ER:
                        e.wait_ge(m_done, MB_EG * g + k - MB_ER + 1)
                    e.activation(E[:, 512 * (k % MB_ER):512 * (k % MB_ER + 1)], ps[:, 3 + k % 2, :], ACT.Exp).then_inc(exped, 1)
                e.wait_ge(ecum_mm, g + 1)
                e.activation(ec.rearrange("p j t -> p (j t)"), ps[:, 3:5, :].rearrange("p b n -> p (b n)"), ACT.Exp)\
                    .then_inc(ec_done, 1)
                if not is_last:
                    project_x(g + 1, False)
                    project_z(g + 1)

            chunks(e, l, body)
            split_y(l * TT + TT - 1)

    def pool(e):
        e.memset(mhalf[:], -0.5).then_inc(pool_own, 1)
        e.wait_ge(pool_own, 1)
        with e.Fori(0, LAYERS) as l:
            e.wait_ge(layer_open, l + 1)
            core.apart(e)
            e.memset(S[:], 0.0)
            e.memset(bcp[:, :, 0:3], 0.0)
            e.memset(xp[:, :, 0:3], 0.0).then_inc(zeroed, 1)
            with e.Fori(0, TT) as i:
                e.wait_ge(uf_done, l * TT + i + 1)
                core.apart(e)
                e.tensor_copy(u_hi[:, :, ds(i * P, P)], uf[:, i, :].rearrange("p (k c) -> p k c", k=KD)).then_inc(uhi_done, 1)
            e.wait_ge(prep, l + 1)

            def r_build(i):
                e.tensor_tensor(r_hi, la_hi[:, i, :].unsqueeze(1).to_broadcast([P, P, H2]), tri_th[:], ALU.mult)\
                    .then_inc(rhi_done, 1)

            def keep_halo(g):
                e.wait_ge(acc, 3 * (g + 1))
                core.apart(e)
                e.tensor_copy(bcp[:, :, 0:3], bcp[:, :, P:P + 3])
                e.tensor_copy(xp[:, :, 0:3], xp[:, :, P:P + 3]).then_inc(halo, 1)

            def power(g):
                e.wait_ge(rv_done, g + 1)
                e.tensor_tensor(rs[:], rv[:], mhalf[:], ALU.pow).then_inc(pow_done, 1)

            r_build(0)
            keep_halo(l * TT)

            def body(i, g, is_first, is_last):
                if not is_first:
                    power(g - 1)
                    e.wait_ge(s_done, g)
                e.wait_ge(inter_mm, g + 1)
                e.tensor_tensor(heads(S[:]), heads(S[:]), edec[0:NS, i, :].unsqueeze(2).to_broadcast([NS, H2, 32]),
                                ALU.mult).then_inc(smul, 1)
                e.wait_ge(xc_done, 2 * (g + 1))
                e.tensor_tensor(dx, xc[:], par[:, MB_DCOL:MB_DCOL + JD].unsqueeze(2).to_broadcast([P, JD, P]), ALU.mult)\
                    .then_inc(dx_done, 1)
                e.wait_ge(dx_done, g + 1)
                e.wait_ge(yi_done, g + 1)
                e.tensor_tensor(yi, yi, dx, ALU.add).then_inc(yid_done, 1)
                if not is_last:
                    e.wait_ge(diff, MB_EG * (g + 1))
                    r_build(i + 1)
                    keep_halo(g + 1)

            chunks(e, l, body)
            power(l * TT + TT - 1)

    def pe(e):
        with e.Fori(0, LAYERS) as l:
            e.wait_ge(layer_open, l + 1)
            for i in range(TT):
                e.wait_ge(un_done, l * TT + i + 1)
                for k in range(KD):
                    x = e.transpose(ps[:, i, k * P:(k + 1) * P], un[:, i, k * P:(k + 1) * P], core.ident[:])
                x.then_inc(turned, 1)
            e.wait_ge(w_lo, l * MB_PIECES + KD)
            e.wait_ge(uf_done, (l + 1) * TT)
            core.apart(e)
            with e.Fori(0, TT) as i:
                e.wait_ge(ulo_done, l * TT + i + 1)
                core.apart(e)
                for k in range(KD):
                    for n, (a, b) in enumerate(((u_hi, wi_hi), (u_hi, wi_lo), (u_lo, wi_hi))):
                        x = e.matmul(ps[:, 2, ds(i * H2, H2)], a[:, k, ds(i * P, P)], b[:, k, MB_CDT:MB_CDT + H2],
                                     start=(k == 0 and n == 0), stop=(k == KD - 1 and n == 2))
                x.then_inc(dt_done_mm, 1)
            x = e.matmul(ps[0:1, 6, 0:1], core.ones[:, 0:1], core.ones[:, 0:1], start=True, stop=True)
            x.then_inc(dt_mm, 1)
            e.wait_ge(la_done, l + 1)
            la2 = la[:].rearrange("p i h -> p (i h)")
            e.matmul(ps[:, 3, 0:TT * H2], core.after[:], la2, start=True, stop=True)
            e.matmul(ps[:, 3, TT * H2:2 * TT * H2], core.ones[:], la2, start=True, stop=True)
            for i in range(TT):
                x = e.matmul(ps[0:H2, 4 + i // 4, (i % 4) * P:(i % 4 + 1) * P], la[:, i, :], core.tri[:], start=True, stop=True)
            x.then_inc(sums_mm, 1)

            def project(i, bank, tiles, width, done):
                for n, f in enumerate(tiles):
                    for k in range(KD):
                        for m, (a, b) in enumerate(((wi_hi, u_hi), (wi_lo, u_hi), (wi_hi, u_lo))):
                            x = e.matmul(ps[0:width, bank, n * P:(n + 1) * P], a[:, k, f:f + width],
                                         b[:, k, ds(i * P, P)], start=(k == 0 and m == 0), stop=(k == KD - 1 and m == 2))
                x.then_inc(done, 1)

            def project_x(i, g, is_first):
                if not is_first:
                    e.wait_ge(sz_done, 2 * g)
                for q in range(2):
                    project(i, q, [MB_CX + P * j for j in range(4 * q, 4 * q + 4)], P, x_mm)
                e.wait_ge(x_ev, 2 * g + 1)
                core.apart(e)
                project(i, 0, [MB_CB, MB_CC], NS, bc_mm)

            def project_z(i, g):
                e.wait_ge(x_ev, 2 * g + 2)
                project(i, 1, [P * j for j in range(4)], P, z_mm)
                e.wait_ge(bc_ev, g + 1)
                project(i, 0, [P * j for j in range(4, 8)], P, z_mm)

            def out_project(i, g):
                e.wait_ge(ysq_done, g + 1)
                for j in range(JD):
                    x = e.matmul(ps[:, 2, 384:385], ysq[:, j, :], core.ones[:, 0:1], start=(j == 0), stop=(j == JD - 1))
                x.then_inc(rms_mm, 1)
                e.wait_ge(ylo_done, g + 1)
                for j in range(JD):
                    for m, (a, b) in enumerate(((y_hi, wo_hi), (y_hi, wo_lo), (y_lo, wo_hi))):
                        x = e.matmul(ps[:, 7, :], a[:, j, :], b[:, j, :], start=(j == 0 and m == 0),
                                     stop=(j == JD - 1 and m == 2))
                x.then_inc(out_mm, 1)

            e.wait_ge(sums_exp, l + 1)
            e.wait_ge(w_lo, (l + 1) * MB_PIECES)
            project_x(0, l * TT, True)
            project_z(0, l * TT)

            def body(i, g, is_first, is_last):
                e.wait_ge(xc_done, 2 * (g + 1))
                e.wait_ge(bcc_done, g + 1)
                if not is_first:
                    e.wait_ge(yi_done, g)
                    e.wait_ge(ya_done, g)
                core.apart(e)
                e.transpose(ps[:, 2, 0:NS], bcc[:, 0, :], core.ident[0:NS, 0:NS])
                e.matmul(ps[:, 2, P:2 * P], bcc[:, 0, :], bcc[:, 1, :], start=True, stop=True).then_inc(g_mm, 1)
                for j in range(JD):
                    x = e.transpose(ps[:, 5 + j // 4, (j % 4) * P:(j % 4 + 1) * P], xc[:, j, :], core.ident[:])
                x.then_inc(xtr, 1)
                e.wait_ge(rhi_done, g + 1)
                e.wait_ge(rlo_done, g + 1)
                if not is_first:
                    e.wait_ge(s_done, g)
                for k in range(MB_EG):
                    if k >= 2:
                        e.wait_ge(exped, MB_EG * g + k - 1)
                    for m, r in enumerate((r_hi, r_lo)):
                        x = e.matmul(ps[:, 3 + k % 2, :], core.after16[:], r[:, 16 * k:16 * k + 16, :].rearrange("p t h -> p (t h)"),
                                     start=(m == 0), stop=(m == 1))
                    x.then_inc(diff, 1)
                e.wait_ge(gm_done, g + 1)
                e.wait_ge(bt_done, g + 1)
                if not is_first:
                    out_project(i - 1, g - 1)
                e.wait_ge(exped, MB_EG * (g + 1))
                for j in range(JD):
                    x = e.matmul(ps[:, 3 + j // 4, (j % 4) * P:(j % 4 + 1) * P], core.sel[:, j, :], cumT[:, ds(i * P, P)],
                                 start=True, stop=True)
                x.then_inc(ecum_mm, 1)
                e.wait_ge(x_scaled, g + 1)
                for j in range(JD):
                    x = e.matmul(ps[:, 5 + j // 4, (j % 4) * P:(j % 4 + 1) * P], S[:, j * P:(j + 1) * P], bcc[:, 1, :],
                                 start=True, stop=True)
                x.then_inc(inter_mm, 1)
                e.wait_ge(ec_done, g + 1)
                for q in range(2):
                    x = e.matmul(ps[0:NS, 3 + q, :], btok[:], xe[:, q * 512:(q + 1) * 512], start=True, stop=True)
                x.then_inc(ds_mm, 1)
                if not is_last:
                    project_x(i + 1, g + 1, False)
                e.wait_ge(m_done, MB_EG * (g + 1))
                if not is_first:
                    e.wait_ge(h_done, g)
                for hh in range(H2):
                    bank = 7 if hh < 16 else 2
                    c = (hh // 4) % 4
                    x = e.matmul(ps[32 * (hh % 4):32 * (hh % 4) + 32, bank, c * P:(c + 1) * P],
                                 xdt[:, 32 * hh:32 * hh + 32], M[:, hh, :], start=True, stop=True)
                x.then_inc(intra_mm, 1)
                if not is_last:
                    project_z(i + 1, g + 1)

            chunks(e, l, body)
            out_project(TT - 1, l * TT + TT - 1)

    dt_done_mm = sem("dt_done_mm")
    t_kept, t_back = sem("t_kept"), sem("t_back")
    return dict(sp=sp, dve=dve, act=act, pe=pe, pool=pool, cx=cx, used=used)


FF_QEPS = 1e-5
FF_MAGIC = 1.5 * 2.0 ** 23
FF_RSQ = float(np.float32(1 / np.sqrt(D)))


def stage_ffn(core, ps):
    nc, ins, t = core.nc, core.ins, core.t
    cx = ExitStack()
    sb = lambda n, s, d=F32: core.sb("f_" + n, s, d, cx)
    used = []
    sem = lambda n: core.stage_sem("f_" + n, cx, used)
    wn = sb("wn", [P, KD, D])
    low = sb("low", [P, KD, D])
    tern = sb("tern", [P, KD, D])
    ternT = sb("ternT", [P, KD, D], F16)
    had = sb("had", [P, KD, D], F16)
    asum, scale, half, nhalf = (sb(n, [P, KD]) for n in ("asum", "scale", "half", "nhalf"))
    diag = sb("diag", [P, KD, P])
    wscale = sb("wscale", [P, D])
    stats, mv, rstd = sb("stats", [P, TT, 6]), sb("mv", [P, TT, 2]), sb("rstd", [P, TT])
    un, u32 = sb("un", [P, D]), sb("u32", [P, D])
    u_hi, u_lo = sb("u_hi", [P, D], F16), sb("u_lo", [P, D], F16)
    amax, tscale, inv, mult = (sb(n, [P, 1]) for n in ("amax", "tscale", "inv", "mult"))
    qa, qb = sb("qa", [P, D]), sb("qb", [P, D])
    qf = sb("qf", [P, D])
    qT = sb("qT", [P, D], F16)
    upd = sb("upd", [P, D])

    w_in, had_in = sem("w_in"), sem("had_in")
    dve_own = sem("dve_own")
    var_done, sd_done = sem("var_done"), sem("sd_done")
    tern_done, wsc_done = sem("tern_done"), sem("wsc_done")
    w_tr, w_ev, wsc_mm = sem("w_tr"), sem("w_ev"), sem("wsc_mm")
    un_done, turned, u32_done, hi_done, lo_done = (sem(n) for n in ("un_done", "turned", "u32_done", "hi_done", "lo_done"))
    h_mm, q_done, q_tr, q_ev, o_mm, o_done, t_done = (sem(n) for n in ("h_mm", "q_done", "q_tr", "q_ev", "o_mm", "o_done", "t_done"))

    def sp(e):
        e.dma_start(wn[:], ins["f_w"].rearrange("(j p) i -> p j i", p=P)).then_inc(w_in, 16)
        e.dma_start(had[:], ins["c_had"].rearrange("(k p) n -> p k n", p=P)).then_inc(had_in, 16)

    def tiles(e, first, both, last):
        first(0)
        with e.Fori(0, TT - 1) as i:
            both(i)
        last(TT - 1)

    def dve(e):
        own = Chain(e, dve_own)
        with e.Fori(0, TT) as i:
            e.bn_stats(stats[:, i, :], t[:, i, :]).then_inc(dve_own, 1)
        own.n = TT
        e.wait_ge(dve_own, TT)
        for i in range(TT):
            x = e.bn_aggr(mv[:, i, :], stats[:, i, :])
        own(x)
        e.tensor_scalar(rstd[:], mv[:, :, 1], 1e-5, None, ALU.add).then_inc(var_done, 1)
        e.wait_ge(w_in, 16)
        own(e.tensor_reduce(asum[:], wn[:], AX.X, ALU.add, apply_absolute_value=True))
        own(e.tensor_scalar(scale[:], asum[:], 1.0 / D, FF_QEPS, ALU.mult, ALU.max))
        e.tensor_scalar(half[:], scale[:], 0.5, None, ALU.mult)
        own(e.tensor_scalar(nhalf[:], scale[:], -0.5, None, ALU.mult))
        for j in range(KD):
            e.tensor_scalar(diag[:, j, :], core.ident[:], scale[:, j:j + 1], None, ALU.mult)
            own(e.tensor_scalar(low[:, j, :], wn[:, j, :], nhalf[:, j:j + 1], None, ALU.is_lt))
            e.scalar_tensor_tensor(out=tern[:, j, :], in0=wn[:, j, :], scalar=half[:, j:j + 1], in1=low[:, j, :],
                                   op0=ALU.is_gt, op1=ALU.subtract).then_inc(tern_done, 1)
        e.wait_ge(sd_done, 1)
        own(e.reciprocal(rstd[:], rstd[:]))
        e.wait_ge(wsc_done, 1)
        base = own.n

        def rotate(i, n):
            e.tensor_scalar(un[:], t[:, i, :], mv[:, i, 0:1], rstd[:, ds(i, 1)], ALU.subtract, ALU.mult)\
                .then_inc(un_done, 1)
            e.wait_ge(hi_done, n + 1)
            e.tensor_tensor(u_lo[:], u32[:], u_hi[:], ALU.subtract).then_inc(lo_done, 1)

        def quant(i):
            own.n = base + OWN_Q * i
            e.wait_ge(h_mm, i + 1)
            own(e.tensor_reduce(amax[:], ps[:, 1, :], AX.X, ALU.max, apply_absolute_value=True))
            own(e.tensor_scalar(tscale[:], amax[:], FF_RSQ, FF_QEPS, ALU.mult, ALU.max))
            own(e.tensor_scalar(tscale[:], tscale[:], 1.0 / 7, None, ALU.mult))
            own(e.reciprocal(inv[:], tscale[:]))
            own(e.tensor_scalar(mult[:], inv[:], FF_RSQ, None, ALU.mult))
            own(e.tensor_scalar(qa[:], ps[:, 1, :], mult[:, 0:1], FF_MAGIC, ALU.mult, ALU.add))
            own(e.tensor_scalar(qb[:], qa[:], FF_MAGIC, -8.0, ALU.subtract, ALU.max))
            e.tensor_scalar(qf[:], qb[:], 7.0, None, ALU.min).then_inc(q_done, 1)

        def product(i):
            e.wait_ge(o_mm, i + 1)
            e.scalar_tensor_tensor(out=upd[:], in0=ps[:, 3, :], scalar=tscale[:, 0:1], in1=wscale[:], op0=ALU.mult,
                                   op1=ALU.mult).then_inc(o_done, 1)
            e.wait_ge(o_done, i + 1)
            e.tensor_tensor(t[:, i, :], t[:, i, :], upd[:], ALU.add).then_inc(t_done, 1)

        rotate(0, 0)
        with e.Fori(0, TT - 1) as i:
            quant(i)
            e.wait_ge(lo_done, i + 1)
            e.wait_ge(turned, i + 1)
            rotate(i + 1, i + 1)
            product(i)
            e.wait_ge(t_done, i + 1)
            core.apart(e)
        quant(TT - 1)
        product(TT - 1)

    OWN_Q = 7

    def act(e):
        e.wait_ge(var_done, 1)
        e.activation(rstd[:], rstd[:], ACT.Sqrt).then_inc(sd_done, 1)
        for k in range(KD):
            e.wait_ge(w_tr, k + 1)
            e.activation(ternT[:, k, :], ps[:, 4 + k % 2, :], ACT.Copy).then_inc(w_ev, 1)
        e.wait_ge(wsc_mm, 1)
        e.activation(wscale[:], ps[:, 6, :], ACT.Copy).then_inc(wsc_done, 1)

        def rotate(n):
            e.wait_ge(turned, n + 1)
            e.activation(u32[:], ps[:, 0, :], ACT.Copy).then_inc(u32_done, 1)
            e.wait_ge(u32_done, n + 1)
            e.activation(u_hi[:], u32[:], ACT.Copy).then_inc(hi_done, 1)

        def quant(i):
            e.wait_ge(q_tr, i + 1)
            e.activation(qT[:], ps[:, 2, :], ACT.Copy).then_inc(q_ev, 1)

        rotate(0)
        with e.Fori(0, TT - 1) as i:
            e.wait_ge(h_mm, i + 1)
            rotate(i + 1)
            quant(i)
        quant(TT - 1)

    def pe(e):
        for k in range(KD):
            if k >= 2:
                e.wait_ge(w_ev, k - 1)
            for j in range(KD):
                if k == 0:
                    e.wait_ge(tern_done, j + 1)
                x = e.transpose(ps[:, 4 + k % 2, j * P:(j + 1) * P], tern[:, j, k * P:(k + 1) * P], core.ident[:])
            x.then_inc(w_tr, 1)
        for j in range(KD):
            x = e.matmul(ps[:, 6, j * P:(j + 1) * P], core.ones[:], diag[:, j, :], start=True, stop=True)
        x.then_inc(wsc_mm, 1)
        e.wait_ge(had_in, 16)
        e.wait_ge(w_ev, KD)

        def rotate(n):
            e.wait_ge(un_done, n + 1)
            for k in range(KD):
                x = e.transpose(ps[:, 0, k * P:(k + 1) * P], un[:, k * P:(k + 1) * P], core.ident[:])
            x.then_inc(turned, 1)
            e.wait_ge(lo_done, n + 1)
            for k in range(KD):
                for m, a in enumerate((u_hi, u_lo)):
                    x = e.matmul(ps[:, 1, :], a[:, k * P:(k + 1) * P], had[:, k, :], start=(k == 0 and m == 0),
                                 stop=(k == KD - 1 and m == 1))
            x.then_inc(h_mm, 1)

        def product(i):
            for k in range(KD):
                x = e.transpose(ps[:, 2, k * P:(k + 1) * P], qf[:, k * P:(k + 1) * P], core.ident[:])
            x.then_inc(q_tr, 1)
            e.wait_ge(q_ev, i + 1)
            for k in range(KD):
                x = e.matmul(ps[:, 3, :], qT[:, k * P:(k + 1) * P], ternT[:, k, :], start=(k == 0), stop=(k == KD - 1))
            x.then_inc(o_mm, 1)

        rotate(0)
        with e.Fori(0, TT - 1) as i:
            e.wait_ge(q_done, i + 1)
            rotate(i + 1)
            product(i)
            e.wait_ge(o_done, i + 1)
            core.apart(e)
        e.wait_ge(q_done, TT)
        product(TT - 1)

    return dict(sp=sp, dve=dve, act=act, pe=pe, pool=None, cx=cx, used=used)


AT_RMS_EPS = 1.1920929e-07
AT_LN_EPS = 1e-5
AT_HN = 4
AT_HW = DI // AT_HN
AT_DPROJ = 2 * DI + AT_HN + 2 * AT_HN * NS
AT_CX, AT_CDT, AT_CBC = DI, 2 * DI, 2 * DI + AT_HN
AT_PIECES = 6


def stage_l3(core, ps):
    nc, ins, t = core.nc, core.ins, core.t
    cx = ExitStack()
    sb = lambda n, s, d=F32: core.sb("ab_" + n, s, d, cx)
    used = []
    sem = lambda n: core.stage_sem("a_" + n, cx, used)
    wi_hi, wi_lo = sb("wi_hi", [P, KD, AT_DPROJ], F16), sb("wi_lo", [P, KD, AT_DPROJ], F16)
    wo_hi, wo_lo = sb("wo_hi", [P, JD, D], F16), sb("wo_lo", [P, JD, D], F16)
    raw = [sb(f"raw{b}", [P, AT_DPROJ]) for b in range(2)]
    nw = sb("nw", [P, KD])
    inb, outb = sb("inb", [P, AT_DPROJ]), sb("outb", [P, D])
    alog, dpar, dtb = sb("alog", [P, AT_HN]), sb("dpar", [P, AT_HN]), sb("dtb", [P, AT_HN])
    nega, dtbb = sb("nega", [P, AT_HN]), sb("dtbb", [P, AT_HN])
    stats, mv = sb("stats", [P, TT, 6]), sb("mv", [P, TT, 2])
    rstd, v2, r2 = sb("rstd", [P, TT]), sb("v2", [P, TT]), sb("r2", [P, TT])
    un = sb("un", [P, 2, D])
    u_hi, u_lo = sb("u_hi", [P, KD, TOK], F16), sb("u_lo", [P, KD, TOK], F16)
    small = lambda n, d=F32: sb(n, [P, TT, AT_HN], d)
    dtx, dtn, dtl, dt, la, dend, ecum, edec, dte = (small(n) for n in "dtx dtn dtl dt la dend ecum edec dte".split())
    la_hi, la_lo = small("la_hi", F16), small("la_lo", F16)
    bc = sb("bc", [P, 2 * AT_HN * NS])
    bct = sb("bct", [NS, 2 * AT_HN, P])
    r_hi, r_lo = sb("r_hi", [P, AT_HN, P], F16), sb("r_lo", [P, AT_HN, P], F16)
    E, gm, M = sb("E", [P, AT_HN, P]), sb("gm", [P, AT_HN, P]), sb("M", [P, AT_HN, P])
    xs, xdt, xe, dx = (sb(n, [P, DI]) for n in ("xs", "xdt", "xe", "dx"))
    zt, th, sz, y1, y = (sb(n, [P, DI]) for n in ("zt", "th", "sz", "y1", "y"))
    S = sb("S", [NS, DI])
    yT_hi, yT_lo = sb("yT_hi", [P, DI], F16), sb("yT_lo", [P, DI], F16)

    dve_own, act_own = sem("dve_own"), sem("act_own")
    par_in = sem("par_in")
    raw_in = [sem(f"raw_in{b}") for b in range(2)]
    names = """w_hi w_lo var_done sd_done un_done turned hi_done lo_done dt_mm dtn_done dt_log nega_done la_done sums_mm
        sums_exp prep bias_added zeroed bc_mm x_mm z_mm bc_done x_done z_ev thz_done sz_done bct_mm bct_done g_mm
        r_done diff gm_done exped m_done inter_mm y1_done smul ds_mm s_done intra_mm xdt_done xe_done dx_done y2_done
        y3_done y_done yt_mm yhi_done ylo_done out_mm t_done""".split()
    s = {n: sem(n) for n in names}
    (w_hi, w_lo, var_done, sd_done, un_done, turned, hi_done, lo_done, dt_mm, dtn_done, dt_log, nega_done, la_done,
     sums_mm, sums_exp, prep, bias_added, zeroed, bc_mm, x_mm, z_mm, bc_done, x_done, z_ev, thz_done, sz_done, bct_mm,
     bct_done, g_mm, r_done, diff, gm_done, exped, m_done, inter_mm, y1_done, smul, ds_mm, s_done, intra_mm, xdt_done,
     xe_done, dx_done, y2_done, y3_done, y_done, yt_mm, yhi_done, ylo_done, out_mm, t_done) = (s[n] for n in names)

    def chunks(e, body):
        body(0, True, False)
        with e.Fori(1, TT - 1) as i:
            body(i, False, False)
        body(TT - 1, False, True)

    def two(a, b):
        return ps[:, a:b, :].rearrange("p b n -> p (b n)")

    def per_head(x, i):
        return x[:, i, :].unsqueeze(2).to_broadcast([P, AT_HN, AT_HW])

    def hv(x):
        return x.rearrange("p (h q) -> p h q", h=AT_HN)

    PARS = ("a_nw", "a_in_b", "a_out_b", "a_alog", "a_D", "a_dtb")

    def sp(e):
        for dst, name in zip((nw, inb, outb, alog, dpar, dtb), PARS):
            src = ins[name]
            if name != "a_nw":
                src = src.partition_broadcast(P)
            e.dma_start(dst[:], src).then_inc(par_in, 16)
        for n in range(AT_PIECES):
            if n >= 2:
                e.wait_ge(w_hi, n - 1)
                e.wait_ge(w_lo, n - 1)
            if n < KD:
                e.dma_start(raw[n % 2][:], ins["a_in_w"][n * P:(n + 1) * P, :]).then_inc(raw_in[n % 2], 16)
            else:
                e.dma_start(raw[n % 2][:, 0:4 * D].rearrange("p (j f) -> p j f", j=4),
                            ins["a_out_w"][(n - KD) * 512:(n - KD + 1) * 512, :].rearrange("(j p) f -> p j f", p=P))\
                    .then_inc(raw_in[n % 2], 16)

    PAR = 16 * len(PARS)

    def dve(e):
        own = Chain(e, dve_own)
        with e.Fori(0, TT) as i:
            e.bn_stats(stats[:, i, :], t[:, i, :]).then_inc(dve_own, 1)
        own.n = TT
        e.wait_ge(dve_own, TT)
        for i in range(TT):
            x = e.bn_aggr(mv[:, i, :], stats[:, i, :])
        own(x)
        e.tensor_scalar(rstd[:], mv[:, :, 1], AT_LN_EPS, None, ALU.add).then_inc(var_done, 1)
        e.wait_ge(sd_done, 1)
        own(e.reciprocal(rstd[:], rstd[:]))
        own(e.tensor_tensor(v2[:], rstd[:], rstd[:], ALU.mult))
        own(e.tensor_tensor(v2[:], v2[:], mv[:, :, 1], ALU.mult))
        e.tensor_scalar(r2[:], v2[:], AT_RMS_EPS, None, ALU.add).then_inc(var_done, 1)
        e.wait_ge(sd_done, 2)
        own(e.reciprocal(r2[:], r2[:]))
        own(e.tensor_tensor(rstd[:], rstd[:], r2[:], ALU.mult))
        for i in range(TT):
            if i >= 2:
                e.wait_ge(turned, i - 1)
            e.tensor_scalar(un[:, i % 2, :], t[:, i, :], mv[:, i, 0:1], rstd[:, i:i + 1], ALU.subtract, ALU.mult)\
                .then_inc(un_done, 1)
            if i >= 1:
                low_part(e, i - 1)
        low_part(e, TT - 1)
        for n in range(AT_PIECES):
            e.wait_ge(w_hi, n + 1)
            if n < KD:
                e.scalar_tensor_tensor(out=wi_lo[:, n, :], in0=raw[n % 2][:], scalar=nw[:, n:n + 1], in1=wi_hi[:, n, :],
                                       op0=ALU.mult, op1=ALU.subtract).then_inc(w_lo, 1)
            else:
                j = 4 * (n - KD)
                e.tensor_tensor(wo_lo[:, j:j + 4, :], raw[n % 2][:, 0:4 * D].rearrange("p (j f) -> p j f", j=4),
                                wo_hi[:, j:j + 4, :], ALU.subtract).then_inc(w_lo, 1)
        e.wait_ge(dt_mm, 1)
        own(e.tensor_tensor(dtbb[:], dtb[:], inb[:, AT_CDT:AT_CDT + AT_HN], ALU.add))
        own(e.tensor_tensor(dtx[:], ps[:, 6, 0:TT * AT_HN].rearrange("p (i h) -> p i h", i=TT),
                            dtbb[:].unsqueeze(1).to_broadcast([P, TT, AT_HN]), ALU.add))
        e.scalar_tensor_tensor(out=dtn[:], in0=dtx[:], scalar=-1.0, in1=dtx[:], op0=ALU.mult, op1=ALU.min)\
            .then_inc(dtn_done, 1)
        e.wait_ge(dt_log, 1)
        own(e.scalar_tensor_tensor(out=dt[:], in0=dtx[:], scalar=0.0, in1=dtl[:], op0=ALU.max, op1=ALU.add))
        e.wait_ge(nega_done, 1)
        e.tensor_tensor(la[:], dt[:], nega[:].unsqueeze(1).to_broadcast([P, TT, AT_HN]), ALU.mult).then_inc(la_done, 1)
        e.wait_ge(la_done, 1)
        own(e.tensor_copy(la_hi[:], la[:]))
        own(e.tensor_tensor(la_lo[:], la[:], la_hi[:], ALU.subtract))
        e.wait_ge(sums_exp, 1)
        e.tensor_tensor(dte[:], dend[:], dt[:], ALU.mult).then_inc(prep, 1)
        e.wait_ge(prep, 1)

        def take_bc(g):
            e.wait_ge(bc_mm, g + 1)
            e.tensor_tensor(bc[:], ps[:, 1, 0:2 * AT_HN * NS], inb[:, AT_CBC:AT_DPROJ], ALU.add).then_inc(bc_done, 1)

        def take_z(g):
            e.wait_ge(z_mm, g + 1)
            e.tensor_tensor(zt[:], two(4, 6), inb[:, 0:DI], ALU.add).then_inc(z_ev, 1)

        def gate(g):
            e.wait_ge(thz_done, g + 1)
            e.scalar_tensor_tensor(out=sz[:], in0=th[:], scalar=1.0, in1=zt[:], op0=ALU.add, op1=ALU.mult)\
                .then_inc(sz_done, 1)

        def take_x(i, g):
            e.wait_ge(x_mm, g + 1)
            e.tensor_tensor(xs[:], two(2, 4), inb[:, AT_CX:AT_CX + DI], ALU.add).then_inc(x_done, 1)
            e.wait_ge(x_done, g + 1)
            e.tensor_tensor(hv(xdt[:]), hv(xs[:]), per_head(dt, i), ALU.mult).then_inc(xdt_done, 1)

        def decays(i):
            for r, l in ((r_hi, la_hi), (r_lo, la_lo)):
                x = e.tensor_tensor(r[:], l[:, i, :].unsqueeze(2).to_broadcast([P, AT_HN, P]),
                                    core.tri16[:].unsqueeze(1).to_broadcast([P, AT_HN, P]), ALU.mult)
            x.then_inc(r_done, 1)

        take_bc(0)
        take_z(0)
        gate(0)
        take_x(0, 0)
        decays(0)

        def body(i, first, last):
            g = i
            e.wait_ge(g_mm, g + 1)
            e.tensor_tensor(gm[:], ps[:, 6, :].rearrange("p (h t) -> p h t", h=AT_HN),
                            core.tri[:].unsqueeze(1).to_broadcast([P, AT_HN, P]), ALU.mult).then_inc(gm_done, 1)
            e.wait_ge(gm_done, g + 1)
            e.wait_ge(exped, g + 1)
            e.tensor_tensor(M[:], E[:], gm[:], ALU.mult).then_inc(m_done, 1)
            e.wait_ge(inter_mm, g + 1)
            e.tensor_tensor(hv(y1[:]), hv(two(4, 6)), per_head(ecum, i), ALU.mult).then_inc(y1_done, 1)
            e.wait_ge(ds_mm, g + 1)
            e.wait_ge(smul, g + 1)
            e.tensor_tensor(S[:], S[:], ps[0:NS, 6:8, :].rearrange("p b n -> p (b n)"), ALU.add).then_inc(s_done, 1)
            if not last:
                take_bc(g + 1)
            e.wait_ge(intra_mm, g + 1)
            e.wait_ge(y1_done, g + 1)
            e.tensor_tensor(y1[:], y1[:], two(2, 4), ALU.add).then_inc(y2_done, 1)
            e.wait_ge(y3_done, g + 1)
            e.tensor_tensor(y[:], y1[:], sz[:], ALU.mult).then_inc(y_done, 1)
            if not last:
                e.wait_ge(y_done, g + 1)
                take_z(g + 1)
                gate(g + 1)
            e.wait_ge(yhi_done, g + 1)
            e.tensor_tensor(yT_lo[:], two(2, 4), yT_hi[:], ALU.subtract).then_inc(ylo_done, 1)
            if not last:
                e.wait_ge(diff, g + 1)
                decays(i + 1)
                e.wait_ge(dx_done, g + 1)
                e.wait_ge(xe_done, g + 1)
                take_x(i + 1, g + 1)
            e.wait_ge(out_mm, g + 1)
            e.scalar_tensor_tensor(out=t[:, i, :], in0=ps[:, 0, :], scalar=0.5, in1=t[:, i, :], op0=ALU.mult,
                                   op1=ALU.add).then_inc(t_done, 1)

        e.wait_ge(bias_added, 1)
        chunks(e, body)

    def low_part(e, i):
        e.wait_ge(hi_done, i + 1)
        e.tensor_tensor(u_lo[:, :, i * P:(i + 1) * P], ps[:, i % 4, :].rearrange("p (k c) -> p k c", k=KD),
                        u_hi[:, :, i * P:(i + 1) * P], ALU.subtract).then_inc(lo_done, 1)

    def act(e):
        own = Chain(e, act_own)
        e.wait_ge(var_done, 1)
        e.activation(rstd[:], rstd[:], ACT.Sqrt).then_inc(sd_done, 1)
        e.wait_ge(var_done, 2)
        e.activation(r2[:], r2[:], ACT.Sqrt).then_inc(sd_done, 1)
        for i in range(TT):
            e.wait_ge(turned, i + 1)
            e.activation(u_hi[:, :, i * P:(i + 1) * P], ps[:, i % 4, :].rearrange("p (k c) -> p k c", k=KD), ACT.Copy)\
                .then_inc(hi_done, 1)
        e.wait_ge(par_in, PAR)
        for n in range(AT_PIECES):
            e.wait_ge(raw_in[n % 2], (n // 2 + 1) * 16)
            if n < KD:
                e.activation(wi_hi[:, n, :], raw[n % 2][:], ACT.Copy, scale=nw[:, n:n + 1]).then_inc(w_hi, 1)
            else:
                j = 4 * (n - KD)
                e.activation(wo_hi[:, j:j + 4, :], raw[n % 2][:, 0:4 * D].rearrange("p (j f) -> p j f", j=4), ACT.Copy)\
                    .then_inc(w_hi, 1)
        own(e.activation(nega[:], alog[:], ACT.Exp))
        e.mul(nega[:], nega[:], -1.0).then_inc(nega_done, 1)
        e.wait_ge(dtn_done, 1)
        own(e.activation(dtl[:], dtn[:], ACT.Exp))
        e.activation(dtl[:], dtl[:], ACT.Ln, bias=1.0).then_inc(dt_log, 1)
        e.wait_ge(sums_mm, 1)
        for n, d in enumerate((dend, ecum, edec)):
            x = e.activation(d[:], ps[:, 7, 32 * n:32 * n + 32].rearrange("p (i h) -> p i h", i=TT), ACT.Exp)
        x.then_inc(sums_exp, 1)

        def tanh_z(g):
            e.wait_ge(z_ev, g + 1)
            e.activation(th[:], zt[:], ACT.Tanh, scale=0.5).then_inc(thz_done, 1)

        tanh_z(0)

        def body(i, first, last):
            g = i
            e.wait_ge(bct_mm, g + 1)
            e.activation(bct[:], ps[0:NS, 6:8, :].rearrange("p b (c t) -> p (b c) t", t=P), ACT.Copy).then_inc(bct_done, 1)
            e.wait_ge(diff, g + 1)
            e.activation(E[:], ps[:, 7, :].rearrange("p (h t) -> p h t", h=AT_HN), ACT.Exp).then_inc(exped, 1)
            if not last:
                tanh_z(g + 1)
            e.wait_ge(yt_mm, g + 1)
            e.activation(yT_hi[:], two(2, 4), ACT.Copy).then_inc(yhi_done, 1)

        chunks(e, body)

    def pool(e):
        e.memset(S[:], 0.0).then_inc(zeroed, 1)
        e.wait_ge(zeroed, 1)
        e.wait_ge(un_done, TT)
        e.wait_ge(par_in, PAR)
        e.tensor_tensor(t[:], t[:], outb[:].unsqueeze(1).to_broadcast([P, TT, D]), ALU.add).then_inc(bias_added, 1)
        e.wait_ge(prep, 1)

        def body(i, first, last):
            g = i
            e.wait_ge(x_done, g + 1)
            e.tensor_tensor(hv(xe[:]), hv(xs[:]), per_head(dte, i), ALU.mult).then_inc(xe_done, 1)
            e.tensor_tensor(hv(dx[:]), hv(xs[:]), dpar[:].unsqueeze(2).to_broadcast([P, AT_HN, AT_HW]), ALU.mult)\
                .then_inc(dx_done, 1)
            if not first:
                e.wait_ge(s_done, g)
            e.wait_ge(inter_mm, g + 1)
            e.tensor_tensor(hv(S[:]), hv(S[:]), edec[0:NS, i, :].unsqueeze(2).to_broadcast([NS, AT_HN, AT_HW]), ALU.mult)\
                .then_inc(smul, 1)
            e.wait_ge(y2_done, g + 1)
            e.wait_ge(dx_done, g + 1)
            e.tensor_tensor(y1[:], y1[:], dx[:], ALU.add).then_inc(y3_done, 1)

        chunks(e, body)

    def pe(e):
        for i in range(TT):
            e.wait_ge(un_done, i + 1)
            if i >= 4:
                e.wait_ge(lo_done, i - 3)
            for k in range(KD):
                x = e.transpose(ps[:, i % 4, k * P:(k + 1) * P], un[:, i % 2, k * P:(k + 1) * P], core.ident[:])
            x.then_inc(turned, 1)
        e.wait_ge(w_lo, KD)
        e.wait_ge(lo_done, TT)
        for i in range(TT):
            for k in range(KD):
                for m, (a, b) in enumerate(((u_hi, wi_hi), (u_hi, wi_lo), (u_lo, wi_hi))):
                    x = e.matmul(ps[:, 6, i * AT_HN:(i + 1) * AT_HN], a[:, k, i * P:(i + 1) * P], b[:, k, AT_CDT:AT_CDT + AT_HN],
                                 start=(k == 0 and m == 0), stop=(k == KD - 1 and m == 2))
        x.then_inc(dt_mm, 1)
        e.wait_ge(la_done, 1)
        la2 = la[:].rearrange("p i h -> p (i h)")
        for n, w in enumerate((core.after, core.tri, core.ones)):
            x = e.matmul(ps[:, 7, 32 * n:32 * n + 32], w[:], la2, start=True, stop=True)
        x.then_inc(sums_mm, 1)

        def project(i, out, col, width):
            for k in range(KD):
                for m, (a, b) in enumerate(((u_hi, wi_hi), (u_hi, wi_lo), (u_lo, wi_hi))):
                    x = e.matmul(out, a[:, k, ds(i * P, P)], b[:, k, col:col + width],
                                 start=(k == 0 and m == 0), stop=(k == KD - 1 and m == 2))
            return x

        def project_bc(i):
            project(i, ps[:, 1, 0:2 * AT_HN * NS], AT_CBC, 2 * AT_HN * NS).then_inc(bc_mm, 1)

        def project_z(i):
            project(i, ps[:, 4, :], 0, 512)
            project(i, ps[:, 5, :], 512, 512).then_inc(z_mm, 1)

        def project_x(i):
            project(i, ps[:, 2, :], AT_CX, 512)
            project(i, ps[:, 3, :], AT_CX + 512, 512).then_inc(x_mm, 1)

        project_bc(0)
        project_z(0)
        project_x(0)

        def body(i, first, last):
            g = i
            e.wait_ge(bc_done, g + 1)
            if first:
                e.wait_ge(sums_exp, 1)
                e.wait_ge(zeroed, 1)
            else:
                e.wait_ge(s_done, g)
            for c in range(2 * AT_HN):
                x = e.transpose(ps[0:NS, 6 + c // 4, (c % 4) * P:(c % 4 + 1) * P], bc[:, c * NS:(c + 1) * NS], core.ident[:])
            x.then_inc(bct_mm, 1)
            e.wait_ge(r_done, g + 1)
            e.wait_ge(bct_done, g + 1)
            for m, r in enumerate((r_hi, r_lo)):
                x = e.matmul(ps[:, 7, :], core.after16[:], r[:].rearrange("p h t -> p (h t)"), start=(m == 0), stop=(m == 1))
            x.then_inc(diff, 1)
            for h in range(AT_HN):
                x = e.matmul(ps[:, 6, h * P:(h + 1) * P], bct[:, 2 * h, :], bct[:, 2 * h + 1, :], start=True, stop=True)
            x.then_inc(g_mm, 1)
            e.wait_ge(z_ev, g + 1)
            for h in range(AT_HN):
                x = e.matmul(ps[:, 4 + h // 2, (h % 2) * AT_HW:(h % 2 + 1) * AT_HW], bct[:, 2 * h + 1, :], S[:, h * AT_HW:(h + 1) * AT_HW],
                             start=True, stop=True)
            x.then_inc(inter_mm, 1)
            e.wait_ge(xdt_done, g + 1)
            e.wait_ge(m_done, g + 1)
            for h in range(AT_HN):
                x = e.matmul(ps[:, 2 + h // 2, (h % 2) * AT_HW:(h % 2 + 1) * AT_HW], M[:, h, :], xdt[:, h * AT_HW:(h + 1) * AT_HW],
                             start=True, stop=True)
            x.then_inc(intra_mm, 1)
            e.wait_ge(xe_done, g + 1)
            for h in range(AT_HN):
                x = e.matmul(ps[0:NS, 6 + h // 2, (h % 2) * AT_HW:(h % 2 + 1) * AT_HW], bc[:, 2 * h * NS:(2 * h + 1) * NS],
                             xe[:, h * AT_HW:(h + 1) * AT_HW], start=True, stop=True)
            x.then_inc(ds_mm, 1)
            if not last:
                project_bc(i + 1)
                e.wait_ge(y1_done, g + 1)
                project_z(i + 1)
            e.wait_ge(y_done, g + 1)
            core.apart(e)
            for j in range(JD):
                x = e.transpose(ps[:, 2 + j // 4, (j % 4) * P:(j % 4 + 1) * P], y[:, j * P:(j + 1) * P], core.ident[:])
            x.then_inc(yt_mm, 1)
            e.wait_ge(ylo_done, g + 1)
            if not first:
                e.wait_ge(t_done, g)
            for j in range(JD):
                for m, (a, b) in enumerate(((yT_hi, wo_hi), (yT_hi, wo_lo), (yT_lo, wo_hi))):
                    x = e.matmul(ps[:, 0, :], a[:, j * P:(j + 1) * P], b[:, j, :], start=(j == 0 and m == 0),
                                 stop=(j == JD - 1 and m == 2))
            x.then_inc(out_mm, 1)
            if not last:
                project_x(i + 1)

        chunks(e, body)

    return dict(sp=sp, dve=dve, act=act, pe=pe, pool=pool, cx=cx, used=used)


EX_E = 8
EX_TOPK = 2
EX_F = 2048
EX_FB = EX_F // P
EX_GB = 4
EX_FG = EX_FB // EX_GB
EX_PIECES = 8
EX_BLOCKS = TOK // P
EX_FILLED = EX_TOPK * TT + EX_E + 1
EX_TABLE = EX_FILLED + EX_BLOCKS
EX_MAGIC = 1.5 * 2.0 ** 23
EX_LN_EPS = 1e-5


def stage_moe(core, ps):
    nc, ins, t = core.nc, core.ins, core.t
    cx = ExitStack()
    sb = lambda n, s, d=F32: core.sb("eb_" + n, s, d, cx)
    used = []
    sem = lambda n: core.stage_sem("e_" + n, cx, used)
    w_hi = [sb(f"w_hi{b}", [P, EX_PIECES, EX_F], F16) for b in range(2)]
    w_lo = [sb(f"w_lo{b}", [P, EX_PIECES, EX_F], F16) for b in range(2)]
    raw = [sb(f"raw{b}", [P, EX_F]) for b in range(2)]
    un = sb("un", [P, TT, D])
    gw = sb("gw", [P, KD, EX_E])
    b1, b2 = sb("b1", [P, EX_E, EX_FB]), sb("b2", [EX_E, D])
    iota = sb("iota", [P, EX_E])
    stats, mv, rstd = sb("stats", [P, TT, 6]), sb("mv", [P, TT, 2]), sb("rstd", [P, TT])
    lg, pr, top, pos, pk = (sb(n, [P, TT, EX_E]) for n in ("lg", "pr", "top", "pos", "pk"))
    pick = [sb(f"pick{k}", [P, TT, EX_E]) for k in range(EX_TOPK)]
    mask, tot = sb("mask", [P, TT, EX_E]), sb("tot", [P, TT, EX_E])
    topi, topf = sb("topi", [P, TT, EX_E], U32), sb("topf", [P, TT, EX_E])
    red, inv = sb("red", [P, TT]), sb("inv", [P, TT])
    before = sb("before", [P, TT + 1, EX_E])
    nb, cum, first, first_slot = (sb(n, [P, EX_E]) for n in ("nb", "cum", "first", "first_slot"))
    plan = sb("plan", [P, 2 * EX_E + 1], U32)
    slotf, slot = sb("slotf", [P, EX_TOPK, TT]), sb("slot", [P, EX_TOPK, TT], U32)
    xg, x_hi, x_lo = sb("xg", [P, D]), sb("x_hi", [P, KD, P], F16), sb("x_lo", [P, KD, P], F16)
    hb = sb("hb", [P, 2, EX_GB * P])
    h_hi, h_lo = sb("h_hi", [P, EX_FG, EX_GB * P], F16), sb("h_lo", [P, EX_FG, EX_GB * P], F16)
    y = sb("y", [P, D])
    xs_dram = nc.dram_tensor("xs_table", [EX_TABLE * P, D], F32).ap()
    ys_dram = nc.dram_tensor("ys_table", [EX_TABLE * P, D], F32).ap()

    names = """par_in var_done sd_done un_done turned0 copied0 logits max_done exp_done mask_done ranks table_done
        zero_set zero_out scattered xg_in turned xhi_done xlo_done whi_done wlo_done h_mm h_taken silu_done hhi_done
        hlo_done y_mm y_ev y_out expert_done t_done y_sent mix_done mix_turned mix_ev b2_mm b2_done dve_own act_own""".split()
    s_ = {n: sem(n) for n in names}
    (par_in, var_done, sd_done, un_done, turned0, copied0, logits, max_done, exp_done, mask_done, ranks, table_done,
     zero_set, zero_out, scattered, xg_in, turned, xhi_done, xlo_done, whi_done, wlo_done, h_mm, h_taken, silu_done,
     hhi_done, hlo_done, y_mm, y_ev, y_out, expert_done, t_done, y_sent, mix_done, mix_turned, mix_ev, b2_mm, b2_done, dve_own, act_own) = \
        (s_[n] for n in names)
    raw_in = [sem(f"raw_in{b}") for b in range(2)]
    back = [sem(f"back{b}") for b in range(TT)]

    PARS = ((gw, "e_gw"), (b1, "e_b1"), (b2, "e_b2"), (iota, "c_iota"))
    PAR = 16 * len(PARS)
    H_TAKEN0, HLO0, YMM0, YEV0, YSENT0, EXPERT0 = EX_FG, 2, 1, 1, 1, 1

    def experts(e, piece, block, end):
        def body(x, side, last):
            count = e.value_load(plan[0:1, ds(x, 1)], min_val=0, max_val=EX_BLOCKS)
            start = e.value_load(plan[0:1, ds(x + EX_E, 1)], min_val=0, max_val=EX_FILLED - 2)
            with e.Fori(0, EX_BLOCKS // 2) as i:
                for q in range(2):
                    b = i * 2 + q
                    if piece and not last:
                        piece(x + 1, 1 - side, b, q, i)
                    with e.If(b < count):
                        block(x, side, start + b)
            if end:
                end(x)

        with e.Fori(0, EX_E // 2 - 1) as i:
            body(i * 2, 0, False)
            body(i * 2 + 1, 1, False)
        body(EX_E - 2, 0, False)
        body(EX_E - 1, 1, True)

    def sp(e):
        for dst, name in PARS:
            e.dma_start(dst[:], ins[name]).then_inc(par_in, 16)

        def load(i, q):
            e.dma_start(raw[q][:], ins["e_w"][ds((i * 2 + q) * P, P), :]).then_inc(raw_in[q], 16)

        for q in range(2):
            load(0, q)
        with e.Fori(1, EX_E * EX_PIECES // 2) as i:
            for q in range(2):
                e.wait_ge(wlo_done, i * 2 + (q - 1))
                load(i, q)

    def dve(e):
        own = Chain(e, dve_own)
        e.sem_inc(h_taken, H_TAKEN0)
        e.sem_inc(hlo_done, HLO0)
        e.sem_inc(y_ev, YEV0)
        for i in range(TT):
            x = e.bn_stats(stats[:, i, :], t[:, i, :])
        own(x)
        for i in range(TT):
            x = e.bn_aggr(mv[:, i, :], stats[:, i, :])
        own(x)
        e.tensor_scalar(rstd[:], mv[:, :, 1], EX_LN_EPS, None, ALU.add).then_inc(var_done, 1)
        e.wait_ge(sd_done, 1)
        own(e.reciprocal(rstd[:], rstd[:]))
        for i in range(TT):
            e.tensor_scalar(un[:, i, :], t[:, i, :], mv[:, i, 0:1], rstd[:, i:i + 1], ALU.subtract, ALU.mult)\
                .then_inc(un_done, 1)
        for n in range(EX_PIECES):
            lower(e, 0, 0, n, n % 2, n // 2)
        wide = lambda x: x.unsqueeze(2).to_broadcast([P, TT, EX_E])
        e.wait_ge(logits, 1)
        own(e.tensor_copy(lg[:], ps[:, 7, 0:TT * EX_E].rearrange("p (i x) -> p i x", i=TT)))
        own(e.tensor_reduce(red[:], lg[:], AX.X, ALU.max))
        e.tensor_tensor(lg[:], lg[:], wide(red[:]), ALU.subtract).then_inc(max_done, 1)
        e.wait_ge(exp_done, 1)
        own(e.tensor_reduce(inv[:], pr[:], AX.X, ALU.add))
        own(e.reciprocal(inv[:], inv[:]))
        own(e.tensor_tensor(pr[:], pr[:], wide(inv[:]), ALU.mult))
        for i in range(TT):
            x = e.max(top[:, i, :], pr[:, i, :])
        own(x)
        for i in range(TT):
            x = e.max_index(topi[:, i, :], top[:, i, :], pr[:, i, :])
        own(x)
        own(e.tensor_copy(topf[:], topi[:]))
        e.wait_ge(par_in, PAR)
        for k in range(EX_TOPK):
            x = e.tensor_tensor(pick[k][:], iota[:].unsqueeze(1).to_broadcast([P, TT, EX_E]), wide(topf[:, :, k]), ALU.is_equal)
        own(x)
        e.tensor_tensor(mask[:], pick[0][:], pick[1][:], ALU.add).then_inc(mask_done, 1)
        own(e.memset(before[:, 0, :], 0.0))
        e.wait_ge(ranks, 1)
        own(e.tensor_copy(tot[:], ps[:, 6, 0:TT * EX_E].rearrange("p (i x) -> p i x", i=TT)))
        for i in range(TT):
            own(e.tensor_tensor(before[:, i + 1, :], before[:, i, :], tot[:, i, :], ALU.add))
        own(e.tensor_scalar(nb[:], before[:, TT, :], 1.0 / P, 0.5 - 0.5 / P, ALU.mult, ALU.add))
        own(e.tensor_scalar(nb[:], nb[:], EX_MAGIC, None, ALU.add))
        own(e.tensor_scalar(nb[:], nb[:], EX_MAGIC, None, ALU.subtract))
        own(e.tensor_tensor_scan(cum[:], core.ones[:, 0:EX_E], nb[:], 0.0, ALU.mult, ALU.add))
        own(e.tensor_tensor(first[:], cum[:], nb[:], ALU.subtract))
        e.tensor_copy(plan[:, 0:EX_E], nb[:])
        e.tensor_copy(plan[:, EX_E:2 * EX_E], first[:])
        own(e.tensor_copy(plan[:, 2 * EX_E:], cum[:, EX_E - 1:EX_E]))
        own(e.tensor_scalar(first_slot[:], first[:], float(P), None, ALU.mult))
        own(e.tensor_tensor(pos[:], ps[:, 7, TT * EX_E:2 * TT * EX_E].rearrange("p (i x) -> p i x", i=TT), mask[:], ALU.subtract))
        own(e.tensor_tensor(pos[:], pos[:], before[:, 0:TT, :], ALU.add))
        own(e.tensor_tensor(pos[:], pos[:], first_slot[:].unsqueeze(1).to_broadcast([P, TT, EX_E]), ALU.add))
        for k in range(EX_TOPK):
            own(e.tensor_tensor(pk[:], pick[k][:], pos[:], ALU.mult))
            own(e.tensor_reduce(slotf[:, k, :], pk[:], AX.X, ALU.add))
        e.tensor_copy(slot[:], slotf[:]).then_inc(table_done, 1)
        e.wait_ge(table_done, 1)
        lower_x(e, 0)

        def bias(x, s, j):
            e.wait_ge(h_mm, s * EX_FG + (j + 1))
            e.wait_ge(hlo_done, s * EX_FG + (j + 1))
            e.tensor_tensor(hb[:, j % 2, :].rearrange("p (c n) -> p c n", c=EX_GB),
                            ps[:, j, :].rearrange("p (c n) -> p c n", c=EX_GB),
                            b1[:, ds(x, 1), j * EX_GB:(j + 1) * EX_GB].rearrange("p o c -> p (o c)").unsqueeze(2)
                            .to_broadcast([P, EX_GB, P]), ALU.add).then_inc(h_taken, 1)

        def low(s, j):
            e.wait_ge(hhi_done, s * EX_FG + (j + 1))
            e.tensor_tensor(h_lo[:, j, :], hb[:, j % 2, :], h_hi[:, j, :], ALU.subtract).then_inc(hlo_done, 1)

        def block(x, side, s):
            for j in range(EX_FG):
                bias(x, s, j)
                if j:
                    low(s, j - 1)
            low(s, EX_FG - 1)
            lower_x(e, s + 1)
            e.wait_ge(y_mm, s + 1 + YMM0)
            e.wait_ge(y_sent, s + YSENT0)
            core.apart(e)
            e.tensor_copy(y[:], ps[:, 5, :]).then_inc(y_ev, 1)

        experts(e, lambda x, side, n, q, i: lower(e, x, side, n, q, x * (EX_PIECES // 2) + i), block, None)
        e.tensor_tensor(pick[0][:], pick[0][:], wide(top[:, :, 0]), ALU.mult)
        own(e.tensor_tensor(pick[1][:], pick[1][:], wide(top[:, :, 1]), ALU.mult))
        e.tensor_tensor(mask[:], pick[0][:], pick[1][:], ALU.add).then_inc(mix_done, 1)
        for i in range(TT):
            e.wait_ge(b2_mm, i + 1)
            e.tensor_tensor(t[:, i, :], t[:, i, :], ps[:, i % 4, :], ALU.add).then_inc(b2_done, 1)
        for n in range(EX_TOPK * TT):
            i, k = n // EX_TOPK, n % EX_TOPK
            e.wait_ge(back[n % TT], 16 * (n // TT + 1))
            if k:
                e.wait_ge(t_done, n)
            else:
                e.wait_ge(b2_done, i + 1)
            e.scalar_tensor_tensor(out=t[:, i, :], in0=un[:, n % TT, :], scalar=top[:, i, k:k + 1], in1=t[:, i, :],
                                   op0=ALU.mult, op1=ALU.add).then_inc(t_done, 1)

    def lower(e, x, side, n, q, m):
        e.wait_ge(whi_done, x * EX_PIECES + (n + 1))
        e.tensor_tensor(w_lo[side][:, n, :], raw[q][:], w_hi[side][:, n, :], ALU.subtract).then_inc(wlo_done, 1)

    def upper(e, x, side, n, q, m):
        e.wait_ge(raw_in[q], (m + 1) * 16)
        e.wait_ge(expert_done, x)
        e.activation(w_hi[side][:, n, :], raw[q][:], ACT.Copy).then_inc(whi_done, 1)

    def lower_x(e, s):
        e.wait_ge(xhi_done, s + 1)
        e.tensor_tensor(x_lo[:], ps[:, 4, :].rearrange("p (k n) -> p k n", k=KD), x_hi[:], ALU.subtract)\
            .then_inc(xlo_done, 1)

    def upper_x(e, s):
        e.wait_ge(turned, s + 1)
        e.activation(x_hi[:], ps[:, 4, :].rearrange("p (k n) -> p k n", k=KD), ACT.Copy).then_inc(xhi_done, 1)

    def act(e):
        own = Chain(e, act_own)
        e.wait_ge(var_done, 1)
        e.activation(rstd[:], rstd[:], ACT.Sqrt).then_inc(sd_done, 1)
        for i in range(TT):
            e.wait_ge(turned0, i + 1)
            e.activation(hb[:, i % 2, :], ps[:, i % 2, :], ACT.Copy).then_inc(copied0, 1)
        for n in range(EX_PIECES):
            e.wait_ge(raw_in[n % 2], 16 * (n // 2 + 1))
            e.activation(w_hi[0][:, n, :], raw[n % 2][:], ACT.Copy).then_inc(whi_done, 1)
        e.wait_ge(max_done, 1)
        e.activation(pr[:], lg[:], ACT.Exp).then_inc(exp_done, 1)
        upper_x(e, 0)
        e.wait_ge(table_done, 1)

        def block(x, side, s):
            for j in range(EX_FG):
                e.wait_ge(h_taken, s * EX_FG + (j + 1 + H_TAKEN0))
                if j == 0:
                    e.wait_ge(y_mm, s + YMM0)
                e.activation(hb[:, j % 2, :], hb[:, j % 2, :], ACT.Silu).then_inc(silu_done, 1)
                e.wait_ge(silu_done, s * EX_FG + (j + 1))
                e.activation(h_hi[:, j, :], hb[:, j % 2, :], ACT.Copy).then_inc(hhi_done, 1)
            upper_x(e, s + 1)

        experts(e, lambda x, side, n, q, i: upper(e, x, side, n, q, x * (EX_PIECES // 2) + i), block, None)
        e.wait_ge(mix_turned, 1)
        e.activation(hb[0:EX_E, :, :], ps[0:EX_E, 6:8, :], ACT.Copy).then_inc(mix_ev, 1)

    def pe(e):
        for i in range(TT + 1):
            if i < TT:
                e.wait_ge(un_done, i + 1)
                if i >= 2:
                    e.wait_ge(copied0, i - 1)
                for k in range(KD):
                    x = e.transpose(ps[:, i % 2, k * P:(k + 1) * P], un[:, i, k * P:(k + 1) * P], core.ident[:])
                x.then_inc(turned0, 1)
            if i == 1:
                e.wait_ge(par_in, PAR)
            if i >= 1:
                e.wait_ge(copied0, i)
                for k in range(KD):
                    x = e.matmul(ps[:, 7, (i - 1) * EX_E:i * EX_E], hb[:, (i - 1) % 2, k * P:(k + 1) * P], gw[:, k, :],
                                 start=(k == 0), stop=(k == KD - 1))
        x.then_inc(logits, 1)
        e.wait_ge(mask_done, 1)
        m2 = mask[:].rearrange("p i x -> p (i x)")
        e.matmul(ps[:, 7, TT * EX_E:2 * TT * EX_E], core.tri[:], m2, start=True, stop=True)
        e.matmul(ps[:, 6, 0:TT * EX_E], core.ones[:], m2, start=True, stop=True).then_inc(ranks, 1)
        e.sem_inc(y_mm, YMM0)
        e.sem_inc(expert_done, EXPERT0)

        def turn(s):
            e.wait_ge(xg_in, s * 16 + 16)
            core.apart(e)
            for k in range(KD):
                x = e.transpose(ps[:, 4, k * P:(k + 1) * P], xg[:, k * P:(k + 1) * P], core.ident[:])
            x.then_inc(turned, 1)

        turn(0)
        e.wait_ge(table_done, 1)

        def block(x, side, s):
            e.wait_ge(wlo_done, x * EX_PIECES + KD)
            e.wait_ge(xlo_done, s + 1)
            for j in range(EX_FG):
                e.wait_ge(h_taken, s * EX_FG + (j + 1))
                for c in range(EX_GB):
                    f = j * EX_GB + c
                    for k in range(KD):
                        for m, (a, b) in enumerate(((w_hi, x_hi), (w_hi, x_lo), (w_lo, x_hi))):
                            o = e.matmul(ps[:, j, c * P:(c + 1) * P], a[side][:, k, f * P:(f + 1) * P], b[:, k, :],
                                         start=(k == 0 and m == 0), stop=(k == KD - 1 and m == 2))
                o.then_inc(h_mm, 1)
            turn(s + 1)
            e.wait_ge(wlo_done, x * EX_PIECES + EX_PIECES)
            for j in range(EX_FG):
                e.wait_ge(hlo_done, s * EX_FG + (j + 1 + HLO0))
                if j == 0:
                    e.wait_ge(y_ev, s + YEV0)
                for c in range(EX_GB):
                    for m, (a, b) in enumerate(((h_hi, w_hi), (h_hi, w_lo), (h_lo, w_hi))):
                        o = e.matmul(ps[:, 5, :], a[:, j, c * P:(c + 1) * P], b[side][:, KD + j, c * D:(c + 1) * D],
                                     start=(j == 0 and c == 0 and m == 0), stop=(j == EX_FG - 1 and c == EX_GB - 1 and m == 2))
            o.then_inc(y_mm, 1)

        experts(e, None, block, lambda x: e.drain().then_inc(expert_done, 1))
        e.wait_ge(mix_done, 1)
        for i in range(TT):
            x = e.transpose(ps[0:EX_E, 6 + i // 4, (i % 4) * P:(i % 4 + 1) * P], mask[:, i, :], core.ident[:])
        x.then_inc(mix_turned, 1)
        e.wait_ge(mix_ev, 1)
        for i in range(TT):
            if i >= 4:
                e.wait_ge(b2_done, i - 3)
            e.matmul(ps[:, i % 4, :], hb[0:EX_E, i // 4, (i % 4) * P:(i % 4 + 1) * P], b2[:], start=True, stop=True)\
                .then_inc(b2_mm, 1)

    def pool(e):
        e.memset(y[:], 0.0).then_inc(zero_set, 1)
        e.wait_ge(zero_set, 1)
        e.dma_start(xs_dram[0:EX_FILLED * P, :].rearrange("(b p) f -> p b f", p=P),
                    y[:].unsqueeze(1).to_broadcast([P, EX_FILLED, D])).then_inc(zero_out, 16)
        e.dma_start(ys_dram[EX_TOPK * TT * P:(EX_FILLED - 2) * P, :].rearrange("(b p) f -> p b f", p=P),
                    y[:].unsqueeze(1).to_broadcast([P, EX_FILLED - 2 - EX_TOPK * TT, D])).then_inc(zero_out, 16)
        e.wait_ge(zero_out, 32)
        e.wait_ge(un_done, TT)
        e.wait_ge(table_done, 1)
        for i in range(TT):
            for k in range(EX_TOPK):
                e.indirect_dma_start(out=xs_dram, out_offset=bass.IndirectOffsetOnAxis(ap=slot[:, k, i:i + 1], axis=0),
                                     in_=un[:, i, :], in_offset=None).then_inc(scattered, 16)
        e.wait_ge(scattered, 16 * TT * EX_TOPK)

        def fetch(s):
            e.dma_start(xg[:], xs_dram[ds(s * P, P), :]).then_inc(xg_in, 16)

        fetch(0)
        e.wait_ge(turned, 1)
        fetch(1)
        e.sem_inc(y_sent, YSENT0)

        def block(x, side, s):
            e.wait_ge(turned, s + 2)
            core.apart(e)
            fetch(s + 2)
            e.wait_ge(y_ev, s + 1 + YEV0)
            core.apart(e)
            e.dma_start(ys_dram[ds(s * P, P), :], y[:]).then_inc(y_out, 16)
            e.wait_ge(y_out, s * 16 + 16)
            e.sem_inc(y_sent, 1)

        experts(e, None, block, None)
        total = e.value_load(plan[0:1, 2 * EX_E:2 * EX_E + 1], min_val=EX_TOPK * TT, max_val=EX_FILLED - 2)
        e.wait_ge(y_out, total * 16)
        e.wait_ge(xg_in, total * 16 + 32)
        core.apart(e)
        for n in range(EX_TOPK * TT):
            i, k = n // EX_TOPK, n % EX_TOPK
            if n >= TT:
                e.wait_ge(t_done, n - TT + 1)
            e.indirect_dma_start(out=un[:, n % TT, :], out_offset=None, in_=ys_dram[0:(EX_FILLED - 2) * P, :],
                                 in_offset=bass.IndirectOffsetOnAxis(ap=slot[:, k, i:i + 1], axis=0)).then_inc(back[n % TT], 16)

    return dict(sp=sp, dve=dve, act=act, pe=pe, pool=pool, cx=cx, used=used)


ENGINES = 5
OUT_TILES = TT


def program(nc, ins, out):
    with ExitStack() as ctx:
        core = Core(nc, ctx, ins)
        ps = ctx.enter_context(nc.psum_tensor("banks", [P, 8, 512], F32))
        stages = []
        for make in (stage_l01, stage_mamba, stage_ffn, stage_l3, stage_moe):
            stage = make(core, ps)
            stage["cx"].close()
            stages.append(stage)
        out_sent = core.sem("out_sent")

        def open_stage(e, k):
            if k:
                e.wait_ge(core.cleared, k)
            if k == 1:
                e.wait_ge(core.consts_in, core.CONSTS)

        block = ctx.enter_context(nc.Block())

        @block.sync
        def _(sp):
            for k, stage in enumerate(stages):
                open_stage(sp, k)
                stage["sp"](sp)
                sp.sem_inc(core.stage_end, 1)
            sp.wait_ge(core.stage_end, len(stages) * ENGINES)
            sp.dma_start(out.rearrange("(i p) f -> p i f", p=P), core.t[:]).then_inc(out_sent, 16)
            sp.wait_ge(out_sent, 16)

        @block.scalar
        def _(act):
            for k, stage in enumerate(stages):
                open_stage(act, k)
                stage["act"](act)
                act.drain().then_inc(core.stage_end, 1)

        @block.vector
        def _(dve):
            for k, stage in enumerate(stages):
                open_stage(dve, k)
                stage["dve"](dve)
                dve.drain().then_inc(core.stage_end, 1)

        @block.gpsimd
        def _(pool):
            for k, stage in enumerate(stages):
                if k:
                    pool.wait_ge(core.stage_end, k * ENGINES)
                    for number in sorted(s.num for s in stages[k - 1]["used"]):
                        pool.sem_clear(range(number, number + 1))
                    pool.sem_inc(core.cleared, 1)
                open_stage(pool, k)
                if stage["pool"]:
                    stage["pool"](pool)
                pool.drain().then_inc(core.stage_end, 1)

        @block.tensor
        def _(pe):
            for k, stage in enumerate(stages):
                open_stage(pe, k)
                stage["pe"](pe)
                pe.drain().then_inc(core.stage_end, 1)


def shape_constants():
    k = np.arange(P)
    c = {"c_ident": np.eye(P, dtype=np.float32),
         "c_tri": (k[:, None] <= k[None, :]).astype(np.float32),
         "c_after": (k[:, None] > k[None, :]).astype(np.float32)}
    c["c_tri16"] = c["c_tri"].astype(np.float16)
    c["c_after16"] = c["c_after"].astype(np.float16)
    c["c_ones"] = np.ones((P, P), np.float32)
    r, j, p = np.arange(H2)[:, None, None], np.arange(JD)[None, :, None], k[None, None, :]
    c["c_sel"] = (r == 4 * j + p // 32).astype(np.float32)
    c["c_selT"] = (np.arange(H2)[None, None, :] == 4 * j + k[:, None, None] // 32).astype(np.float32)
    per_group = SEQ // GROUPS
    c["c_g16"] = ((k[:, None] // per_group == k[None, :] // per_group) / per_group).astype(np.float32)
    c["c_onesn"] = np.full((P, P), 1 / (per_group * TOK), np.float32)
    signs = np.ones((1, 1))
    while signs.shape[0] < D:
        signs = np.block([[signs, signs], [signs, -signs]])
    c["c_had"] = signs.astype(np.float16)
    c["c_iota"] = np.tile(np.arange(EX_E, dtype=np.float32), (P, 1))
    return c


def laid_out(i):
    x = i["x"].reshape(SEQ, TOK)
    columns = lambda a: a.reshape(LAYERS, -1, P).transpose(0, 2, 1)
    par = np.zeros((LAYERS, P, MB_NPAR), np.float32)
    conv_w, conv_b = i["L2_attn_conv_w"], i["L2_attn_conv_b"]
    par[:, :, MB_LNW:MB_LNW + KD] = columns(i["L2_attn_ln_w"])
    par[:, :, MB_LNB:MB_LNB + KD] = columns(i["L2_attn_ln_b"])
    par[:, :, MB_CVW:MB_CVB] = conv_w[:, :DI].reshape(LAYERS, JD, P, TAPS).transpose(0, 2, 1, 3).reshape(LAYERS, P, -1)
    par[:, :, MB_CVB:MB_BCW] = columns(conv_b[:, :DI])
    par[:, :NS, MB_BCW:MB_BCB] = conv_w[:, DI:].reshape(LAYERS, 2, NS, TAPS).transpose(0, 2, 1, 3).reshape(LAYERS, NS, -1)
    par[:, :NS, MB_BCB:MB_DCOL] = conv_b[:, DI:].reshape(LAYERS, 2, NS).transpose(0, 2, 1)
    par[:, :, MB_DCOL:MB_RMSW] = columns(np.repeat(i["L2_attn_D"], DI // H2, axis=1))
    par[:, :, MB_RMSW:MB_DTB] = columns(i["L2_attn_rms_w"])
    par[:, :, MB_DTB:MB_ALOG] = i["L2_attn_dt_bias"][:, None, :]
    par[:, :, MB_ALOG:] = i["L2_attn_A_log"][:, None, :]
    w1 = i["L3_ffn_w1"].reshape(EX_E, KD, P, EX_F)
    w2 = i["L3_ffn_w2"].reshape(EX_E, EX_FG, EX_GB, P, D).transpose(0, 1, 3, 2, 4).reshape(EX_E, EX_FG, P, EX_F)
    return {
        "x_cm": x, "x_tm": x.T,
        "ln2d_w": i["L0_conv_ln_w"].reshape(TT, P).T, "ln2d_b": i["L0_conv_ln_b"].reshape(TT, P).T,
        "dt_w01": np.stack([np.tile(i["L0_conv_dt_w"][0], 4), np.tile(i["L1_conv_w_dt"][0], 4)], 1),
        "dt_b01": np.stack([np.tile(i["L0_conv_dt_b"], SIDE), np.tile(i["L1_conv_b_dt"], SIDE)], 1),
        "log_A01": np.stack([i["L0_conv_log_A"], i["L1_conv_log_A"]], 1),
        "m_par": par,
        "m_in_w": i["L2_attn_in_proj_w"].transpose(0, 2, 1), "m_out_w": i["L2_attn_out_proj_w"].transpose(0, 2, 1),
        "f_w": i["L2_ffn_weight"],
        "a_nw": i["L3_attn_norm_w"].reshape(KD, P).T, "a_in_b": i["L3_attn_in_proj_b"],
        "a_out_b": i["L3_attn_out_proj_b"], "a_alog": i["L3_attn_A_log"], "a_D": i["L3_attn_D"],
        "a_dtb": i["L3_attn_dt_bias"], "a_in_w": i["L3_attn_in_proj_w"].T, "a_out_w": i["L3_attn_out_proj_w"].T,
        "e_gw": i["L3_ffn_gate_w"].T.reshape(KD, P, EX_E).transpose(1, 0, 2),
        "e_b1": i["L3_ffn_b1"].reshape(EX_E, EX_FB, P).transpose(2, 0, 1), "e_b2": i["L3_ffn_b2"],
        "e_w": np.concatenate([w1, w2], 1).reshape(-1, EX_F)}


def kernel(**inputs):
    import concourse.bacc as bacc
    from concourse.bass_utils import run_bass_kernel_spmd

    arrays = {**shape_constants(), **laid_out({k: np.asarray(v) for k, v in inputs.items()})}
    arrays = {k: np.ascontiguousarray(v) for k, v in arrays.items()}
    nc = bacc.Bacc("TRN2", target_bir_lowering=False, num_devices=1)
    ins = {k: nc.dram_tensor(k, v.shape, mybir.dt.from_np(v.dtype), kind="ExternalInput").ap() for k, v in arrays.items()}
    out = nc.dram_tensor("out", [TOK, D], F32, kind="ExternalOutput").ap()
    program(nc, ins, out)
    result = run_bass_kernel_spmd(nc, [arrays], core_ids=[0]).results[0]["out"]
    return np.ascontiguousarray(np.asarray(result).T).reshape(1, SEQ, SIDE, SIDE)
```

```python
from contextlib import ExitStack

import numpy as np
import concourse.bass as bass
from concourse import mybir

P = 128
F32 = mybir.dt.float32
F16 = mybir.dt.float16
U32 = mybir.dt.uint32
ACT = mybir.ActivationFunctionType
ALU = mybir.AluOpType
AX = mybir.AxisListType
ds = bass.ds

SEQ, SIDE = 512, 32
TOK = SIDE * SIDE
TT = TOK // P
D = 512
KD = D // P
GROUPS = 32
DI = 1024
JD = DI // P
NS = 32
H2 = 32
LAYERS = 2
TAPS = 4
E, TOPK = 8, 2
BLOCKS = TOK // P
FILLED = TOPK * TT + E + 1
TABLE = FILLED + BLOCKS


class Core:

    def __init__(self, nc, ctx, ins):
        self.nc, self.ctx, self.ins = nc, ctx, ins
        self.stages = 0
        self.stage_end = self.sem("stage_end")
        self.cleared = self.sem("cleared")
        self.t = self.sb("t_res", [P, TT, D])
        self.ident = self.sb("ident", [P, P])
        self.tri = self.sb("tri", [P, P])
        self.after = self.sb("after", [P, P])
        self.after16 = self.sb("after16", [P, P], F16)
        self.tri16 = self.sb("tri16", [P, P], F16)
        self.ones = self.sb("ones", [P, P])
        self.sel = self.sb("sel", [H2, JD, P])
        self.xs_dram = nc.dram_tensor("xs_table", [TABLE * P, D], F32).ap()
        self.ys_dram = nc.dram_tensor("ys_table", [TABLE * P, D], F32).ap()
        self.zero_set, self.zero_out = self.sem("zero_set"), self.sem("zero_out")
        self.passed = self.sem("passed")
        self.consts_in = self.sem("consts_in")

    def sb(self, name, shape, dt=F32, ctx=None):
        return (ctx or self.ctx).enter_context(self.nc.sbuf_tensor(name, shape, dt))

    def sem(self, name, ctx=None):
        return (ctx or self.ctx).enter_context(self.nc.semaphore(name))

    def stage_sem(self, name, ctx, used):
        used.append(self.sem(name, ctx))
        return used[-1]

    def load_consts(self, sp):
        for dst, name in ((self.ident, "c_ident"), (self.tri, "c_tri"), (self.after, "c_after"),
                          (self.after16, "c_after16"), (self.tri16, "c_tri16"), (self.ones, "c_ones"), (self.sel, "c_sel")):
            sp.dma_start(dst[:], self.ins[name]).then_inc(self.consts_in, 16)

    CONSTS = 7 * 16

    def zero_tables(self, e, zero):
        e.memset(zero[:], 0.0).then_inc(self.zero_set, 1)
        e.wait_ge(self.zero_set, 1)
        e.dma_start(self.xs_dram[0:FILLED * P, :].rearrange("(b p) f -> p b f", p=P),
                    zero[:].unsqueeze(1).to_broadcast([P, FILLED, D])).then_inc(self.zero_out, 16)
        e.dma_start(self.ys_dram[TOPK * TT * P:(FILLED - 2) * P, :].rearrange("(b p) f -> p b f", p=P),
                    zero[:].unsqueeze(1).to_broadcast([P, FILLED - 2 - TOPK * TT, D])).then_inc(self.zero_out, 16)

    def apart(self, e):
        e.sem_inc(self.passed, 1)


class Chain:

    def __init__(self, eng, sem):
        self.eng, self.sem, self.n = eng, sem, 0

    def __call__(self, instruction):
        instruction.then_inc(self.sem, 1)
        self.n = self.n + 1
        self.eng.wait_ge(self.sem, self.n)


L01_EPS_GN = 1e-5
L01_EPS_LN2 = 1e-5


def stage_l01(core, ps):
    nc, ins, t = core.nc, core.ins, core.t
    cx = ExitStack()
    sb = lambda n, s, d=F32: core.sb(n, s, d, cx)
    used = []
    sem = lambda n: core.stage_sem("c_" + n, cx, used)
    xcm = sb("xcm", [P, KD, TOK])
    xn = sb("xn", [P, TT, D])
    sq = sb("sq", [P, TT, D])
    selT = sb("selT", [P, TT, H2])
    wsel = sb("wsel", [P, 2, TT, H2])
    g16 = sb("g16", [P, P])
    lnw = sb("lnw2d", [P, TT])
    lnb = sb("lnb2d", [P, TT])
    dtw = sb("dtw", [P, 2])
    dtb = sb("dtb", [H2, 2])
    loga = sb("loga", [H2, 2])
    nega = sb("nega", [H2, 2])
    stats = sb("stats0", [P, KD, 2, 6])
    mv = sb("mv0", [P, KD, 2])
    dev = sb("dev0", [P, KD])
    q = sb("q0", [P, KD])
    rg = sb("rg0", [P, KD])
    rc = sb("rc0", [P, KD])
    sh = sb("sh0", [P, KD])
    xb = sb("xb01", [H2, D])
    ab = sb("ab01", [H2, D])
    ex = sb("ex01", [H2, D])
    lg = sb("lg01", [H2, D])
    dtt = sb("dtt01", [H2, D])
    dec = sb("dec01", [H2, D])
    s1 = sb("s1", [P, GROUPS])
    mg = sb("mg", [P, GROUPS])
    rgr = sb("rgr", [P, GROUPS])

    onesn = sb("onesn", [P, P])
    zero = sb("zero", [P, D])
    x_cm_in = sem("x_cm_in")
    x_tm_in = sem("x_tm_in")
    par_in = sem("par01_in")
    dve_own = sem("dve_own01")
    act_own = sem("act_own01")
    ch_mean = sem("ch_mean")
    g_mean = sem("g_mean")
    ch_spread = sem("ch_spread")
    g_var = sem("g_var")
    sq_in = sem("sq_in")
    sq_out = sem("sq_out")
    x_hat = sem("x_hat")
    turned = sem("turned")
    affine = sem("affine")
    weights = sem("weights01")
    dt_raw = sem("dt_raw01")
    pre = sem("pre01")
    negabs = sem("negabs01")
    log1p = sem("log1p01")
    dt_done = sem("dt_done01")
    decayed = sem("decayed01")
    spread_d = sem("spread_d01")
    scanned = sem("scanned")
    added = sem("added01")
    sums = sem("sums01")
    tot = sem("tot01")
    centred = sem("centred")
    squared = sem("squared")
    scaled = sem("scaled01")
    PAR = 8 * 16

    def sp(e):
        for j in range(KD):
            e.dma_start(xcm[:, j, :], ins["x_cm"][j * P:(j + 1) * P, :]).then_inc(x_cm_in, 16)
        for dst, name in ((selT, "c_selT"), (g16, "c_g16"), (onesn, "c_onesn"), (lnw, "ln2d_w"), (lnb, "ln2d_b"),
                          (dtw, "dt_w01"), (dtb, "dt_b01"), (loga, "log_A01")):
            e.dma_start(dst[:], ins[name]).then_inc(par_in, 16)
        core.load_consts(e)
        e.dma_start(t[:], ins["x_tm"].rearrange("(i p) f -> p i f", p=P)).then_inc(x_tm_in, 16)

    def dve(e):
        own = Chain(e, dve_own)
        e.wait_ge(x_cm_in, 16 * KD)
        for j in range(KD):
            e.bn_stats(stats[:, j, 0, :], xcm[:, j, 0:512])
            own(e.bn_stats(stats[:, j, 1, :], xcm[:, j, 512:1024]))
        for j in range(KD):
            own(e.bn_aggr(mv[:, j, :], stats[:, j, :, :].rearrange("p a b -> p (a b)")))
        e.tensor_copy(dev[:], mv[:, :, 0]).then_inc(ch_mean, 1)
        e.wait_ge(g_mean, 1)
        own(e.tensor_tensor(dev[:], mv[:, :, 0], ps[:, 0, 0:KD], ALU.subtract))
        own(e.tensor_tensor(q[:], dev[:], dev[:], ALU.mult))
        e.tensor_tensor(q[:], q[:], mv[:, :, 1], ALU.add).then_inc(ch_spread, 1)
        e.wait_ge(g_var, 1)
        e.tensor_scalar(rg[:], ps[:, 1, 0:KD], L01_EPS_GN, None, ALU.add).then_inc(sq_in, 1)
        e.wait_ge(sq_out, 1)
        own(e.reciprocal(rg[:], rg[:]))
        own(e.tensor_tensor(q[:], rg[:], rg[:], ALU.mult))
        own(e.tensor_tensor(q[:], q[:], mv[:, :, 1], ALU.mult))
        e.tensor_scalar(rc[:], q[:], L01_EPS_LN2, None, ALU.add).then_inc(sq_in, 1)
        e.wait_ge(sq_out, 2)
        own(e.reciprocal(rc[:], rc[:]))
        own(e.tensor_tensor(rc[:], rc[:], rg[:], ALU.mult))
        own(e.scalar_tensor_tensor(out=sh[:], in0=mv[:, :, 0], scalar=-1.0, in1=rc[:], op0=ALU.mult, op1=ALU.mult))
        for j in range(KD):
            e.tensor_scalar(xcm[:, j, :], xcm[:, j, :], rc[:, j:j + 1], sh[:, j:j + 1], ALU.mult, ALU.add).then_inc(x_hat, 1)
        e.wait_ge(par_in, PAR)
        for l in range(2):
            e.tensor_scalar(wsel[:, l, :, :], selT[:], dtw[:, l:l + 1], None, ALU.mult).then_inc(weights, 1)
        scans(e, 0)
        e.wait_ge(added, TT)
        e.tensor_reduce(s1[:], t[:].rearrange("p i (g c) -> p g i c", g=GROUPS), AX.XY, ALU.add).then_inc(sums, 1)
        e.wait_ge(tot, 1)
        own(e.tensor_copy(mg[:], ps[:, 0, 0:GROUPS]))
        for i in range(TT):
            e.tensor_tensor(grp(xn[:, i, :]), grp(t[:, i, :]), per_group(mg), ALU.subtract).then_inc(centred, 1)
        e.wait_ge(squared, TT)
        e.tensor_reduce(s1[:], sq[:].rearrange("p i (g c) -> p g i c", g=GROUPS), AX.XY, ALU.add).then_inc(sums, 1)
        e.wait_ge(tot, 2)
        e.tensor_scalar(rgr[:], ps[:, 1, 0:GROUPS], L01_EPS_GN, None, ALU.add).then_inc(sq_in, 1)
        e.wait_ge(sq_out, 3)
        own(e.reciprocal(rgr[:], rgr[:]))
        for i in range(TT):
            e.tensor_tensor(grp(xn[:, i, :]), grp(xn[:, i, :]), per_group(rgr), ALU.mult).then_inc(scaled, 1)
        scans(e, 1)

    def grp(x):
        return x.rearrange("p (g c) -> p g c", g=GROUPS)

    def per_group(x):
        return x[:].unsqueeze(2).to_broadcast([P, GROUPS, SEQ // GROUPS])

    def scans(e, l):
        e.wait_ge(pre, l + 1)
        e.scalar_tensor_tensor(out=ab[:], in0=xb[:], scalar=-1.0, in1=xb[:], op0=ALU.mult, op1=ALU.min).then_inc(negabs, 1)
        e.wait_ge(log1p, 2 * l + 2)
        e.scalar_tensor_tensor(out=dtt[:], in0=xb[:], scalar=0.0, in1=lg[:], op0=ALU.max, op1=ALU.add).then_inc(dt_done, 1)
        for i in range(TT):
            e.wait_ge(spread_d, l * TT + i + 1)
            e.tensor_tensor_scan(sq[:, i, :], ps[:, i % 4, :], xn[:, i, :], 0.0, ALU.mult, ALU.add).then_inc(scanned, 1)

    def pool(e):
        e.wait_ge(x_tm_in, 16)
        core.zero_tables(e, zero)
        for l in range(2):
            for i in range(TT):
                e.wait_ge(scanned, l * TT + i + 1)
                e.tensor_tensor(t[:, i, :], t[:, i, :], sq[:, i, :], ALU.add).then_inc(added, 1)
        e.wait_ge(added, 2 * TT)
        e.wait_ge(core.zero_out, 32)

    def act(e):
        own = Chain(e, act_own)
        for k, s in enumerate((rg, rc)):
            e.wait_ge(sq_in, k + 1)
            e.activation(s[:], s[:], ACT.Sqrt).then_inc(sq_out, 1)
        e.wait_ge(par_in, PAR)
        own(e.activation(nega[:], loga[:], ACT.Exp))
        own(e.mul(nega[:], nega[:], -1.0))
        for i in range(TT):
            e.wait_ge(turned, i + 1)
            e.activation(xn[:, i, :], ps[:, 2 + i % 4, :], ACT.Identity, scale=lnw[:, i:i + 1], bias=lnb[:, i:i + 1])\
                .then_inc(affine, 1)
        decay(e, 0)
        for i in range(TT):
            e.wait_ge(centred, i + 1)
            e.activation(sq[:, i, :], xn[:, i, :], ACT.Square).then_inc(squared, 1)
        e.wait_ge(sq_in, 3)
        e.activation(rgr[:], rgr[:], ACT.Sqrt).then_inc(sq_out, 1)
        decay(e, 1)

    def decay(e, l):
        e.wait_ge(dt_raw, l + 1)
        e.activation(xb[:], ps[0:H2, 6, :], ACT.Identity, bias=dtb[:, l:l + 1]).then_inc(pre, 1)
        e.wait_ge(negabs, l + 1)
        e.activation(ex[:], ab[:], ACT.Exp).then_inc(log1p, 1)
        e.wait_ge(log1p, 2 * l + 1)
        e.activation(lg[:], ex[:], ACT.Ln, bias=1.0).then_inc(log1p, 1)
        e.wait_ge(dt_done, l + 1)
        e.activation(dec[:], dtt[:], ACT.Exp, scale=nega[:, l:l + 1]).then_inc(decayed, 1)

    def pe(e):
        e.wait_ge(par_in, PAR)
        e.wait_ge(core.consts_in, core.CONSTS)
        e.wait_ge(ch_mean, 1)
        e.matmul(ps[:, 0, 0:KD], g16[:], dev[:], start=True, stop=True).then_inc(g_mean, 1)
        e.wait_ge(ch_spread, 1)
        e.matmul(ps[:, 1, 0:KD], g16[:], q[:], start=True, stop=True).then_inc(g_var, 1)
        for i in range(TT):
            if i >= 4:
                e.wait_ge(affine, i - 3)
            for j in range(KD):
                if i == 0:
                    e.wait_ge(x_hat, j + 1)
                x = e.transpose(ps[:, 2 + i % 4, j * P:(j + 1) * P], xcm[:, j, i * P:(i + 1) * P], core.ident[:])
            x.then_inc(turned, 1)
        decays(e, 0)
        e.wait_ge(sums, 1)
        e.matmul(ps[:, 0, 0:GROUPS], onesn[:], s1[:], start=True, stop=True).then_inc(tot, 1)
        e.wait_ge(sums, 2)
        e.matmul(ps[:, 1, 0:GROUPS], onesn[:], s1[:], start=True, stop=True).then_inc(tot, 1)
        decays(e, 1)

    def decays(e, l):
        e.wait_ge(weights, l + 1)
        for i in range(TT):
            e.wait_ge(scaled if l else affine, i + 1)
            x = e.matmul(ps[0:H2, 6, :], wsel[:, l, i, :], xn[:, i, :], start=(i == 0), stop=(i == TT - 1))
        x.then_inc(dt_raw, 1)
        e.wait_ge(decayed, l + 1)
        for i in range(TT):
            if i >= 4:
                e.wait_ge(scanned, l * TT + i - 3)
            e.matmul(ps[:, i % 4, :], core.sel[:, i, :], dec[:], start=True, stop=True).then_inc(spread_d, 1)

    return dict(sp=sp, dve=dve, act=act, pe=pe, pool=pool, cx=cx, used=used)


MB_EPS = 1e-5
MB_DPROJ = 2 * DI + 2 * NS + H2
MB_CX, MB_CB, MB_CC, MB_CDT = DI, 2 * DI, 2 * DI + NS, 2 * DI + 2 * NS
MB_PIECES = 6
MB_ER = 2
MB_EG = 8
MB_LNW, MB_LNB, MB_CVW, MB_CVB, MB_BCW, MB_BCB, MB_DCOL, MB_RMSW, MB_DTB, MB_ALOG = 0, 4, 8, 40, 48, 56, 58, 66, 74, 106
MB_NPAR = 138


def stage_mamba(core, ps):
    nc, ins, t = core.nc, core.ins, core.t
    cx = ExitStack()
    sb = lambda n, s, d=F32: core.sb("mb_" + n, s, d, cx)
    used = []
    sem = lambda n: core.stage_sem("m_" + n, cx, used)
    h = t
    kept = nc.dram_tensor("t_kept", [TOK, D], F32).ap().rearrange("(i p) f -> p i f", p=P)
    par = sb("par", [P, MB_NPAR])
    wi_hi, wi_lo = sb("wi_hi", [P, KD, MB_DPROJ], F16), sb("wi_lo", [P, KD, MB_DPROJ], F16)
    wo_hi, wo_lo = sb("wo_hi", [P, JD, D], F16), sb("wo_lo", [P, JD, D], F16)
    ring = sb("ring", [P, 2 * MB_DPROJ])
    raw = [ring[:, b * MB_DPROJ:(b + 1) * MB_DPROJ] for b in range(2)]
    u_hi, u_lo = sb("u_hi", [P, KD, TOK], F16), sb("u_lo", [P, KD, TOK], F16)
    stats, mv = sb("stats", [P, TT, 6]), sb("mv", [P, TT, 2])
    rstd = sb("rstd", [P, TT])
    nega = sb("nega", [P, H2])
    dtx, dtn, dte_ = sb("dtx", [P, TT, H2]), sb("dtn", [P, TT, H2]), sb("dte_", [P, TT, H2])
    dt, la, dend = sb("dt", [P, TT, H2]), sb("la", [P, TT, H2]), sb("dend", [P, TT, H2])
    edec, dte = sb("edec", [P, TT, H2]), sb("dte", [P, TT, H2])
    la_hi, la_lo = sb("la_hi", [P, TT, H2], F16), sb("la_lo", [P, TT, H2], F16)
    cumT = sb("cumT", [H2, TOK])
    tri_th = sb("tri_th", [P, P, H2], F16)
    r_hi, r_lo = (ring[:, b * 2048:(b + 1) * 2048].bitcast(F16).rearrange("p (t h) -> p t h", h=H2) for b in range(2))
    E = sb("E", [P, MB_ER * 512])
    M = sb("M", [P, H2, P])
    uf = M[:].rearrange("p h t -> p (h t)").rearrange("p (i f) -> p i f", i=TT)
    xp, bcp = sb("xp", [P, JD, P + 3]), sb("bcp", [NS, 2, P + 3])
    ca, cbc = sb("ca", [P, JD, P]), sb("cbc", [NS, 2, P])
    th, thbc = sb("th", [P, JD, P]), sb("thbc", [NS, 2, P])
    xc, bcc = sb("xc", [P, JD, P]), sb("bcc", [NS, 2, P])
    thz, sz = th, sb("sz", [P, JD, P])
    xdt, xe = sb("xdt", [P, DI]), sb("xe", [P, DI])
    btok = sb("btok", [P, NS])
    gm = sb("gm", [P, P])
    S = sb("S", [NS, DI])
    quad = sb("quad", [P, 4, DI])
    un = quad[:].rearrange("p a b -> p (a b)").rearrange("p (i f) -> p i f", i=TT)
    ec, yi, dx, y = (quad[:, a, :].rearrange("p (j t) -> p j t", j=JD) for a in range(4))
    ysq = sb("ysq", [P, JD, P])
    y_hi, y_lo = sb("y_hi", [P, JD, P], F16), sb("y_lo", [P, JD, P], F16)
    rv, rs, mhalf = sb("rv", [P, 1]), sb("rs", [P, 1]), sb("mhalf", [P, 1])

    dve_own, act_own, pool_own = sem("dve_own"), sem("act_own"), sem("pool_own")
    layer_open = sem("layer_open")
    par_in = sem("par_in")
    raw_in = [sem(f"raw_in{b}") for b in range(2)]
    w_hi, w_lo = sem("w_hi"), sem("w_lo")
    var_done, sd_done = sem("var_done"), sem("sd_done")
    un_done, turned, uf_done, uhi_done, ulo_done = (sem(n) for n in ("un_done", "turned", "uf_done", "uhi_done", "ulo_done"))
    dt_mm, dtn_done, dt_log, la_done, sums_mm, sums_exp, cum_ev, prep = (
        sem(n) for n in ("dt_mm", "dtn_done", "dt_log", "la_done", "sums_mm", "sums_exp", "cum_ev", "prep"))
    nega_done = sem("nega_done")
    zeroed = sem("zeroed")
    x_mm, bc_mm, z_mm = sem("x_mm"), sem("bc_mm"), sem("z_mm")
    x_ev, bc_ev = sem("x_ev"), sem("bc_ev")
    halo = sem("halo")
    acc, tanh, xc_done, bcc_done = sem("acc"), sem("tanh"), sem("xc_done"), sem("bcc_done")
    thz_done, sz_done = sem("thz_done"), sem("sz_done")
    rhi_done, rlo_done = sem("rhi_done"), sem("rlo_done")
    xtr, x_scaled, g_mm, gm_done, bt_done = (sem(n) for n in ("xtr", "x_scaled", "g_mm", "gm_done", "bt_done"))
    diff, exped, m_done = sem("diff"), sem("exped"), sem("m_done")
    ecum_mm, ec_done, inter_mm, yi_done, yid_done, dx_done = (
        sem(n) for n in ("ecum_mm", "ec_done", "inter_mm", "yi_done", "yid_done", "dx_done"))
    ds_mm, smul, s_done = sem("ds_mm"), sem("smul"), sem("s_done")
    intra_mm, ya_done, y_done, yhi_done, ylo_done, ysq_done = (
        sem(n) for n in ("intra_mm", "ya_done", "y_done", "yhi_done", "ylo_done", "ysq_done"))
    rms_mm, rv_done, pow_done, out_mm, h_done = (sem(n) for n in ("rms_mm", "rv_done", "pow_done", "out_mm", "h_done"))

    W_IN = ins["m_in_w"]
    W_OUT = ins["m_out_w"]

    def chunks(e, l, body):
        body(0, l * TT, True, False)
        with e.Fori(1, TT - 1) as i:
            body(i, l * TT + i, False, False)
        body(TT - 1, l * TT + TT - 1, False, True)

    def heads(x):
        return x.rearrange("p (h q) -> p h q", h=H2)

    def sp(e):
        e.dma_start(kept, t[:]).then_inc(t_kept, 16)
        with e.Fori(0, LAYERS) as l:
            e.wait_ge(layer_open, l + 1)
            e.dma_start(par[:], ins["m_par"][l, :, :]).then_inc(par_in, 16)
            for n in range(MB_PIECES):
                if n >= 2:
                    e.wait_ge(w_hi, l * MB_PIECES + n - 1)
                    e.wait_ge(w_lo, l * MB_PIECES + n - 1)
                if n < KD:
                    e.dma_start(raw[n % 2], W_IN[l, n * P:(n + 1) * P, :]).then_inc(raw_in[n % 2], 16)
                else:
                    e.dma_start(raw[n % 2][:, 0:4 * D].rearrange("p (j f) -> p j f", j=4),
                                W_OUT[l, (n - KD) * 512:(n - KD + 1) * 512, :].rearrange("(j p) f -> p j f", p=P))\
                        .then_inc(raw_in[n % 2], 16)

        e.wait_ge(layer_open, LAYERS + 1)
        e.dma_start(uf, kept).then_inc(t_back, 16)

    def dve(e):
        own = Chain(e, dve_own)

        def loop8(body):
            base = own.n
            with e.Fori(0, TT) as i:
                own.n = base + i
                body(i).then_inc(dve_own, 1)
            own.n = base + TT
            e.wait_ge(dve_own, own.n)
            core.apart(e)

        def layernorm(src, n):
            loop8(lambda i: e.bn_stats(stats[:, i, :], src[:, i, :]))
            for i in range(TT):
                x = e.bn_aggr(mv[:, i, :], stats[:, i, :])
            own(x)
            e.tensor_scalar(rstd[:], mv[:, :, 1], MB_EPS, None, ALU.add).then_inc(var_done, 1)
            e.wait_ge(sd_done, n)
            own(e.reciprocal(rstd[:], rstd[:]))

        e.wait_ge(t_kept, 16)
        e.tensor_copy(tri_th[:], core.tri16[:].unsqueeze(2).to_broadcast([P, P, H2]))
        layernorm(t, 1)
        loop8(lambda i: e.tensor_scalar(h[:, i, :], t[:, i, :], mv[:, i, 0:1], rstd[:, ds(i, 1)],
                                        ALU.subtract, ALU.mult))
        e.tensor_copy(rv[:], rstd[:, 0:1]).then_inc(layer_open, 1)

        start = own.n
        with e.Fori(0, LAYERS) as l:
            own.n = start + l * OWN_PER_LAYER
            e.wait_ge(layer_open, l + 1)
            core.apart(e)
            layernorm(h, l + 2)
            core.apart(e)
            with e.Fori(0, TT) as i:
                e.tensor_scalar(un[:, i, :], h[:, i, :], mv[:, i, 0:1], rstd[:, ds(i, 1)],
                                ALU.subtract, ALU.mult).then_inc(un_done, 1)
            e.wait_ge(par_in, (l + 1) * 16)
            core.apart(e)
            own(e.tensor_scalar(par[:, MB_CVW:MB_DCOL], par[:, MB_CVW:MB_DCOL], 0.5, None, ALU.mult))
            for n in range(MB_PIECES):
                e.wait_ge(w_hi, l * MB_PIECES + n + 1)
                if n < KD:
                    e.tensor_tensor(wi_lo[:, n, :], raw[n % 2], wi_hi[:, n, :], ALU.subtract).then_inc(w_lo, 1)
                else:
                    for q in range(4):
                        j = 4 * (n - KD) + q
                        x = e.scalar_tensor_tensor(out=wo_lo[:, j, :], in0=raw[n % 2][:, q * D:(q + 1) * D],
                                                   scalar=par[:, MB_RMSW + j:MB_RMSW + j + 1], in1=wo_hi[:, j, :],
                                                   op0=ALU.mult, op1=ALU.subtract)
                    x.then_inc(w_lo, 1)
            core.apart(e)
            with e.Fori(0, TT) as i:
                e.wait_ge(uhi_done, l * TT + i + 1)
                e.tensor_tensor(u_lo[:, :, ds(i * P, P)], uf[:, i, :].rearrange("p (k c) -> p k c", k=KD),
                                u_hi[:, :, ds(i * P, P)], ALU.subtract).then_inc(ulo_done, 1)
            e.wait_ge(dt_mm, l + 1)
            own(e.tensor_tensor(dtx[:], ps[:, 2, 0:TT * H2].rearrange("p (i h) -> p i h", i=TT),
                                par[:, MB_DTB:MB_DTB + H2].unsqueeze(1).to_broadcast([P, TT, H2]), ALU.add))
            e.scalar_tensor_tensor(out=dtn[:], in0=dtx[:], scalar=-1.0, in1=dtx[:], op0=ALU.mult, op1=ALU.min)\
                .then_inc(dtn_done, 1)
            e.wait_ge(dt_log, l + 1)
            own(e.scalar_tensor_tensor(out=dt[:], in0=dtx[:], scalar=0.0, in1=dte_[:], op0=ALU.max, op1=ALU.add))
            e.wait_ge(nega_done, l + 1)
            e.tensor_tensor(la[:], dt[:], nega[:].unsqueeze(1).to_broadcast([P, TT, H2]), ALU.mult).then_inc(la_done, 1)
            e.wait_ge(la_done, l + 1)
            own(e.tensor_copy(la_hi[:], la[:]))
            own(e.tensor_tensor(la_lo[:], la[:], la_hi[:], ALU.subtract))
            e.wait_ge(sums_exp, l + 1)
            e.tensor_tensor(dte[:], dend[:], dt[:], ALU.mult).then_inc(prep, 1)
            e.wait_ge(prep, l + 1)

            def r_build(i):
                e.tensor_tensor(r_lo, la_lo[:, i, :].unsqueeze(1).to_broadcast([P, P, H2]), tri_th[:], ALU.mult)\
                    .then_inc(rlo_done, 1)

            def conv(g):
                for q in range(2):
                    e.wait_ge(x_ev, 2 * g + q + 1)
                    for k in range(TAPS):
                        for j in range(4 * q, 4 * q + 4):
                            w = par[:, MB_CVW + 4 * j + k:MB_CVW + 4 * j + k + 1]
                            if k == 0:
                                x = e.tensor_scalar(ca[:, j, :], xp[:, j, 0:P], w, par[:, MB_CVB + j:MB_CVB + j + 1],
                                                    ALU.mult, ALU.add)
                            else:
                                x = e.scalar_tensor_tensor(out=ca[:, j, :], in0=xp[:, j, k:k + P], scalar=w,
                                                           in1=ca[:, j, :], op0=ALU.mult, op1=ALU.add)
                        if k < TAPS - 1:
                            own(x)
                    x.then_inc(acc, 1)
                e.wait_ge(bc_ev, g + 1)
                for k in range(TAPS):
                    for c in range(2):
                        w = par[0:NS, MB_BCW + 4 * c + k:MB_BCW + 4 * c + k + 1]
                        if k == 0:
                            x = e.tensor_scalar(cbc[:, c, :], bcp[:, c, 0:P], w, par[0:NS, MB_BCB + c:MB_BCB + c + 1],
                                                ALU.mult, ALU.add)
                        else:
                            x = e.scalar_tensor_tensor(out=cbc[:, c, :], in0=bcp[:, c, k:k + P], scalar=w,
                                                       in1=cbc[:, c, :], op0=ALU.mult, op1=ALU.add)
                    if k < TAPS - 1:
                        own(x)
                x.then_inc(acc, 1)
                for q in range(2):
                    e.wait_ge(tanh, 3 * g + q + 1)
                    e.scalar_tensor_tensor(out=xc[:, 4 * q:4 * q + 4, :], in0=th[:, 4 * q:4 * q + 4, :], scalar=1.0,
                                           in1=ca[:, 4 * q:4 * q + 4, :], op0=ALU.add, op1=ALU.mult).then_inc(xc_done, 1)
                e.wait_ge(tanh, 3 * g + 3)
                e.scalar_tensor_tensor(out=bcc[:], in0=thbc[:], scalar=1.0, in1=cbc[:], op0=ALU.add, op1=ALU.mult)\
                    .then_inc(bcc_done, 1)

            def gate(g):
                for q in range(2):
                    e.wait_ge(thz_done, 2 * g + q + 1)
                    e.scalar_tensor_tensor(out=sz[:, 4 * q:4 * q + 4, :], in0=thz[:, 4 * q:4 * q + 4, :], scalar=1.0,
                                           in1=ps[:, 1 - q, :].rearrange("p (j t) -> p j t", j=4),
                                           op0=ALU.add, op1=ALU.mult).then_inc(sz_done, 1)

            def finish(i, g):
                e.wait_ge(rms_mm, g + 1)
                e.tensor_scalar(rv[:], ps[:, 2, 384:385], 1.0 / DI, 4 * MB_EPS, ALU.mult, ALU.add).then_inc(rv_done, 1)
                e.wait_ge(pow_done, g + 1)
                e.wait_ge(out_mm, g + 1)
                e.scalar_tensor_tensor(out=h[:, i, :], in0=ps[:, 7, :], scalar=rs[:], in1=h[:, i, :],
                                       op0=ALU.mult, op1=ALU.add).then_inc(h_done, 1)

            def split_y(g):
                e.wait_ge(yhi_done, g + 1)
                e.tensor_tensor(y_lo[:], y, y_hi[:], ALU.subtract).then_inc(ylo_done, 1)

            r_build(0)
            conv(l * TT)
            gate(l * TT)

            def body(i, g, is_first, is_last):
                if not is_first:
                    split_y(g - 1)
                e.wait_ge(g_mm, g + 1)
                e.tensor_tensor(gm[:], ps[:, 2, P:2 * P], core.tri[:], ALU.mult).then_inc(gm_done, 1)
                e.wait_ge(xtr, g + 1)
                xt = heads(ps[:, 5:7, :].rearrange("p b n -> p (b n)"))
                e.tensor_tensor(heads(xdt[:]), xt, dt[:, i, :].unsqueeze(2).to_broadcast([P, H2, 32]), ALU.mult)
                e.tensor_tensor(heads(xe[:]), xt, dte[:, i, :].unsqueeze(2).to_broadcast([P, H2, 32]), ALU.mult)\
                    .then_inc(x_scaled, 1)
                e.wait_ge(gm_done, g + 1)
                for k in range(MB_EG):
                    e.wait_ge(exped, g * MB_EG + k + 1)
                    e.tensor_tensor(M[:].rearrange("p h t -> p t h")[:, 16 * k:16 * k + 16, :],
                                    E[:, 512 * (k % MB_ER):512 * (k % MB_ER + 1)].rearrange("p (t h) -> p t h", h=H2),
                                    gm[:, 16 * k:16 * k + 16].unsqueeze(2).to_broadcast([P, 16, H2]), ALU.mult)\
                        .then_inc(m_done, 1)
                if not is_first:
                    finish(i - 1, g - 1)
                e.wait_ge(inter_mm, g + 1)
                e.wait_ge(ec_done, g + 1)
                e.tensor_tensor(yi.rearrange("p j t -> p (j t)"), ps[:, 5:7, :].rearrange("p b n -> p (b n)"),
                                ec.rearrange("p j t -> p (j t)"), ALU.mult).then_inc(yi_done, 1)
                e.wait_ge(ds_mm, g + 1)
                e.wait_ge(smul, g + 1)
                e.tensor_tensor(S[:], S[:], ps[0:NS, 3:5, :].rearrange("p b n -> p (b n)"), ALU.add).then_inc(s_done, 1)
                if not is_last:
                    e.wait_ge(diff, MB_EG * (g + 1))
                    r_build(i + 1)
                    e.wait_ge(dx_done, g + 1)
                    conv(g + 1)
                e.wait_ge(intra_mm, g + 1)
                e.wait_ge(yid_done, g + 1)
                e.tensor_tensor(y[:, 0:4, :], ps[:, 7, :].rearrange("p (j t) -> p j t", j=4), yi[:, 0:4, :], ALU.add)
                e.tensor_tensor(y[:, 4:8, :], ps[:, 2, :].rearrange("p (j t) -> p j t", j=4), yi[:, 4:8, :], ALU.add)\
                    .then_inc(ya_done, 1)
                e.wait_ge(ya_done, g + 1)
                e.tensor_tensor(y, y, sz[:], ALU.mult).then_inc(y_done, 1)
                if not is_last:
                    e.wait_ge(y_done, g + 1)
                    gate(g + 1)

            own_before = own.n
            body(0, l * TT, True, False)
            per_chunk = OWN_PER_CONV
            own.n = own_before + per_chunk
            with e.Fori(1, TT - 1) as i:
                own.n = own_before + i * per_chunk
                body(i, l * TT + i, False, False)
            own.n = own_before + (TT - 1) * per_chunk
            body(TT - 1, l * TT + TT - 1, False, True)
            split_y(l * TT + TT - 1)
            finish(TT - 1, l * TT + TT - 1)
            e.wait_ge(h_done, (l + 1) * TT)
            e.tensor_copy(rv[:], rstd[:, 0:1]).then_inc(layer_open, 1)
        e.wait_ge(layer_open, LAYERS + 1)
        e.wait_ge(t_back, 16)
        e.tensor_tensor(t[:], h[:], uf, ALU.add)

    OWN_PER_CONV = 2 * (TAPS - 1) + TAPS - 1
    OWN_PER_LAYER = TT + 1 + 1 + 1 + 1 + 1 + 1 + 1 + TT * OWN_PER_CONV

    def act(e):
        own = Chain(e, act_own)
        e.wait_ge(var_done, 1)
        e.activation(rstd[:], rstd[:], ACT.Sqrt).then_inc(sd_done, 1)
        with e.Fori(0, LAYERS) as l:
            e.wait_ge(layer_open, l + 1)
            e.wait_ge(var_done, l + 2)
            e.activation(rstd[:], rstd[:], ACT.Sqrt).then_inc(sd_done, 1)
            e.wait_ge(par_in, (l + 1) * 16)
            with e.Fori(0, TT) as i:
                e.wait_ge(turned, l * TT + i + 1)
                for k in range(KD):
                    x = e.activation(uf[:, i, k * P:(k + 1) * P], ps[:, i, k * P:(k + 1) * P], ACT.Identity,
                                     scale=par[:, MB_LNW + k:MB_LNW + k + 1], bias=par[:, MB_LNB + k:MB_LNB + k + 1])
                x.then_inc(uf_done, 1)
            for n in range(MB_PIECES):
                e.wait_ge(raw_in[n % 2], (l * (MB_PIECES // 2) + n // 2 + 1) * 16)
                if n < KD:
                    e.activation(wi_hi[:, n, :], raw[n % 2], ACT.Copy).then_inc(w_hi, 1)
                else:
                    for q in range(4):
                        j = 4 * (n - KD) + q
                        x = e.activation(wo_hi[:, j, :], raw[n % 2][:, q * D:(q + 1) * D], ACT.Copy,
                                         scale=par[:, MB_RMSW + j:MB_RMSW + j + 1])
                    x.then_inc(w_hi, 1)
            own.n = l * 4
            own(e.activation(nega[:], par[:, MB_ALOG:MB_ALOG + H2], ACT.Exp))
            e.mul(nega[:], nega[:], -1.0).then_inc(nega_done, 1)
            e.wait_ge(dtn_done, l + 1)
            own(e.activation(dte_[:], dtn[:], ACT.Exp))
            e.activation(dte_[:], dte_[:], ACT.Ln, bias=1.0).then_inc(dt_log, 1)
            e.wait_ge(sums_mm, l + 1)
            own(e.activation(dend[:], ps[:, 3, 0:TT * H2].rearrange("p (i h) -> p i h", i=TT), ACT.Exp))
            own(e.activation(edec[:], ps[:, 3, TT * H2:2 * TT * H2].rearrange("p (i h) -> p i h", i=TT), ACT.Exp))
            e.activation(cumT[:], ps[0:H2, 4:6, :].rearrange("p b n -> p (b n)"), ACT.Copy).then_inc(sums_exp, 1)

            def project_x(g, is_first):
                if not is_first:
                    e.wait_ge(halo, g)
                for q in range(2):
                    e.wait_ge(x_mm, 2 * g + q + 1)
                    e.activation(xp[:, 4 * q:4 * q + 4, 3:P + 3], ps[:, q, :].rearrange("p (j t) -> p j t", j=4),
                                 ACT.Copy).then_inc(x_ev, 1)
                e.wait_ge(bc_mm, g + 1)
                e.activation(bcp[:, :, 3:P + 3], ps[0:NS, 0, 0:2 * P].rearrange("p (c t) -> p c t", c=2), ACT.Copy)\
                    .then_inc(bc_ev, 1)
                for q in range(2):
                    e.wait_ge(acc, 3 * g + q + 1)
                    e.activation(th[:, 4 * q:4 * q + 4, :], ca[:, 4 * q:4 * q + 4, :], ACT.Tanh).then_inc(tanh, 1)
                e.wait_ge(acc, 3 * g + 3)
                e.activation(thbc[:], cbc[:], ACT.Tanh).then_inc(tanh, 1)

            def project_z(g):
                e.wait_ge(xc_done, 2 * g + 2)
                for q in range(2):
                    e.wait_ge(z_mm, 2 * g + q + 1)
                    e.activation(thz[:, 4 * q:4 * q + 4, :], ps[:, 1 - q, :].rearrange("p (j t) -> p j t", j=4),
                                 ACT.Tanh, scale=0.5).then_inc(thz_done, 1)

            def split_y(g):
                e.wait_ge(y_done, g + 1)
                e.activation(y_hi[:], y, ACT.Copy).then_inc(yhi_done, 1)
                e.activation(ysq[:], y, ACT.Square).then_inc(ysq_done, 1)

            e.wait_ge(zeroed, l + 1)
            project_x(l * TT, True)
            project_z(l * TT)

            def body(i, g, is_first, is_last):
                if not is_first:
                    split_y(g - 1)
                e.wait_ge(gm_done, g + 1)
                e.activation(btok[:], ps[:, 2, 0:NS], ACT.Copy).then_inc(bt_done, 1)
                for k in range(MB_EG):
                    e.wait_ge(diff, MB_EG * g + k + 1)
                    if k >= MB_ER:
                        e.wait_ge(m_done, MB_EG * g + k - MB_ER + 1)
                    e.activation(E[:, 512 * (k % MB_ER):512 * (k % MB_ER + 1)], ps[:, 3 + k % 2, :], ACT.Exp).then_inc(exped, 1)
                e.wait_ge(ecum_mm, g + 1)
                e.activation(ec.rearrange("p j t -> p (j t)"), ps[:, 3:5, :].rearrange("p b n -> p (b n)"), ACT.Exp)\
                    .then_inc(ec_done, 1)
                if not is_last:
                    project_x(g + 1, False)
                    project_z(g + 1)

            chunks(e, l, body)
            split_y(l * TT + TT - 1)

    def pool(e):
        e.memset(mhalf[:], -0.5).then_inc(pool_own, 1)
        e.wait_ge(pool_own, 1)
        with e.Fori(0, LAYERS) as l:
            e.wait_ge(layer_open, l + 1)
            core.apart(e)
            e.memset(S[:], 0.0)
            e.memset(bcp[:, :, 0:3], 0.0)
            e.memset(xp[:, :, 0:3], 0.0).then_inc(zeroed, 1)
            with e.Fori(0, TT) as i:
                e.wait_ge(uf_done, l * TT + i + 1)
                core.apart(e)
                e.tensor_copy(u_hi[:, :, ds(i * P, P)], uf[:, i, :].rearrange("p (k c) -> p k c", k=KD)).then_inc(uhi_done, 1)
            e.wait_ge(prep, l + 1)

            def r_build(i):
                e.tensor_tensor(r_hi, la_hi[:, i, :].unsqueeze(1).to_broadcast([P, P, H2]), tri_th[:], ALU.mult)\
                    .then_inc(rhi_done, 1)

            def keep_halo(g):
                e.wait_ge(acc, 3 * (g + 1))
                core.apart(e)
                e.tensor_copy(bcp[:, :, 0:3], bcp[:, :, P:P + 3])
                e.tensor_copy(xp[:, :, 0:3], xp[:, :, P:P + 3]).then_inc(halo, 1)

            def power(g):
                e.wait_ge(rv_done, g + 1)
                e.tensor_tensor(rs[:], rv[:], mhalf[:], ALU.pow).then_inc(pow_done, 1)

            r_build(0)
            keep_halo(l * TT)

            def body(i, g, is_first, is_last):
                if not is_first:
                    power(g - 1)
                    e.wait_ge(s_done, g)
                e.wait_ge(inter_mm, g + 1)
                e.tensor_tensor(heads(S[:]), heads(S[:]), edec[0:NS, i, :].unsqueeze(2).to_broadcast([NS, H2, 32]),
                                ALU.mult).then_inc(smul, 1)
                e.wait_ge(xc_done, 2 * (g + 1))
                e.tensor_tensor(dx, xc[:], par[:, MB_DCOL:MB_DCOL + JD].unsqueeze(2).to_broadcast([P, JD, P]), ALU.mult)\
                    .then_inc(dx_done, 1)
                e.wait_ge(dx_done, g + 1)
                e.wait_ge(yi_done, g + 1)
                e.tensor_tensor(yi, yi, dx, ALU.add).then_inc(yid_done, 1)
                if not is_last:
                    e.wait_ge(diff, MB_EG * (g + 1))
                    r_build(i + 1)
                    keep_halo(g + 1)

            chunks(e, l, body)
            power(l * TT + TT - 1)

    def pe(e):
        with e.Fori(0, LAYERS) as l:
            e.wait_ge(layer_open, l + 1)
            for i in range(TT):
                e.wait_ge(un_done, l * TT + i + 1)
                for k in range(KD):
                    x = e.transpose(ps[:, i, k * P:(k + 1) * P], un[:, i, k * P:(k + 1) * P], core.ident[:])
                x.then_inc(turned, 1)
            e.wait_ge(w_lo, l * MB_PIECES + KD)
            e.wait_ge(uf_done, (l + 1) * TT)
            core.apart(e)
            with e.Fori(0, TT) as i:
                e.wait_ge(ulo_done, l * TT + i + 1)
                core.apart(e)
                for k in range(KD):
                    for n, (a, b) in enumerate(((u_hi, wi_hi), (u_hi, wi_lo), (u_lo, wi_hi))):
                        x = e.matmul(ps[:, 2, ds(i * H2, H2)], a[:, k, ds(i * P, P)], b[:, k, MB_CDT:MB_CDT + H2],
                                     start=(k == 0 and n == 0), stop=(k == KD - 1 and n == 2))
                x.then_inc(dt_done_mm, 1)
            x = e.matmul(ps[0:1, 6, 0:1], core.ones[:, 0:1], core.ones[:, 0:1], start=True, stop=True)
            x.then_inc(dt_mm, 1)
            e.wait_ge(la_done, l + 1)
            la2 = la[:].rearrange("p i h -> p (i h)")
            e.matmul(ps[:, 3, 0:TT * H2], core.after[:], la2, start=True, stop=True)
            e.matmul(ps[:, 3, TT * H2:2 * TT * H2], core.ones[:], la2, start=True, stop=True)
            for i in range(TT):
                x = e.matmul(ps[0:H2, 4 + i // 4, (i % 4) * P:(i % 4 + 1) * P], la[:, i, :], core.tri[:], start=True, stop=True)
            x.then_inc(sums_mm, 1)

            def project(i, bank, tiles, width, done):
                for n, f in enumerate(tiles):
                    for k in range(KD):
                        for m, (a, b) in enumerate(((wi_hi, u_hi), (wi_lo, u_hi), (wi_hi, u_lo))):
                            x = e.matmul(ps[0:width, bank, n * P:(n + 1) * P], a[:, k, f:f + width],
                                         b[:, k, ds(i * P, P)], start=(k == 0 and m == 0), stop=(k == KD - 1 and m == 2))
                x.then_inc(done, 1)

            def project_x(i, g, is_first):
                if not is_first:
                    e.wait_ge(sz_done, 2 * g)
                for q in range(2):
                    project(i, q, [MB_CX + P * j for j in range(4 * q, 4 * q + 4)], P, x_mm)
                e.wait_ge(x_ev, 2 * g + 1)
                core.apart(e)
                project(i, 0, [MB_CB, MB_CC], NS, bc_mm)

            def project_z(i, g):
                e.wait_ge(x_ev, 2 * g + 2)
                project(i, 1, [P * j for j in range(4)], P, z_mm)
                e.wait_ge(bc_ev, g + 1)
                project(i, 0, [P * j for j in range(4, 8)], P, z_mm)

            def out_project(i, g):
                e.wait_ge(ysq_done, g + 1)
                for j in range(JD):
                    x = e.matmul(ps[:, 2, 384:385], ysq[:, j, :], core.ones[:, 0:1], start=(j == 0), stop=(j == JD - 1))
                x.then_inc(rms_mm, 1)
                e.wait_ge(ylo_done, g + 1)
                for j in range(JD):
                    for m, (a, b) in enumerate(((y_hi, wo_hi), (y_hi, wo_lo), (y_lo, wo_hi))):
                        x = e.matmul(ps[:, 7, :], a[:, j, :], b[:, j, :], start=(j == 0 and m == 0),
                                     stop=(j == JD - 1 and m == 2))
                x.then_inc(out_mm, 1)

            e.wait_ge(sums_exp, l + 1)
            e.wait_ge(w_lo, (l + 1) * MB_PIECES)
            project_x(0, l * TT, True)
            project_z(0, l * TT)

            def body(i, g, is_first, is_last):
                e.wait_ge(xc_done, 2 * (g + 1))
                e.wait_ge(bcc_done, g + 1)
                if not is_first:
                    e.wait_ge(yi_done, g)
                    e.wait_ge(ya_done, g)
                core.apart(e)
                e.transpose(ps[:, 2, 0:NS], bcc[:, 0, :], core.ident[0:NS, 0:NS])
                e.matmul(ps[:, 2, P:2 * P], bcc[:, 0, :], bcc[:, 1, :], start=True, stop=True).then_inc(g_mm, 1)
                for j in range(JD):
                    x = e.transpose(ps[:, 5 + j // 4, (j % 4) * P:(j % 4 + 1) * P], xc[:, j, :], core.ident[:])
                x.then_inc(xtr, 1)
                e.wait_ge(rhi_done, g + 1)
                e.wait_ge(rlo_done, g + 1)
                if not is_first:
                    e.wait_ge(s_done, g)
                for k in range(MB_EG):
                    if k >= 2:
                        e.wait_ge(exped, MB_EG * g + k - 1)
                    for m, r in enumerate((r_hi, r_lo)):
                        x = e.matmul(ps[:, 3 + k % 2, :], core.after16[:], r[:, 16 * k:16 * k + 16, :].rearrange("p t h -> p (t h)"),
                                     start=(m == 0), stop=(m == 1))
                    x.then_inc(diff, 1)
                e.wait_ge(gm_done, g + 1)
                e.wait_ge(bt_done, g + 1)
                if not is_first:
                    out_project(i - 1, g - 1)
                e.wait_ge(exped, MB_EG * (g + 1))
                for j in range(JD):
                    x = e.matmul(ps[:, 3 + j // 4, (j % 4) * P:(j % 4 + 1) * P], core.sel[:, j, :], cumT[:, ds(i * P, P)],
                                 start=True, stop=True)
                x.then_inc(ecum_mm, 1)
                e.wait_ge(x_scaled, g + 1)
                for j in range(JD):
                    x = e.matmul(ps[:, 5 + j // 4, (j % 4) * P:(j % 4 + 1) * P], S[:, j * P:(j + 1) * P], bcc[:, 1, :],
                                 start=True, stop=True)
                x.then_inc(inter_mm, 1)
                e.wait_ge(ec_done, g + 1)
                for q in range(2):
                    x = e.matmul(ps[0:NS, 3 + q, :], btok[:], xe[:, q * 512:(q + 1) * 512], start=True, stop=True)
                x.then_inc(ds_mm, 1)
                if not is_last:
                    project_x(i + 1, g + 1, False)
                e.wait_ge(m_done, MB_EG * (g + 1))
                if not is_first:
                    e.wait_ge(h_done, g)
                for hh in range(H2):
                    bank = 7 if hh < 16 else 2
                    c = (hh // 4) % 4
                    x = e.matmul(ps[32 * (hh % 4):32 * (hh % 4) + 32, bank, c * P:(c + 1) * P],
                                 xdt[:, 32 * hh:32 * hh + 32], M[:, hh, :], start=True, stop=True)
                x.then_inc(intra_mm, 1)
                if not is_last:
                    project_z(i + 1, g + 1)

            chunks(e, l, body)
            out_project(TT - 1, l * TT + TT - 1)

    dt_done_mm = sem("dt_done_mm")
    t_kept, t_back = sem("t_kept"), sem("t_back")
    return dict(sp=sp, dve=dve, act=act, pe=pe, pool=pool, cx=cx, used=used)


FF_QEPS = 1e-5
FF_MAGIC = 1.5 * 2.0 ** 23
FF_RSQ = float(np.float32(1 / np.sqrt(D)))


def stage_ffn(core, ps):
    nc, ins, t = core.nc, core.ins, core.t
    cx = ExitStack()
    sb = lambda n, s, d=F32: core.sb("f_" + n, s, d, cx)
    used = []
    sem = lambda n: core.stage_sem("f_" + n, cx, used)
    wn = sb("wn", [P, KD, D])
    low = sb("low", [P, KD, D])
    tern = sb("tern", [P, KD, D])
    ternT = sb("ternT", [P, KD, D], F16)
    had = sb("had", [P, KD, D], F16)
    asum, scale, half, nhalf = (sb(n, [P, KD]) for n in ("asum", "scale", "half", "nhalf"))
    diag = sb("diag", [P, KD, P])
    wscale = sb("wscale", [P, D])
    stats, mv, rstd = sb("stats", [P, TT, 6]), sb("mv", [P, TT, 2]), sb("rstd", [P, TT])
    un = sb("un", [P, 2, D])
    u_hi, u_lo = sb("u_hi", [P, 2, D], F16), sb("u_lo", [P, 2, D], F16)
    amax, tscale, inv, mult = (sb(n, [P, TT]) for n in ("amax", "tscale", "inv", "mult"))
    minus_magic = sb("minus_magic", [P, 1])
    qa, qc = sb("qa", [P, D]), sb("qc", [P, 2, D])
    qT = sb("qT", [P, 2, D], F16)
    upd = sb("upd", [P, 2, D])

    w_in, had_in = sem("w_in"), sem("had_in")
    dve_own = sem("dve_own")
    var_done, sd_done, magic_set = sem("var_done"), sem("sd_done"), sem("magic_set")
    tern_done, wsc_done = sem("tern_done"), sem("wsc_done")
    w_tr, w_ev, wsc_mm = sem("w_tr"), sem("w_ev"), sem("wsc_mm")
    un_done, turned, hi_done, lo_done = (sem(n) for n in ("un_done", "turned", "hi_done", "lo_done"))
    h_mm, qa_done, q_done, q_tr, q_ev, o_mm, o_done, t_done = (
        sem(n) for n in ("h_mm", "qa_done", "q_done", "q_tr", "q_ev", "o_mm", "o_done", "t_done"))

    def rounds(*steps):
        for r in range(TT + max(lag for lag, _ in steps)):
            for lag, step in steps:
                if 0 <= r - lag < TT:
                    step(r - lag)

    def sp(e):
        e.dma_start(wn[:], ins["f_w"].rearrange("(j p) i -> p j i", p=P)).then_inc(w_in, 16)
        e.dma_start(had[:], ins["c_had"].rearrange("(k p) n -> p k n", p=P)).then_inc(had_in, 16)

    def dve(e):
        own = Chain(e, dve_own)
        for i in range(TT):
            x = e.bn_stats(stats[:, i, :], t[:, i, :])
        own(x)
        for i in range(TT):
            x = e.bn_aggr(mv[:, i, :], stats[:, i, :])
        own(x)
        e.tensor_scalar(rstd[:], mv[:, :, 1], 1e-5, None, ALU.add).then_inc(var_done, 1)
        e.wait_ge(w_in, 16)
        own(e.tensor_reduce(asum[:], wn[:], AX.X, ALU.add, apply_absolute_value=True))
        own(e.tensor_scalar(scale[:], asum[:], 1.0 / D, FF_QEPS, ALU.mult, ALU.max))
        e.tensor_scalar(half[:], scale[:], 0.5, None, ALU.mult)
        own(e.tensor_scalar(nhalf[:], scale[:], -0.5, None, ALU.mult))
        e.wait_ge(sd_done, 1)
        own(e.reciprocal(rstd[:], rstd[:]))

        def weights(j):
            e.tensor_scalar(diag[:, j, :], core.ident[:], scale[:, j:j + 1], None, ALU.mult)
            own(e.tensor_scalar(low[:, j, :], wn[:, j, :], nhalf[:, j:j + 1], None, ALU.is_lt))
            e.scalar_tensor_tensor(out=tern[:, j, :], in0=wn[:, j, :], scalar=half[:, j:j + 1], in1=low[:, j, :],
                                   op0=ALU.is_gt, op1=ALU.subtract).then_inc(tern_done, 1)

        def normalise(i):
            if i >= 2:
                e.wait_ge(turned, i - 1)
            e.tensor_scalar(un[:, i % 2, :], t[:, i, :], mv[:, i, 0:1], rstd[:, i:i + 1], ALU.subtract, ALU.mult)\
                .then_inc(un_done, 1)
            if i < 2:
                weights(2 * i)
                weights(2 * i + 1)

        def low_part(i):
            e.wait_ge(hi_done, i + 1)
            if i >= 2:
                e.wait_ge(h_mm, i - 1)
            e.tensor_tensor(u_lo[:, i % 2, :], ps[:, i % 2, :], u_hi[:, i % 2, :], ALU.subtract).then_inc(lo_done, 1)

        def quantise(i):
            e.wait_ge(h_mm, i + 1)
            c = slice(i, i + 1)
            h = ps[:, 2 + i % 2, :]
            own(e.tensor_reduce(amax[:, c], h, AX.X, ALU.max, apply_absolute_value=True))
            own(e.tensor_scalar(tscale[:, c], amax[:, c], FF_RSQ, FF_QEPS, ALU.mult, ALU.max))
            own(e.tensor_scalar(tscale[:, c], tscale[:, c], 1.0 / 7, None, ALU.mult))
            own(e.reciprocal(inv[:, c], tscale[:, c]))
            own(e.tensor_scalar(mult[:, c], inv[:, c], FF_RSQ, None, ALU.mult))
            e.tensor_scalar(qa[:], h, mult[:, c], FF_MAGIC, ALU.mult, ALU.add).then_inc(qa_done, 1)
            e.wait_ge(qa_done, i + 1)
            if i >= 2:
                e.wait_ge(q_tr, i - 1)
            e.tensor_scalar(qc[:, i % 2, :], qa[:], FF_MAGIC - 8, FF_MAGIC + 7, ALU.max, ALU.min).then_inc(q_done, 1)

        def update(i):
            e.wait_ge(o_mm, i + 1)
            if i == 0:
                e.wait_ge(wsc_done, 1)
            if i >= 2:
                e.wait_ge(t_done, i - 1)
            e.scalar_tensor_tensor(out=upd[:, i % 2, :], in0=ps[:, 6 + i % 2, :], scalar=tscale[:, i:i + 1],
                                   in1=wscale[:], op0=ALU.mult, op1=ALU.mult).then_inc(o_done, 1)

        rounds((0, normalise), (1, low_part), (2, quantise), (3, update))

    def act(e):
        e.wait_ge(var_done, 1)
        e.activation(rstd[:], rstd[:], ACT.Sqrt).then_inc(sd_done, 1)
        e.wait_ge(magic_set, 1)

        def high_part(i):
            e.wait_ge(turned, i + 1)
            if i >= 2:
                e.wait_ge(h_mm, i - 1)
            e.activation(u_hi[:, i % 2, :], ps[:, i % 2, :], ACT.Copy).then_inc(hi_done, 1)
            if i == 0:
                for k in range(KD):
                    e.wait_ge(w_tr, k + 1)
                    e.activation(ternT[:, k, :], ps[:, 4 + k, :], ACT.Copy).then_inc(w_ev, 1)
                e.wait_ge(wsc_mm, 1)
                e.activation(wscale[:], ps[:, 2, :], ACT.Copy).then_inc(wsc_done, 1)

        def quantised(i):
            e.wait_ge(q_tr, i + 1)
            if i >= 2:
                e.wait_ge(o_mm, i - 1)
            e.activation(qT[:, i % 2, :], ps[:, 4 + i % 2, :], ACT.Identity, bias=minus_magic[:]).then_inc(q_ev, 1)

        rounds((0, high_part), (2, quantised))

    def pool(e):
        e.memset(minus_magic[:], -FF_MAGIC).then_inc(magic_set, 1)
        for i in range(TT):
            e.wait_ge(o_done, i + 1)
            e.tensor_tensor(t[:, i, :], t[:, i, :], upd[:, i % 2, :], ALU.add).then_inc(t_done, 1)

    def pe(e):
        def turn(i):
            e.wait_ge(un_done, i + 1)
            if i >= 2:
                e.wait_ge(lo_done, i - 1)
            for k in range(KD):
                x = e.transpose(ps[:, i % 2, k * P:(k + 1) * P], un[:, i % 2, k * P:(k + 1) * P], core.ident[:])
            x.then_inc(turned, 1)
            if i == 1:
                for k in range(KD):
                    for j in range(KD):
                        e.wait_ge(tern_done, j + 1)
                        x = e.transpose(ps[:, 4 + k, j * P:(j + 1) * P], tern[:, j, k * P:(k + 1) * P], core.ident[:])
                    x.then_inc(w_tr, 1)
                for j in range(KD):
                    x = e.matmul(ps[:, 2, j * P:(j + 1) * P], core.ones[:], diag[:, j, :], start=True, stop=True)
                x.then_inc(wsc_mm, 1)

        def rotate(i):
            e.wait_ge(lo_done, i + 1)
            if i == 0:
                e.wait_ge(had_in, 16)
                e.wait_ge(wsc_done, 1)
            if i >= 2:
                e.wait_ge(q_done, i - 1)
            for k in range(KD):
                for m, a in enumerate((u_hi, u_lo)):
                    x = e.matmul(ps[:, 2 + i % 2, :], a[:, i % 2, k * P:(k + 1) * P], had[:, k, :],
                                 start=(k == 0 and m == 0), stop=(k == KD - 1 and m == 1))
            x.then_inc(h_mm, 1)

        def turn_back(i):
            e.wait_ge(q_done, i + 1)
            if i >= 2:
                e.wait_ge(q_ev, i - 1)
            for k in range(KD):
                x = e.transpose(ps[:, 4 + i % 2, k * P:(k + 1) * P], qc[:, i % 2, k * P:(k + 1) * P], core.ident[:])
            x.then_inc(q_tr, 1)

        def multiply(i):
            e.wait_ge(q_ev, i + 1)
            if i >= 2:
                e.wait_ge(o_done, i - 1)
            for k in range(KD):
                x = e.matmul(ps[:, 6 + i % 2, :], qT[:, i % 2, k * P:(k + 1) * P], ternT[:, k, :], start=(k == 0),
                             stop=(k == KD - 1))
            x.then_inc(o_mm, 1)

        rounds((0, turn), (3, multiply), (1, rotate), (2, turn_back))

    return dict(sp=sp, dve=dve, act=act, pe=pe, pool=pool, cx=cx, used=used)


AT_RMS_EPS = 1.1920929e-07
AT_LN_EPS = 1e-5
AT_HN = 4
AT_HW = DI // AT_HN
AT_DPROJ = 2 * DI + AT_HN + 2 * AT_HN * NS
AT_CX, AT_CDT, AT_CBC = DI, 2 * DI, 2 * DI + AT_HN
AT_PIECES = 6


def stage_l3(core, ps):
    nc, ins, t = core.nc, core.ins, core.t
    cx = ExitStack()
    sb = lambda n, s, d=F32: core.sb("ab_" + n, s, d, cx)
    used = []
    sem = lambda n: core.stage_sem("a_" + n, cx, used)
    wi_hi, wi_lo = sb("wi_hi", [P, KD, AT_DPROJ], F16), sb("wi_lo", [P, KD, AT_DPROJ], F16)
    wo_hi, wo_lo = sb("wo_hi", [P, JD, D], F16), sb("wo_lo", [P, JD, D], F16)
    raw = [sb(f"raw{b}", [P, AT_DPROJ]) for b in range(2)]
    nw = sb("nw", [P, KD])
    inb, outb = sb("inb", [P, AT_DPROJ]), sb("outb", [P, D])
    alog, dpar, dtb = sb("alog", [P, AT_HN]), sb("dpar", [P, AT_HN]), sb("dtb", [P, AT_HN])
    nega, dtbb = sb("nega", [P, AT_HN]), sb("dtbb", [P, AT_HN])
    stats, mv = sb("stats", [P, TT, 6]), sb("mv", [P, TT, 2])
    rstd, v2, r2 = sb("rstd", [P, TT]), sb("v2", [P, TT]), sb("r2", [P, TT])
    un = sb("un", [P, 2, D])
    u_hi, u_lo = sb("u_hi", [P, KD, TOK], F16), sb("u_lo", [P, KD, TOK], F16)
    small = lambda n, d=F32: sb(n, [P, TT, AT_HN], d)
    dtx, dtn, dtl, dt, la, dend, ecum, edec, dte = (small(n) for n in "dtx dtn dtl dt la dend ecum edec dte".split())
    la_hi, la_lo = small("la_hi", F16), small("la_lo", F16)
    bc = sb("bc", [P, 2 * AT_HN * NS])
    bct = sb("bct", [NS, 2 * AT_HN, P])
    r_hi, r_lo = sb("r_hi", [P, AT_HN, P], F16), sb("r_lo", [P, AT_HN, P], F16)
    E, gm, M = sb("E", [P, AT_HN, P]), sb("gm", [P, AT_HN, P]), sb("M", [P, AT_HN, P])
    xs, xdt, xe, dx = (sb(n, [P, DI]) for n in ("xs", "xdt", "xe", "dx"))
    zt, th, sz, y1, y = (sb(n, [P, DI]) for n in ("zt", "th", "sz", "y1", "y"))
    S = sb("S", [NS, DI])
    yT_hi, yT_lo = sb("yT_hi", [P, DI], F16), sb("yT_lo", [P, DI], F16)

    dve_own, act_own = sem("dve_own"), sem("act_own")
    par_in = sem("par_in")
    raw_in = [sem(f"raw_in{b}") for b in range(2)]
    names = """w_hi w_lo var_done sd_done un_done turned hi_done lo_done dt_mm dtn_done dt_log nega_done la_done sums_mm
        sums_exp prep bias_added zeroed bc_mm x_mm z_mm bc_done x_done z_ev thz_done sz_done bct_mm bct_done g_mm
        r_done diff gm_done exped m_done inter_mm y1_done smul ds_mm s_done intra_mm xdt_done xe_done dx_done y2_done
        y3_done y_done yt_mm yhi_done ylo_done out_mm t_done""".split()
    s = {n: sem(n) for n in names}
    (w_hi, w_lo, var_done, sd_done, un_done, turned, hi_done, lo_done, dt_mm, dtn_done, dt_log, nega_done, la_done,
     sums_mm, sums_exp, prep, bias_added, zeroed, bc_mm, x_mm, z_mm, bc_done, x_done, z_ev, thz_done, sz_done, bct_mm,
     bct_done, g_mm, r_done, diff, gm_done, exped, m_done, inter_mm, y1_done, smul, ds_mm, s_done, intra_mm, xdt_done,
     xe_done, dx_done, y2_done, y3_done, y_done, yt_mm, yhi_done, ylo_done, out_mm, t_done) = (s[n] for n in names)

    def chunks(e, body):
        body(0, True, False)
        with e.Fori(1, TT - 1) as i:
            body(i, False, False)
        body(TT - 1, False, True)

    def two(a, b):
        return ps[:, a:b, :].rearrange("p b n -> p (b n)")

    def per_head(x, i):
        return x[:, i, :].unsqueeze(2).to_broadcast([P, AT_HN, AT_HW])

    def hv(x):
        return x.rearrange("p (h q) -> p h q", h=AT_HN)

    PARS = ("a_nw", "a_in_b", "a_out_b", "a_alog", "a_D", "a_dtb")

    def sp(e):
        for dst, name in zip((nw, inb, outb, alog, dpar, dtb), PARS):
            src = ins[name]
            if name != "a_nw":
                src = src.partition_broadcast(P)
            e.dma_start(dst[:], src).then_inc(par_in, 16)
        for n in range(AT_PIECES):
            if n >= 2:
                e.wait_ge(w_hi, n - 1)
                e.wait_ge(w_lo, n - 1)
            if n < KD:
                e.dma_start(raw[n % 2][:], ins["a_in_w"][n * P:(n + 1) * P, :]).then_inc(raw_in[n % 2], 16)
            else:
                e.dma_start(raw[n % 2][:, 0:4 * D].rearrange("p (j f) -> p j f", j=4),
                            ins["a_out_w"][(n - KD) * 512:(n - KD + 1) * 512, :].rearrange("(j p) f -> p j f", p=P))\
                    .then_inc(raw_in[n % 2], 16)

    PAR = 16 * len(PARS)

    def dve(e):
        own = Chain(e, dve_own)
        with e.Fori(0, TT) as i:
            e.bn_stats(stats[:, i, :], t[:, i, :]).then_inc(dve_own, 1)
        own.n = TT
        e.wait_ge(dve_own, TT)
        for i in range(TT):
            x = e.bn_aggr(mv[:, i, :], stats[:, i, :])
        own(x)
        e.tensor_scalar(rstd[:], mv[:, :, 1], AT_LN_EPS, None, ALU.add).then_inc(var_done, 1)
        e.wait_ge(sd_done, 1)
        own(e.reciprocal(rstd[:], rstd[:]))
        own(e.tensor_tensor(v2[:], rstd[:], rstd[:], ALU.mult))
        own(e.tensor_tensor(v2[:], v2[:], mv[:, :, 1], ALU.mult))
        e.tensor_scalar(r2[:], v2[:], AT_RMS_EPS, None, ALU.add).then_inc(var_done, 1)
        e.wait_ge(sd_done, 2)
        own(e.reciprocal(r2[:], r2[:]))
        own(e.tensor_tensor(rstd[:], rstd[:], r2[:], ALU.mult))
        for i in range(TT):
            if i >= 2:
                e.wait_ge(turned, i - 1)
            e.tensor_scalar(un[:, i % 2, :], t[:, i, :], mv[:, i, 0:1], rstd[:, i:i + 1], ALU.subtract, ALU.mult)\
                .then_inc(un_done, 1)
            if i >= 1:
                low_part(e, i - 1)
        low_part(e, TT - 1)
        for n in range(AT_PIECES):
            e.wait_ge(w_hi, n + 1)
            if n < KD:
                e.scalar_tensor_tensor(out=wi_lo[:, n, :], in0=raw[n % 2][:], scalar=nw[:, n:n + 1], in1=wi_hi[:, n, :],
                                       op0=ALU.mult, op1=ALU.subtract).then_inc(w_lo, 1)
            else:
                j = 4 * (n - KD)
                e.tensor_tensor(wo_lo[:, j:j + 4, :], raw[n % 2][:, 0:4 * D].rearrange("p (j f) -> p j f", j=4),
                                wo_hi[:, j:j + 4, :], ALU.subtract).then_inc(w_lo, 1)
        e.wait_ge(dt_mm, 1)
        own(e.tensor_tensor(dtbb[:], dtb[:], inb[:, AT_CDT:AT_CDT + AT_HN], ALU.add))
        own(e.tensor_tensor(dtx[:], ps[:, 6, 0:TT * AT_HN].rearrange("p (i h) -> p i h", i=TT),
                            dtbb[:].unsqueeze(1).to_broadcast([P, TT, AT_HN]), ALU.add))
        e.scalar_tensor_tensor(out=dtn[:], in0=dtx[:], scalar=-1.0, in1=dtx[:], op0=ALU.mult, op1=ALU.min)\
            .then_inc(dtn_done, 1)
        e.wait_ge(dt_log, 1)
        own(e.scalar_tensor_tensor(out=dt[:], in0=dtx[:], scalar=0.0, in1=dtl[:], op0=ALU.max, op1=ALU.add))
        e.wait_ge(nega_done, 1)
        e.tensor_tensor(la[:], dt[:], nega[:].unsqueeze(1).to_broadcast([P, TT, AT_HN]), ALU.mult).then_inc(la_done, 1)
        e.wait_ge(la_done, 1)
        own(e.tensor_copy(la_hi[:], la[:]))
        own(e.tensor_tensor(la_lo[:], la[:], la_hi[:], ALU.subtract))
        e.wait_ge(sums_exp, 1)
        e.tensor_tensor(dte[:], dend[:], dt[:], ALU.mult).then_inc(prep, 1)
        e.wait_ge(prep, 1)

        def take_bc(g):
            e.wait_ge(bc_mm, g + 1)
            e.tensor_tensor(bc[:], ps[:, 1, 0:2 * AT_HN * NS], inb[:, AT_CBC:AT_DPROJ], ALU.add).then_inc(bc_done, 1)

        def take_z(g):
            e.wait_ge(z_mm, g + 1)
            e.tensor_tensor(zt[:], two(4, 6), inb[:, 0:DI], ALU.add).then_inc(z_ev, 1)

        def gate(g):
            e.wait_ge(thz_done, g + 1)
            e.scalar_tensor_tensor(out=sz[:], in0=th[:], scalar=1.0, in1=zt[:], op0=ALU.add, op1=ALU.mult)\
                .then_inc(sz_done, 1)

        def take_x(i, g):
            e.wait_ge(x_mm, g + 1)
            e.tensor_tensor(xs[:], two(2, 4), inb[:, AT_CX:AT_CX + DI], ALU.add).then_inc(x_done, 1)
            e.wait_ge(x_done, g + 1)
            e.tensor_tensor(hv(xdt[:]), hv(xs[:]), per_head(dt, i), ALU.mult).then_inc(xdt_done, 1)

        def decays(i):
            for r, l in ((r_hi, la_hi), (r_lo, la_lo)):
                x = e.tensor_tensor(r[:], l[:, i, :].unsqueeze(2).to_broadcast([P, AT_HN, P]),
                                    core.tri16[:].unsqueeze(1).to_broadcast([P, AT_HN, P]), ALU.mult)
            x.then_inc(r_done, 1)

        take_bc(0)
        take_z(0)
        gate(0)
        take_x(0, 0)
        decays(0)

        def body(i, first, last):
            g = i
            e.wait_ge(g_mm, g + 1)
            e.tensor_tensor(gm[:], ps[:, 6, :].rearrange("p (h t) -> p h t", h=AT_HN),
                            core.tri[:].unsqueeze(1).to_broadcast([P, AT_HN, P]), ALU.mult).then_inc(gm_done, 1)
            e.wait_ge(gm_done, g + 1)
            e.wait_ge(exped, g + 1)
            e.tensor_tensor(M[:], E[:], gm[:], ALU.mult).then_inc(m_done, 1)
            e.wait_ge(inter_mm, g + 1)
            e.tensor_tensor(hv(y1[:]), hv(two(4, 6)), per_head(ecum, i), ALU.mult).then_inc(y1_done, 1)
            e.wait_ge(ds_mm, g + 1)
            e.wait_ge(smul, g + 1)
            e.tensor_tensor(S[:], S[:], ps[0:NS, 6:8, :].rearrange("p b n -> p (b n)"), ALU.add).then_inc(s_done, 1)
            if not last:
                take_bc(g + 1)
            e.wait_ge(intra_mm, g + 1)
            e.wait_ge(y1_done, g + 1)
            e.tensor_tensor(y1[:], y1[:], two(2, 4), ALU.add).then_inc(y2_done, 1)
            e.wait_ge(y3_done, g + 1)
            e.tensor_tensor(y[:], y1[:], sz[:], ALU.mult).then_inc(y_done, 1)
            if not last:
                e.wait_ge(y_done, g + 1)
                take_z(g + 1)
                gate(g + 1)
            e.wait_ge(yhi_done, g + 1)
            e.tensor_tensor(yT_lo[:], two(2, 4), yT_hi[:], ALU.subtract).then_inc(ylo_done, 1)
            if not last:
                e.wait_ge(diff, g + 1)
                decays(i + 1)
                e.wait_ge(dx_done, g + 1)
                e.wait_ge(xe_done, g + 1)
                take_x(i + 1, g + 1)
            e.wait_ge(out_mm, g + 1)
            e.scalar_tensor_tensor(out=t[:, i, :], in0=ps[:, 0, :], scalar=0.5, in1=t[:, i, :], op0=ALU.mult,
                                   op1=ALU.add).then_inc(t_done, 1)

        e.wait_ge(bias_added, 1)
        chunks(e, body)

    def low_part(e, i):
        e.wait_ge(hi_done, i + 1)
        e.tensor_tensor(u_lo[:, :, i * P:(i + 1) * P], ps[:, i % 4, :].rearrange("p (k c) -> p k c", k=KD),
                        u_hi[:, :, i * P:(i + 1) * P], ALU.subtract).then_inc(lo_done, 1)

    def act(e):
        own = Chain(e, act_own)
        e.wait_ge(var_done, 1)
        e.activation(rstd[:], rstd[:], ACT.Sqrt).then_inc(sd_done, 1)
        e.wait_ge(var_done, 2)
        e.activation(r2[:], r2[:], ACT.Sqrt).then_inc(sd_done, 1)
        for i in range(TT):
            e.wait_ge(turned, i + 1)
            e.activation(u_hi[:, :, i * P:(i + 1) * P], ps[:, i % 4, :].rearrange("p (k c) -> p k c", k=KD), ACT.Copy)\
                .then_inc(hi_done, 1)
        e.wait_ge(par_in, PAR)
        for n in range(AT_PIECES):
            e.wait_ge(raw_in[n % 2], (n // 2 + 1) * 16)
            if n < KD:
                e.activation(wi_hi[:, n, :], raw[n % 2][:], ACT.Copy, scale=nw[:, n:n + 1]).then_inc(w_hi, 1)
            else:
                j = 4 * (n - KD)
                e.activation(wo_hi[:, j:j + 4, :], raw[n % 2][:, 0:4 * D].rearrange("p (j f) -> p j f", j=4), ACT.Copy)\
                    .then_inc(w_hi, 1)
        own(e.activation(nega[:], alog[:], ACT.Exp))
        e.mul(nega[:], nega[:], -1.0).then_inc(nega_done, 1)
        e.wait_ge(dtn_done, 1)
        own(e.activation(dtl[:], dtn[:], ACT.Exp))
        e.activation(dtl[:], dtl[:], ACT.Ln, bias=1.0).then_inc(dt_log, 1)
        e.wait_ge(sums_mm, 1)
        for n, d in enumerate((dend, ecum, edec)):
            x = e.activation(d[:], ps[:, 7, 32 * n:32 * n + 32].rearrange("p (i h) -> p i h", i=TT), ACT.Exp)
        x.then_inc(sums_exp, 1)

        def tanh_z(g):
            e.wait_ge(z_ev, g + 1)
            e.activation(th[:], zt[:], ACT.Tanh, scale=0.5).then_inc(thz_done, 1)

        tanh_z(0)

        def body(i, first, last):
            g = i
            e.wait_ge(bct_mm, g + 1)
            e.activation(bct[:], ps[0:NS, 6:8, :].rearrange("p b (c t) -> p (b c) t", t=P), ACT.Copy).then_inc(bct_done, 1)
            e.wait_ge(diff, g + 1)
            e.activation(E[:], ps[:, 7, :].rearrange("p (h t) -> p h t", h=AT_HN), ACT.Exp).then_inc(exped, 1)
            if not last:
                tanh_z(g + 1)
            e.wait_ge(yt_mm, g + 1)
            e.activation(yT_hi[:], two(2, 4), ACT.Copy).then_inc(yhi_done, 1)

        chunks(e, body)

    def pool(e):
        e.memset(S[:], 0.0).then_inc(zeroed, 1)
        e.wait_ge(zeroed, 1)
        e.wait_ge(un_done, TT)
        e.wait_ge(par_in, PAR)
        e.tensor_tensor(t[:], t[:], outb[:].unsqueeze(1).to_broadcast([P, TT, D]), ALU.add).then_inc(bias_added, 1)
        e.wait_ge(prep, 1)

        def body(i, first, last):
            g = i
            e.wait_ge(x_done, g + 1)
            e.tensor_tensor(hv(xe[:]), hv(xs[:]), per_head(dte, i), ALU.mult).then_inc(xe_done, 1)
            e.tensor_tensor(hv(dx[:]), hv(xs[:]), dpar[:].unsqueeze(2).to_broadcast([P, AT_HN, AT_HW]), ALU.mult)\
                .then_inc(dx_done, 1)
            if not first:
                e.wait_ge(s_done, g)
            e.wait_ge(inter_mm, g + 1)
            e.tensor_tensor(hv(S[:]), hv(S[:]), edec[0:NS, i, :].unsqueeze(2).to_broadcast([NS, AT_HN, AT_HW]), ALU.mult)\
                .then_inc(smul, 1)
            e.wait_ge(y2_done, g + 1)
            e.wait_ge(dx_done, g + 1)
            e.tensor_tensor(y1[:], y1[:], dx[:], ALU.add).then_inc(y3_done, 1)

        chunks(e, body)

    def pe(e):
        for i in range(TT):
            e.wait_ge(un_done, i + 1)
            if i >= 4:
                e.wait_ge(lo_done, i - 3)
            for k in range(KD):
                x = e.transpose(ps[:, i % 4, k * P:(k + 1) * P], un[:, i % 2, k * P:(k + 1) * P], core.ident[:])
            x.then_inc(turned, 1)
        e.wait_ge(w_lo, KD)
        e.wait_ge(lo_done, TT)
        for i in range(TT):
            for k in range(KD):
                for m, (a, b) in enumerate(((u_hi, wi_hi), (u_hi, wi_lo), (u_lo, wi_hi))):
                    x = e.matmul(ps[:, 6, i * AT_HN:(i + 1) * AT_HN], a[:, k, i * P:(i + 1) * P], b[:, k, AT_CDT:AT_CDT + AT_HN],
                                 start=(k == 0 and m == 0), stop=(k == KD - 1 and m == 2))
        x.then_inc(dt_mm, 1)
        e.wait_ge(la_done, 1)
        la2 = la[:].rearrange("p i h -> p (i h)")
        for n, w in enumerate((core.after, core.tri, core.ones)):
            x = e.matmul(ps[:, 7, 32 * n:32 * n + 32], w[:], la2, start=True, stop=True)
        x.then_inc(sums_mm, 1)

        def project(i, out, col, width):
            for k in range(KD):
                for m, (a, b) in enumerate(((u_hi, wi_hi), (u_hi, wi_lo), (u_lo, wi_hi))):
                    x = e.matmul(out, a[:, k, ds(i * P, P)], b[:, k, col:col + width],
                                 start=(k == 0 and m == 0), stop=(k == KD - 1 and m == 2))
            return x

        def project_bc(i):
            project(i, ps[:, 1, 0:2 * AT_HN * NS], AT_CBC, 2 * AT_HN * NS).then_inc(bc_mm, 1)

        def project_z(i):
            project(i, ps[:, 4, :], 0, 512)
            project(i, ps[:, 5, :], 512, 512).then_inc(z_mm, 1)

        def project_x(i):
            project(i, ps[:, 2, :], AT_CX, 512)
            project(i, ps[:, 3, :], AT_CX + 512, 512).then_inc(x_mm, 1)

        project_bc(0)
        project_z(0)
        project_x(0)

        def body(i, first, last):
            g = i
            e.wait_ge(bc_done, g + 1)
            if first:
                e.wait_ge(sums_exp, 1)
                e.wait_ge(zeroed, 1)
            else:
                e.wait_ge(s_done, g)
            for c in range(2 * AT_HN):
                x = e.transpose(ps[0:NS, 6 + c // 4, (c % 4) * P:(c % 4 + 1) * P], bc[:, c * NS:(c + 1) * NS], core.ident[:])
            x.then_inc(bct_mm, 1)
            e.wait_ge(r_done, g + 1)
            e.wait_ge(bct_done, g + 1)
            for m, r in enumerate((r_hi, r_lo)):
                x = e.matmul(ps[:, 7, :], core.after16[:], r[:].rearrange("p h t -> p (h t)"), start=(m == 0), stop=(m == 1))
            x.then_inc(diff, 1)
            for h in range(AT_HN):
                x = e.matmul(ps[:, 6, h * P:(h + 1) * P], bct[:, 2 * h, :], bct[:, 2 * h + 1, :], start=True, stop=True)
            x.then_inc(g_mm, 1)
            e.wait_ge(z_ev, g + 1)
            for h in range(AT_HN):
                x = e.matmul(ps[:, 4 + h // 2, (h % 2) * AT_HW:(h % 2 + 1) * AT_HW], bct[:, 2 * h + 1, :], S[:, h * AT_HW:(h + 1) * AT_HW],
                             start=True, stop=True)
            x.then_inc(inter_mm, 1)
            e.wait_ge(xdt_done, g + 1)
            e.wait_ge(m_done, g + 1)
            for h in range(AT_HN):
                x = e.matmul(ps[:, 2 + h // 2, (h % 2) * AT_HW:(h % 2 + 1) * AT_HW], M[:, h, :], xdt[:, h * AT_HW:(h + 1) * AT_HW],
                             start=True, stop=True)
            x.then_inc(intra_mm, 1)
            e.wait_ge(xe_done, g + 1)
            for h in range(AT_HN):
                x = e.matmul(ps[0:NS, 6 + h // 2, (h % 2) * AT_HW:(h % 2 + 1) * AT_HW], bc[:, 2 * h * NS:(2 * h + 1) * NS],
                             xe[:, h * AT_HW:(h + 1) * AT_HW], start=True, stop=True)
            x.then_inc(ds_mm, 1)
            if not last:
                project_bc(i + 1)
                e.wait_ge(y1_done, g + 1)
                project_z(i + 1)
            e.wait_ge(y_done, g + 1)
            core.apart(e)
            for j in range(JD):
                x = e.transpose(ps[:, 2 + j // 4, (j % 4) * P:(j % 4 + 1) * P], y[:, j * P:(j + 1) * P], core.ident[:])
            x.then_inc(yt_mm, 1)
            e.wait_ge(ylo_done, g + 1)
            if not first:
                e.wait_ge(t_done, g)
            for j in range(JD):
                for m, (a, b) in enumerate(((yT_hi, wo_hi), (yT_hi, wo_lo), (yT_lo, wo_hi))):
                    x = e.matmul(ps[:, 0, :], a[:, j * P:(j + 1) * P], b[:, j, :], start=(j == 0 and m == 0),
                                 stop=(j == JD - 1 and m == 2))
            x.then_inc(out_mm, 1)
            if not last:
                project_x(i + 1)

        chunks(e, body)

    return dict(sp=sp, dve=dve, act=act, pe=pe, pool=pool, cx=cx, used=used)


EX_F = 2048
EX_FB = EX_F // P
EX_GB = 4
EX_FG = EX_FB // EX_GB
EX_PIECES = 8
EX_MAGIC = 1.5 * 2.0 ** 23
EX_LN_EPS = 1e-5
EX_RAWS = 4


def stage_moe(core, ps):
    nc, ins, t = core.nc, core.ins, core.t
    cx = ExitStack()
    sb = lambda n, s, d=F32: core.sb("eb_" + n, s, d, cx)
    used = []
    sem = lambda n: core.stage_sem("e_" + n, cx, used)
    w_hi = [sb(f"w_hi{b}", [P, EX_PIECES, EX_F], F16) for b in range(2)]
    w_lo = [sb(f"w_lo{b}", [P, EX_PIECES, EX_F], F16) for b in range(2)]
    un = sb("un", [P, TT, D])
    room = un[:].rearrange("p i f -> p (i f)")
    raw = [sb(f"raw{b}", [P, EX_F])[:] for b in range(2)] + [room[:, b * EX_F:(b + 1) * EX_F] for b in range(2)]
    gw = sb("gw", [P, KD, E])
    b1, b2 = sb("b1", [P, E, EX_FB]), sb("b2", [E, D])
    iota = sb("iota", [P, E])
    stats, mv, rstd = sb("stats", [P, TT, 6]), sb("mv", [P, TT, 2]), sb("rstd", [P, TT])
    lg, pr, top, pos, pk = (sb(n, [P, TT, E]) for n in ("lg", "pr", "top", "pos", "pk"))
    pick = [sb(f"pick{k}", [P, TT, E]) for k in range(TOPK)]
    mask, tot = sb("mask", [P, TT, E]), sb("tot", [P, TT, E])
    topi, topf = sb("topi", [P, TT, E], U32), sb("topf", [P, TT, E])
    red, inv = sb("red", [P, TT]), sb("inv", [P, TT])
    before = sb("before", [P, TT + 1, E])
    nb, cum, first, first_slot = (sb(n, [P, E]) for n in ("nb", "cum", "first", "first_slot"))
    plan = sb("plan", [P, 2 * E + 1], U32)
    slotf, slot = sb("slotf", [P, TOPK, TT]), sb("slot", [P, TOPK, TT], U32)
    xg, x_hi, x_lo = sb("xg", [P, D]), sb("x_hi", [P, KD, P], F16), sb("x_lo", [P, KD, P], F16)
    hb = sb("hb", [P, 2, EX_GB * P])
    h_hi, h_lo = sb("h_hi", [P, EX_FG, EX_GB * P], F16), sb("h_lo", [P, EX_FG, EX_GB * P], F16)
    y = sb("y", [P, D])
    xs_dram, ys_dram = core.xs_dram, core.ys_dram

    names = """par_in var_done sd_done un_done turned0 copied0 logits max_done exp_done mask_done ranks table_done
         scattered xg_in turned xhi_done xlo_done whi_done wlo_done h_mm h_taken silu_done hhi_done
        hlo_done y_mm y_ev y_out expert_done t_done y_sent mix_done mix_turned mix_ev b2_mm b2_done dve_own act_own""".split()
    s_ = {n: sem(n) for n in names}
    (par_in, var_done, sd_done, un_done, turned0, copied0, logits, max_done, exp_done, mask_done, ranks, table_done,
     scattered, xg_in, turned, xhi_done, xlo_done, whi_done, wlo_done, h_mm, h_taken, silu_done,
     hhi_done, hlo_done, y_mm, y_ev, y_out, expert_done, t_done, y_sent, mix_done, mix_turned, mix_ev, b2_mm, b2_done, dve_own, act_own) = \
        (s_[n] for n in names)
    raw_in = [sem(f"raw_in{b}") for b in range(EX_RAWS)]
    back = [sem(f"back{b}") for b in range(TT)]

    PARS = ((gw, "e_gw"), (b1, "e_b1"), (b2, "e_b2"), (iota, "c_iota"))
    PAR = 16 * len(PARS)
    H_TAKEN0, HLO0, YMM0, YEV0, YSENT0, EXPERT0 = EX_FG, 2, 1, 1, 1, 1

    def experts(e, piece, block, end):
        def body(x, side, last):
            count = e.value_load(plan[0:1, ds(x, 1)], min_val=0, max_val=BLOCKS)
            start = e.value_load(plan[0:1, ds(x + E, 1)], min_val=0, max_val=FILLED - 2)
            with e.Fori(0, EX_PIECES // EX_RAWS) as i:
                for q in range(2):
                    if piece and not last:
                        for n in (2 * q, 2 * q + 1):
                            piece(x + 1, 1 - side, i * EX_RAWS + n, n, x * (EX_PIECES // EX_RAWS) + i)
                    with e.If(i * 2 + q < count):
                        block(x, side, start + (i * 2 + q))
            with e.Fori(EX_PIECES // 2, BLOCKS) as b:
                with e.If(b < count):
                    block(x, side, start + b)
            if end:
                end(x)

        with e.Fori(0, E // 2 - 1) as i:
            body(i * 2, 0, False)
            body(i * 2 + 1, 1, False)
        body(E - 2, 0, False)
        body(E - 1, 1, True)

    def sp(e):
        for dst, name in PARS:
            e.dma_start(dst[:], ins[name]).then_inc(par_in, 16)

        def load(m, q):
            e.dma_start(raw[q], ins["e_w"][ds(m * P, P), :]).then_inc(raw_in[q], 16)

        for m in range(EX_PIECES):
            if m >= 2:
                e.wait_ge(wlo_done, m - 1)
            load(m, m % 2)
        e.wait_ge(scattered, 16 * TT * TOPK)
        for q in range(EX_RAWS):
            if q < 2:
                e.wait_ge(wlo_done, EX_PIECES - 1 + q)
            load(EX_PIECES + q, q)
        with e.Fori(EX_PIECES // EX_RAWS + 1, E * EX_PIECES // EX_RAWS) as i:
            for q in range(EX_RAWS):
                e.wait_ge(wlo_done, i * EX_RAWS + (q - EX_RAWS + 1))
                load(i * EX_RAWS + q, q)

    def dve(e):
        own = Chain(e, dve_own)
        e.sem_inc(h_taken, H_TAKEN0)
        e.sem_inc(hlo_done, HLO0)
        e.sem_inc(y_ev, YEV0)
        for i in range(TT):
            x = e.bn_stats(stats[:, i, :], t[:, i, :])
        own(x)
        for i in range(TT):
            x = e.bn_aggr(mv[:, i, :], stats[:, i, :])
        own(x)
        e.tensor_scalar(rstd[:], mv[:, :, 1], EX_LN_EPS, None, ALU.add).then_inc(var_done, 1)
        e.wait_ge(sd_done, 1)
        own(e.reciprocal(rstd[:], rstd[:]))
        for i in range(TT):
            e.tensor_scalar(un[:, i, :], t[:, i, :], mv[:, i, 0:1], rstd[:, i:i + 1], ALU.subtract, ALU.mult)\
                .then_inc(un_done, 1)
        for n in range(EX_PIECES // 2):
            lower(e, 0, 0, n, n % 2)
        wide = lambda x: x.unsqueeze(2).to_broadcast([P, TT, E])
        e.wait_ge(logits, 1)
        own(e.tensor_copy(lg[:], ps[:, 7, 0:TT * E].rearrange("p (i x) -> p i x", i=TT)))
        own(e.tensor_reduce(red[:], lg[:], AX.X, ALU.max))
        e.tensor_tensor(lg[:], lg[:], wide(red[:]), ALU.subtract).then_inc(max_done, 1)
        e.wait_ge(exp_done, 1)
        own(e.tensor_reduce(inv[:], pr[:], AX.X, ALU.add))
        own(e.reciprocal(inv[:], inv[:]))
        own(e.tensor_tensor(pr[:], pr[:], wide(inv[:]), ALU.mult))
        for i in range(TT):
            x = e.max(top[:, i, :], pr[:, i, :])
        own(x)
        for i in range(TT):
            x = e.max_index(topi[:, i, :], top[:, i, :], pr[:, i, :])
        own(x)
        own(e.tensor_copy(topf[:], topi[:]))
        e.wait_ge(par_in, PAR)
        for k in range(TOPK):
            x = e.tensor_tensor(pick[k][:], iota[:].unsqueeze(1).to_broadcast([P, TT, E]), wide(topf[:, :, k]), ALU.is_equal)
        own(x)
        e.tensor_tensor(mask[:], pick[0][:], pick[1][:], ALU.add).then_inc(mask_done, 1)
        own(e.memset(before[:, 0, :], 0.0))
        e.wait_ge(ranks, 1)
        own(e.tensor_copy(tot[:], ps[:, 6, 0:TT * E].rearrange("p (i x) -> p i x", i=TT)))
        for i in range(TT):
            own(e.tensor_tensor(before[:, i + 1, :], before[:, i, :], tot[:, i, :], ALU.add))
        own(e.tensor_scalar(nb[:], before[:, TT, :], 1.0 / P, 0.5 - 0.5 / P, ALU.mult, ALU.add))
        own(e.tensor_scalar(nb[:], nb[:], EX_MAGIC, None, ALU.add))
        own(e.tensor_scalar(nb[:], nb[:], EX_MAGIC, None, ALU.subtract))
        own(e.tensor_tensor_scan(cum[:], core.ones[:, 0:E], nb[:], 0.0, ALU.mult, ALU.add))
        own(e.tensor_tensor(first[:], cum[:], nb[:], ALU.subtract))
        e.tensor_copy(plan[:, 0:E], nb[:])
        e.tensor_copy(plan[:, E:2 * E], first[:])
        own(e.tensor_copy(plan[:, 2 * E:], cum[:, E - 1:E]))
        own(e.tensor_scalar(first_slot[:], first[:], float(P), None, ALU.mult))
        own(e.tensor_tensor(pos[:], ps[:, 7, TT * E:2 * TT * E].rearrange("p (i x) -> p i x", i=TT), mask[:], ALU.subtract))
        own(e.tensor_tensor(pos[:], pos[:], before[:, 0:TT, :], ALU.add))
        own(e.tensor_tensor(pos[:], pos[:], first_slot[:].unsqueeze(1).to_broadcast([P, TT, E]), ALU.add))
        for k in range(TOPK):
            own(e.tensor_tensor(pk[:], pick[k][:], pos[:], ALU.mult))
            own(e.tensor_reduce(slotf[:, k, :], pk[:], AX.X, ALU.add))
        e.tensor_copy(slot[:], slotf[:]).then_inc(table_done, 1)
        e.wait_ge(table_done, 1)
        for n in range(EX_PIECES // 2, EX_PIECES):
            lower(e, 0, 0, n, n % 2)
        lower_x(e, 0)

        def bias(x, s, j):
            e.wait_ge(h_mm, s * EX_FG + (j + 1))
            e.wait_ge(hlo_done, s * EX_FG + (j + 1))
            e.tensor_tensor(hb[:, j % 2, :].rearrange("p (c n) -> p c n", c=EX_GB),
                            ps[:, j, :].rearrange("p (c n) -> p c n", c=EX_GB),
                            b1[:, ds(x, 1), j * EX_GB:(j + 1) * EX_GB].rearrange("p o c -> p (o c)").unsqueeze(2)
                            .to_broadcast([P, EX_GB, P]), ALU.add).then_inc(h_taken, 1)

        def low(s, j):
            e.wait_ge(hhi_done, s * EX_FG + (j + 1))
            e.tensor_tensor(h_lo[:, j, :], hb[:, j % 2, :], h_hi[:, j, :], ALU.subtract).then_inc(hlo_done, 1)

        def block(x, side, s):
            for j in range(EX_FG):
                bias(x, s, j)
                if j:
                    low(s, j - 1)
            low(s, EX_FG - 1)
            lower_x(e, s + 1)
            e.wait_ge(y_mm, s + 1 + YMM0)
            e.wait_ge(y_sent, s + YSENT0)
            core.apart(e)
            e.tensor_copy(y[:], ps[:, 5, :]).then_inc(y_ev, 1)

        experts(e, lambda x, side, n, q, m: lower(e, x, side, n, q), block, None)
        e.tensor_tensor(pick[0][:], pick[0][:], wide(top[:, :, 0]), ALU.mult)
        own(e.tensor_tensor(pick[1][:], pick[1][:], wide(top[:, :, 1]), ALU.mult))
        e.tensor_tensor(mask[:], pick[0][:], pick[1][:], ALU.add).then_inc(mix_done, 1)
        for i in range(TT):
            e.wait_ge(b2_mm, i + 1)
            e.tensor_tensor(t[:, i, :], t[:, i, :], ps[:, i % 4, :], ALU.add).then_inc(b2_done, 1)
        for n in range(TOPK * TT):
            i, k = n // TOPK, n % TOPK
            e.wait_ge(back[n % TT], 16 * (n // TT + 1))
            if k:
                e.wait_ge(t_done, n)
            else:
                e.wait_ge(b2_done, i + 1)
            e.scalar_tensor_tensor(out=t[:, i, :], in0=un[:, n % TT, :], scalar=top[:, i, k:k + 1], in1=t[:, i, :],
                                   op0=ALU.mult, op1=ALU.add).then_inc(t_done, 1)

    def lower(e, x, side, n, q):
        e.wait_ge(whi_done, x * EX_PIECES + (n + 1))
        e.tensor_tensor(w_lo[side][:, n, :], raw[q], w_hi[side][:, n, :], ALU.subtract).then_inc(wlo_done, 1)

    def upper(e, x, side, n, q, m):
        e.wait_ge(raw_in[q], (m + 1 + (EX_PIECES // 2 if q < 2 else 0)) * 16)
        e.wait_ge(expert_done, x)
        e.copy(w_hi[side][:, n, :], raw[q]).then_inc(whi_done, 1)

    def lower_x(e, s):
        e.wait_ge(xhi_done, s + 1)
        e.tensor_tensor(x_lo[:], ps[:, 4, :].rearrange("p (k n) -> p k n", k=KD), x_hi[:], ALU.subtract)\
            .then_inc(xlo_done, 1)

    def upper_x(e, s):
        e.wait_ge(turned, s + 1)
        e.copy(x_hi[:], ps[:, 4, :].rearrange("p (k n) -> p k n", k=KD)).then_inc(xhi_done, 1)

    def act(e):
        own = Chain(e, act_own)
        e.wait_ge(var_done, 1)
        e.activation(rstd[:], rstd[:], ACT.Sqrt).then_inc(sd_done, 1)
        for i in range(TT):
            e.wait_ge(turned0, i + 1)
            e.copy(hb[:, i % 2, :], ps[:, i % 2, :]).then_inc(copied0, 1)
        for n in range(EX_PIECES):
            if n == EX_PIECES // 2:
                e.wait_ge(max_done, 1)
                e.activation(pr[:], lg[:], ACT.Exp).then_inc(exp_done, 1)
            e.wait_ge(raw_in[n % 2], 16 * (n // 2 + 1))
            e.copy(w_hi[0][:, n, :], raw[n % 2]).then_inc(whi_done, 1)
        upper_x(e, 0)
        e.wait_ge(table_done, 1)

        def block(x, side, s):
            for j in range(EX_FG):
                e.wait_ge(h_taken, s * EX_FG + (j + 1 + H_TAKEN0))
                if j == 0:
                    e.wait_ge(y_mm, s + YMM0)
                e.activation(hb[:, j % 2, :], hb[:, j % 2, :], ACT.Silu).then_inc(silu_done, 1)
                e.wait_ge(silu_done, s * EX_FG + (j + 1))
                e.copy(h_hi[:, j, :], hb[:, j % 2, :]).then_inc(hhi_done, 1)
            upper_x(e, s + 1)

        experts(e, lambda x, side, n, q, m: upper(e, x, side, n, q, m), block, None)
        e.wait_ge(mix_turned, 1)
        e.copy(hb[0:E, :, :], ps[0:E, 6:8, :]).then_inc(mix_ev, 1)

    def pe(e):
        for i in range(TT + 1):
            if i < TT:
                e.wait_ge(un_done, i + 1)
                if i >= 2:
                    e.wait_ge(copied0, i - 1)
                for k in range(KD):
                    x = e.transpose(ps[:, i % 2, k * P:(k + 1) * P], un[:, i, k * P:(k + 1) * P], core.ident[:])
                x.then_inc(turned0, 1)
            if i == 1:
                e.wait_ge(par_in, PAR)
            if i >= 1:
                e.wait_ge(copied0, i)
                for k in range(KD):
                    x = e.matmul(ps[:, 7, (i - 1) * E:i * E], hb[:, (i - 1) % 2, k * P:(k + 1) * P], gw[:, k, :],
                                 start=(k == 0), stop=(k == KD - 1))
        x.then_inc(logits, 1)
        e.wait_ge(mask_done, 1)
        m2 = mask[:].rearrange("p i x -> p (i x)")
        e.matmul(ps[:, 7, TT * E:2 * TT * E], core.tri[:], m2, start=True, stop=True)
        e.matmul(ps[:, 6, 0:TT * E], core.ones[:], m2, start=True, stop=True).then_inc(ranks, 1)
        e.sem_inc(y_mm, YMM0)
        e.sem_inc(expert_done, EXPERT0)

        def turn(s):
            e.wait_ge(xg_in, s * 16 + 16)
            core.apart(e)
            for k in range(KD):
                x = e.transpose(ps[:, 4, k * P:(k + 1) * P], xg[:, k * P:(k + 1) * P], core.ident[:])
            x.then_inc(turned, 1)

        turn(0)
        e.wait_ge(table_done, 1)

        def block(x, side, s):
            e.wait_ge(wlo_done, x * EX_PIECES + KD)
            e.wait_ge(xlo_done, s + 1)
            for j in range(EX_FG):
                e.wait_ge(h_taken, s * EX_FG + (j + 1))
                for c in range(EX_GB):
                    f = j * EX_GB + c
                    for k in range(KD):
                        for m, (a, b) in enumerate(((w_hi, x_hi), (w_hi, x_lo), (w_lo, x_hi))):
                            o = e.matmul(ps[:, j, c * P:(c + 1) * P], a[side][:, k, f * P:(f + 1) * P], b[:, k, :],
                                         start=(k == 0 and m == 0), stop=(k == KD - 1 and m == 2))
                o.then_inc(h_mm, 1)
            turn(s + 1)
            e.wait_ge(wlo_done, x * EX_PIECES + EX_PIECES)
            for j in range(EX_FG):
                e.wait_ge(hlo_done, s * EX_FG + (j + 1 + HLO0))
                if j == 0:
                    e.wait_ge(y_ev, s + YEV0)
                for c in range(EX_GB):
                    for m, (a, b) in enumerate(((h_hi, w_hi), (h_hi, w_lo), (h_lo, w_hi))):
                        o = e.matmul(ps[:, 5, :], a[:, j, c * P:(c + 1) * P], b[side][:, KD + j, c * D:(c + 1) * D],
                                     start=(j == 0 and c == 0 and m == 0), stop=(j == EX_FG - 1 and c == EX_GB - 1 and m == 2))
            o.then_inc(y_mm, 1)

        experts(e, None, block, lambda x: e.drain().then_inc(expert_done, 1))
        e.wait_ge(mix_done, 1)
        for i in range(TT):
            x = e.transpose(ps[0:E, 6 + i // 4, (i % 4) * P:(i % 4 + 1) * P], mask[:, i, :], core.ident[:])
        x.then_inc(mix_turned, 1)
        e.wait_ge(mix_ev, 1)
        for i in range(TT):
            if i >= 4:
                e.wait_ge(b2_done, i - 3)
            e.matmul(ps[:, i % 4, :], hb[0:E, i // 4, (i % 4) * P:(i % 4 + 1) * P], b2[:], start=True, stop=True)\
                .then_inc(b2_mm, 1)

    def pool(e):
        e.wait_ge(un_done, TT)
        e.wait_ge(table_done, 1)
        for i in range(TT):
            for k in range(TOPK):
                e.indirect_dma_start(out=xs_dram, out_offset=bass.IndirectOffsetOnAxis(ap=slot[:, k, i:i + 1], axis=0),
                                     in_=un[:, i, :], in_offset=None).then_inc(scattered, 16)
        e.wait_ge(scattered, 16 * TT * TOPK)

        def fetch(s):
            e.dma_start(xg[:], xs_dram[ds(s * P, P), :]).then_inc(xg_in, 16)

        fetch(0)
        e.wait_ge(turned, 1)
        fetch(1)
        e.sem_inc(y_sent, YSENT0)

        def block(x, side, s):
            e.wait_ge(turned, s + 2)
            core.apart(e)
            fetch(s + 2)
            e.wait_ge(y_ev, s + 1 + YEV0)
            core.apart(e)
            e.dma_start(ys_dram[ds(s * P, P), :], y[:]).then_inc(y_out, 16)
            e.wait_ge(y_out, s * 16 + 16)
            e.sem_inc(y_sent, 1)

        experts(e, None, block, None)
        total = e.value_load(plan[0:1, 2 * E:2 * E + 1], min_val=TOPK * TT, max_val=FILLED - 2)
        e.wait_ge(y_out, total * 16)
        e.wait_ge(xg_in, total * 16 + 32)
        e.wait_ge(wlo_done, E * EX_PIECES)
        core.apart(e)
        for n in range(TOPK * TT):
            i, k = n // TOPK, n % TOPK
            if n >= TT:
                e.wait_ge(t_done, n - TT + 1)
            e.indirect_dma_start(out=un[:, n % TT, :], out_offset=None, in_=ys_dram[0:(FILLED - 2) * P, :],
                                 in_offset=bass.IndirectOffsetOnAxis(ap=slot[:, k, i:i + 1], axis=0)).then_inc(back[n % TT], 16)

    return dict(sp=sp, dve=dve, act=act, pe=pe, pool=pool, cx=cx, used=used)


ENGINES = 5
OUT_TILES = TT


def program(nc, ins, out):
    with ExitStack() as ctx:
        core = Core(nc, ctx, ins)
        ps = ctx.enter_context(nc.psum_tensor("banks", [P, 8, 512], F32))
        stages = []
        for make in (stage_l01, stage_mamba, stage_ffn, stage_l3, stage_moe):
            stage = make(core, ps)
            stage["cx"].close()
            stages.append(stage)
        out_sent = core.sem("out_sent")

        def open_stage(e, k):
            if k:
                e.wait_ge(core.cleared, k)
            if k == 1:
                e.wait_ge(core.consts_in, core.CONSTS)

        block = ctx.enter_context(nc.Block())

        @block.sync
        def _(sp):
            for k, stage in enumerate(stages):
                open_stage(sp, k)
                stage["sp"](sp)
                sp.sem_inc(core.stage_end, 1)
            sp.wait_ge(core.stage_end, len(stages) * ENGINES)
            sp.dma_start(out.rearrange("(i p) f -> p i f", p=P), core.t[:]).then_inc(out_sent, 16)
            sp.wait_ge(out_sent, 16)

        @block.scalar
        def _(act):
            for k, stage in enumerate(stages):
                open_stage(act, k)
                stage["act"](act)
                act.drain().then_inc(core.stage_end, 1)

        @block.vector
        def _(dve):
            for k, stage in enumerate(stages):
                open_stage(dve, k)
                stage["dve"](dve)
                dve.drain().then_inc(core.stage_end, 1)

        @block.gpsimd
        def _(pool):
            for k, stage in enumerate(stages):
                if k:
                    pool.wait_ge(core.stage_end, k * ENGINES)
                    for number in sorted(s.num for s in stages[k - 1]["used"]):
                        pool.sem_clear(range(number, number + 1))
                    pool.sem_inc(core.cleared, 1)
                open_stage(pool, k)
                if stage["pool"]:
                    stage["pool"](pool)
                pool.drain().then_inc(core.stage_end, 1)

        @block.tensor
        def _(pe):
            for k, stage in enumerate(stages):
                open_stage(pe, k)
                stage["pe"](pe)
                pe.drain().then_inc(core.stage_end, 1)


def shape_constants():
    k = np.arange(P)
    c = {"c_ident": np.eye(P, dtype=np.float32),
         "c_tri": (k[:, None] <= k[None, :]).astype(np.float32),
         "c_after": (k[:, None] > k[None, :]).astype(np.float32)}
    c["c_tri16"] = c["c_tri"].astype(np.float16)
    c["c_after16"] = c["c_after"].astype(np.float16)
    c["c_ones"] = np.ones((P, P), np.float32)
    r, j, p = np.arange(H2)[:, None, None], np.arange(JD)[None, :, None], k[None, None, :]
    c["c_sel"] = (r == 4 * j + p // 32).astype(np.float32)
    c["c_selT"] = (np.arange(H2)[None, None, :] == 4 * j + k[:, None, None] // 32).astype(np.float32)
    per_group = SEQ // GROUPS
    c["c_g16"] = ((k[:, None] // per_group == k[None, :] // per_group) / per_group).astype(np.float32)
    c["c_onesn"] = np.full((P, P), 1 / (per_group * TOK), np.float32)
    signs = np.ones((1, 1))
    while signs.shape[0] < D:
        signs = np.block([[signs, signs], [signs, -signs]])
    c["c_had"] = signs.astype(np.float16)
    c["c_iota"] = np.tile(np.arange(E, dtype=np.float32), (P, 1))
    return c


def laid_out(i):
    x = i["x"].reshape(SEQ, TOK)
    columns = lambda a: a.reshape(LAYERS, -1, P).transpose(0, 2, 1)
    par = np.zeros((LAYERS, P, MB_NPAR), np.float32)
    conv_w, conv_b = i["L2_attn_conv_w"], i["L2_attn_conv_b"]
    par[:, :, MB_LNW:MB_LNW + KD] = columns(i["L2_attn_ln_w"])
    par[:, :, MB_LNB:MB_LNB + KD] = columns(i["L2_attn_ln_b"])
    par[:, :, MB_CVW:MB_CVB] = conv_w[:, :DI].reshape(LAYERS, JD, P, TAPS).transpose(0, 2, 1, 3).reshape(LAYERS, P, -1)
    par[:, :, MB_CVB:MB_BCW] = columns(conv_b[:, :DI])
    par[:, :NS, MB_BCW:MB_BCB] = conv_w[:, DI:].reshape(LAYERS, 2, NS, TAPS).transpose(0, 2, 1, 3).reshape(LAYERS, NS, -1)
    par[:, :NS, MB_BCB:MB_DCOL] = conv_b[:, DI:].reshape(LAYERS, 2, NS).transpose(0, 2, 1)
    par[:, :, MB_DCOL:MB_RMSW] = columns(np.repeat(i["L2_attn_D"], DI // H2, axis=1))
    par[:, :, MB_RMSW:MB_DTB] = columns(i["L2_attn_rms_w"])
    par[:, :, MB_DTB:MB_ALOG] = i["L2_attn_dt_bias"][:, None, :]
    par[:, :, MB_ALOG:] = i["L2_attn_A_log"][:, None, :]
    w1 = i["L3_ffn_w1"].reshape(E, KD, P, EX_F)
    w2 = i["L3_ffn_w2"].reshape(E, EX_FG, EX_GB, P, D).transpose(0, 1, 3, 2, 4).reshape(E, EX_FG, P, EX_F)
    return {
        "x_cm": x, "x_tm": x.T,
        "ln2d_w": i["L0_conv_ln_w"].reshape(TT, P).T, "ln2d_b": i["L0_conv_ln_b"].reshape(TT, P).T,
        "dt_w01": np.stack([np.tile(i["L0_conv_dt_w"][0], 4), np.tile(i["L1_conv_w_dt"][0], 4)], 1),
        "dt_b01": np.stack([np.tile(i["L0_conv_dt_b"], SIDE), np.tile(i["L1_conv_b_dt"], SIDE)], 1),
        "log_A01": np.stack([i["L0_conv_log_A"], i["L1_conv_log_A"]], 1),
        "m_par": par,
        "m_in_w": i["L2_attn_in_proj_w"].transpose(0, 2, 1), "m_out_w": i["L2_attn_out_proj_w"].transpose(0, 2, 1),
        "f_w": i["L2_ffn_weight"],
        "a_nw": i["L3_attn_norm_w"].reshape(KD, P).T, "a_in_b": i["L3_attn_in_proj_b"],
        "a_out_b": i["L3_attn_out_proj_b"], "a_alog": i["L3_attn_A_log"], "a_D": i["L3_attn_D"],
        "a_dtb": i["L3_attn_dt_bias"], "a_in_w": i["L3_attn_in_proj_w"].T, "a_out_w": i["L3_attn_out_proj_w"].T,
        "e_gw": i["L3_ffn_gate_w"].T.reshape(KD, P, E).transpose(1, 0, 2),
        "e_b1": i["L3_ffn_b1"].reshape(E, EX_FB, P).transpose(2, 0, 1), "e_b2": i["L3_ffn_b2"],
        "e_w": np.concatenate([w1, w2], 1).reshape(-1, EX_F)}


def kernel(**inputs):
    import concourse.bacc as bacc
    from concourse.bass_utils import run_bass_kernel_spmd

    arrays = {**shape_constants(), **laid_out({k: np.asarray(v) for k, v in inputs.items()})}
    arrays = {k: np.ascontiguousarray(v) for k, v in arrays.items()}
    nc = bacc.Bacc("TRN2", target_bir_lowering=False, num_devices=1)
    ins = {k: nc.dram_tensor(k, v.shape, mybir.dt.from_np(v.dtype), kind="ExternalInput").ap() for k, v in arrays.items()}
    out = nc.dram_tensor("out", [TOK, D], F32, kind="ExternalOutput").ap()
    program(nc, ins, out)
    result = run_bass_kernel_spmd(nc, [arrays], core_ids=[0]).results[0]["out"]
    return np.ascontiguousarray(np.asarray(result).T).reshape(1, SEQ, SIDE, SIDE)
```

```python
from contextlib import ExitStack

import numpy as np
import concourse.bass as bass
from concourse import mybir

P = 128
F32 = mybir.dt.float32
F16 = mybir.dt.float16
U32 = mybir.dt.uint32
ACT = mybir.ActivationFunctionType
ALU = mybir.AluOpType
AX = mybir.AxisListType
ds = bass.ds

SEQ, SIDE = 512, 32
TOK = SIDE * SIDE
TT = TOK // P
D = 512
KD = D // P
GROUPS = 32
DI = 1024
JD = DI // P
NS = 32
H2 = 32
LAYERS = 2
TAPS = 4
E, TOPK = 8, 2
BLOCKS = TOK // P
FILLED = TOPK * TT + E + 1
TABLE = FILLED + BLOCKS


class Core:

    def __init__(self, nc, ctx, ins, out):
        self.nc, self.ctx, self.ins, self.out = nc, ctx, ins, out
        self.stage_end = self.sem("stage_end")
        self.stage_sems = None
        self.t = self.sb("t_res", [P, TT, D])
        self.stats = self.sb("t_stats", [P, TT, 6])
        self.ident = self.sb("ident", [P, P])
        self.tri = self.sb("tri", [P, P])
        self.after = self.sb("after", [P, P])
        self.after16 = self.sb("after16", [P, P], F16)
        self.tri16 = self.sb("tri16", [P, P], F16)
        self.ones = self.sb("ones", [P, P])
        self.sel16 = self.sb("sel16", [H2, JD, P], F16)
        self.xs_dram = nc.dram_tensor("xs_table", [TABLE * P, D], F32).ap()
        self.ys_dram = nc.dram_tensor("ys_table", [TABLE * P, D], F32).ap()
        self.zero_set, self.zero_out = self.sem("zero_set"), self.sem("zero_out")
        self.passed = self.sem("passed")
        self.consts_in = self.sem("consts_in")

    def sb(self, name, shape, dt=F32, ctx=None):
        return (ctx or self.ctx).enter_context(self.nc.sbuf_tensor(name, shape, dt))

    def sem(self, name, ctx=None):
        return (ctx or self.ctx).enter_context(self.nc.semaphore(name))

    def stage_sem(self, name, used):
        used.append(self.sem(name, self.stage_sems))
        return used[-1]

    def load_consts(self, sp):
        for dst, name in ((self.ident, "c_ident"), (self.tri, "c_tri"), (self.after, "c_after"),
                          (self.after16, "c_after16"), (self.tri16, "c_tri16"), (self.ones, "c_ones"), (self.sel16, "c_sel16")):
            sp.dma_start(dst[:], self.ins[name]).then_inc(self.consts_in, 16)

    CONSTS = 7 * 16

    def zero_tables(self, e, zero):
        e.memset(zero[:], 0.0).then_inc(self.zero_set, 1)
        e.wait_ge(self.zero_set, 1)
        e.dma_start(self.xs_dram[0:FILLED * P, :].rearrange("(b p) f -> p b f", p=P),
                    zero[:].unsqueeze(1).to_broadcast([P, FILLED, D])).then_inc(self.zero_out, 16)
        e.dma_start(self.ys_dram[TOPK * TT * P:(FILLED - 2) * P, :].rearrange("(b p) f -> p b f", p=P),
                    zero[:].unsqueeze(1).to_broadcast([P, FILLED - 2 - TOPK * TT, D])).then_inc(self.zero_out, 16)

    def apart(self, e):
        e.sem_inc(self.passed, 1)


class Chain:

    def __init__(self, eng, sem):
        self.eng, self.sem, self.n = eng, sem, 0

    def __call__(self, instruction):
        instruction.then_inc(self.sem, 1)
        self.n = self.n + 1
        self.eng.wait_ge(self.sem, self.n)


L01_EPS_GN = 1e-5
L01_EPS_LN2 = 1e-5


def stage_l01(core, ps):
    nc, ins, t = core.nc, core.ins, core.t
    cx = ExitStack()
    sb = lambda n, s, d=F32: core.sb(n, s, d, cx)
    used = []
    sem = lambda n: core.stage_sem("c_" + n, used)
    xcm = sb("xcm", [P, KD, TOK])
    xn = sb("xn", [P, TT, D])
    sq = sb("sq", [P, TT, D])
    selT = sb("selT", [P, TT, H2])
    wsel = sb("wsel", [P, 2, TT, H2])
    g16 = sb("g16", [P, P])
    lnw = sb("lnw2d", [P, TT])
    lnb = sb("lnb2d", [P, TT])
    dtw = sb("dtw", [P, 2])
    dtb = sb("dtb", [H2, 2])
    loga = sb("loga", [H2, 2])
    nega = sb("nega", [H2, 2])
    stats = sb("stats0", [P, KD, 2, 6])
    mv = sb("mv0", [P, KD, 2])
    dev = sb("dev0", [P, KD])
    q = sb("q0", [P, KD])
    rg = sb("rg0", [P, KD])
    rc = sb("rc0", [P, KD])
    sh = sb("sh0", [P, KD])
    xb = sb("xb01", [H2, D])
    ab = sb("ab01", [H2, D])
    ex = sb("ex01", [H2, D])
    lg = sb("lg01", [H2, D])
    dtt = sb("dtt01", [H2, D])
    dec = sb("dec01", [H2, D])
    dec_hi, dec_lo = sb("dec_hi01", [H2, D], F16), sb("dec_lo01", [H2, D], F16)
    mg = sb("mg", [P, GROUPS])
    rgr = sb("rgr", [P, GROUPS])

    onesn = sb("onesn", [P, P])
    zero = sb("zero", [P, D])
    x_cm_in = sem("x_cm_in")
    x_tm_in = sem("x_tm_in")
    par_in = sem("par01_in")
    dve_own = sem("dve_own01")
    act_own = sem("act_own01")
    ch_mean = sem("ch_mean")
    g_mean = sem("g_mean")
    ch_spread = sem("ch_spread")
    g_var = sem("g_var")
    sq_in = sem("sq_in")
    sq_out = sem("sq_out")
    x_hat = sem("x_hat")
    turned = sem("turned")
    affine = sem("affine")
    weights = sem("weights01")
    dt_raw = sem("dt_raw01")
    pre = sem("pre01")
    negabs = sem("negabs01")
    log1p = sem("log1p01")
    dt_done = sem("dt_done01")
    decayed = sem("decayed01")
    spread_d = sem("spread_d01")
    scanned = sem("scanned")
    added = sem("added01")
    added_odd = sem("added_odd01")
    dec_high = sem("dec_high01")
    dec_low = sem("dec_low01")
    tot = sem("tot01")
    centred = sem("centred")
    squared = sem("squared")
    scaled = sem("scaled01")
    PAR = 8 * 16

    def sp(e):
        for j in range(KD):
            e.dma_start(xcm[:, j, :], ins["x_cm"][j * P:(j + 1) * P, :]).then_inc(x_cm_in, 16)
        for dst, name in ((selT, "c_selT"), (g16, "c_g16"), (onesn, "c_onesn"), (lnw, "ln2d_w"), (lnb, "ln2d_b"),
                          (dtw, "dt_w01"), (dtb, "dt_b01"), (loga, "log_A01")):
            e.dma_start(dst[:], ins[name]).then_inc(par_in, 16)
        core.load_consts(e)
        e.dma_start(t[:], ins["x_tm"].rearrange("(i p) f -> p i f", p=P)).then_inc(x_tm_in, 16)

    def dve(e):
        own = Chain(e, dve_own)
        e.wait_ge(x_cm_in, 16 * KD)
        for j in range(KD):
            e.bn_stats(stats[:, j, 0, :], xcm[:, j, 0:512])
            own(e.bn_stats(stats[:, j, 1, :], xcm[:, j, 512:1024]))
        for j in range(KD):
            own(e.bn_aggr(mv[:, j, :], stats[:, j, :, :].rearrange("p a b -> p (a b)")))
        e.tensor_copy(dev[:], mv[:, :, 0]).then_inc(ch_mean, 1)
        e.wait_ge(g_mean, 1)
        own(e.tensor_tensor(dev[:], mv[:, :, 0], ps[:, 0, 0:KD], ALU.subtract))
        own(e.tensor_tensor(q[:], dev[:], dev[:], ALU.mult))
        e.tensor_tensor(q[:], q[:], mv[:, :, 1], ALU.add).then_inc(ch_spread, 1)
        e.wait_ge(g_var, 1)
        e.tensor_scalar(rg[:], ps[:, 1, 0:KD], L01_EPS_GN, None, ALU.add).then_inc(sq_in, 1)
        e.wait_ge(sq_out, 1)
        own(e.reciprocal(rg[:], rg[:]))
        own(e.tensor_tensor(q[:], rg[:], rg[:], ALU.mult))
        own(e.tensor_tensor(q[:], q[:], mv[:, :, 1], ALU.mult))
        e.tensor_scalar(rc[:], q[:], L01_EPS_LN2, None, ALU.add).then_inc(sq_in, 1)
        e.wait_ge(sq_out, 2)
        own(e.reciprocal(rc[:], rc[:]))
        own(e.tensor_tensor(rc[:], rc[:], rg[:], ALU.mult))
        own(e.scalar_tensor_tensor(out=sh[:], in0=mv[:, :, 0], scalar=-1.0, in1=rc[:], op0=ALU.mult, op1=ALU.mult))
        for j in range(KD):
            e.tensor_scalar(xcm[:, j, :], xcm[:, j, :], rc[:, j:j + 1], sh[:, j:j + 1], ALU.mult, ALU.add).then_inc(x_hat, 1)
        e.wait_ge(par_in, PAR)
        for l in range(2):
            e.tensor_scalar(wsel[:, l, :, :], selT[:], dtw[:, l:l + 1], None, ALU.mult).then_inc(weights, 1)
        e.wait_ge(x_tm_in, 16)
        scans(e, 0)
        e.wait_ge(added, TT // 2)
        e.wait_ge(added_odd, TT // 2)
        e.wait_ge(tot, 1)
        own(e.tensor_reduce(mg[:], grp(ps[:, 4, :]), AX.X, ALU.add))
        for i in range(TT):
            e.tensor_tensor(grp(xn[:, i, :]), grp(t[:, i, :]), per_group(mg), ALU.subtract).then_inc(centred, 1)
        e.wait_ge(tot, 2)
        own(e.tensor_reduce(rgr[:], grp(ps[:, 5, :]), AX.X, ALU.add))
        e.tensor_scalar(rgr[:], rgr[:], L01_EPS_GN, None, ALU.add).then_inc(sq_in, 1)
        e.wait_ge(sq_out, 3)
        own(e.reciprocal(rgr[:], rgr[:]))
        for i in range(TT):
            e.tensor_tensor(grp(xn[:, i, :]), grp(xn[:, i, :]), per_group(rgr), ALU.mult).then_inc(scaled, 1)
        scans(e, 1)

    def grp(x):
        return x.rearrange("p (g c) -> p g c", g=GROUPS)

    def per_group(x):
        return x[:].unsqueeze(2).to_broadcast([P, GROUPS, SEQ // GROUPS])

    def scans(e, l):
        e.wait_ge(pre, l + 1)
        e.scalar_tensor_tensor(out=ab[:], in0=xb[:], scalar=-1.0, in1=xb[:], op0=ALU.mult, op1=ALU.min).then_inc(negabs, 1)
        e.wait_ge(log1p, 2 * l + 2)
        e.scalar_tensor_tensor(out=dtt[:], in0=xb[:], scalar=0.0, in1=lg[:], op0=ALU.max, op1=ALU.add).then_inc(dt_done, 1)
        e.wait_ge(dec_high, l + 1)
        e.tensor_tensor(dec_lo[:], dec[:], dec_hi[:], ALU.subtract).then_inc(dec_low, 1)
        for i in range(TT + 1):
            if i < TT:
                e.wait_ge(spread_d, l * TT + i + 1)
                e.tensor_tensor_scan(sq[:, i, :], ps[:, i % 4, :], xn[:, i, :], 0.0, ALU.mult, ALU.add)\
                    .then_inc(scanned, 1)
            if i and i % 2 == 0:
                e.wait_ge(scanned, l * TT + i)
                e.tensor_tensor(t[:, i - 1, :], t[:, i - 1, :], sq[:, i - 1, :], ALU.add).then_inc(added_odd, 1)

    def pool(e):
        e.wait_ge(x_tm_in, 16)
        core.zero_tables(e, zero)
        for l in range(2):
            for i in range(0, TT, 2):
                e.wait_ge(scanned, l * TT + i + 1)
                e.tensor_tensor(t[:, i, :], t[:, i, :], sq[:, i, :], ALU.add).then_inc(added, 1)
        e.wait_ge(added, TT)
        e.wait_ge(core.zero_out, 32)

    def act(e):
        own = Chain(e, act_own)
        for k, s in enumerate((rg, rc)):
            e.wait_ge(sq_in, k + 1)
            e.activation(s[:], s[:], ACT.Sqrt).then_inc(sq_out, 1)
        e.wait_ge(par_in, PAR)
        own(e.activation(nega[:], loga[:], ACT.Exp))
        own(e.mul(nega[:], nega[:], -1.0))
        for i in range(TT):
            e.wait_ge(turned, i + 1)
            e.activation(xn[:, i, :], ps[:, 2 + i % 4, :], ACT.Identity, scale=lnw[:, i:i + 1], bias=lnb[:, i:i + 1])\
                .then_inc(affine, 1)
        decay(e, 0)
        for i in range(TT):
            e.wait_ge(centred, i + 1)
            e.activation(sq[:, i, :], xn[:, i, :], ACT.Square).then_inc(squared, 1)
        e.wait_ge(sq_in, 3)
        e.activation(rgr[:], rgr[:], ACT.Sqrt).then_inc(sq_out, 1)
        decay(e, 1)

    def decay(e, l):
        e.wait_ge(dt_raw, l + 1)
        e.activation(xb[:], ps[0:H2, 6, :], ACT.Identity, bias=dtb[:, l:l + 1]).then_inc(pre, 1)
        e.wait_ge(negabs, l + 1)
        e.activation(ex[:], ab[:], ACT.Exp).then_inc(log1p, 1)
        e.wait_ge(log1p, 2 * l + 1)
        e.activation(lg[:], ex[:], ACT.Ln, bias=1.0).then_inc(log1p, 1)
        e.wait_ge(dt_done, l + 1)
        e.activation(dec[:], dtt[:], ACT.Exp, scale=nega[:, l:l + 1]).then_inc(decayed, 1)
        e.wait_ge(decayed, l + 1)
        e.activation(dec_hi[:], dec[:], ACT.Copy).then_inc(dec_high, 1)

    def pe(e):
        e.wait_ge(par_in, PAR)
        e.wait_ge(core.consts_in, core.CONSTS)
        e.wait_ge(ch_mean, 1)
        e.matmul(ps[:, 0, 0:KD], g16[:], dev[:], start=True, stop=True).then_inc(g_mean, 1)
        e.wait_ge(ch_spread, 1)
        e.matmul(ps[:, 1, 0:KD], g16[:], q[:], start=True, stop=True).then_inc(g_var, 1)
        for i in range(TT):
            if i >= 4:
                e.wait_ge(affine, i - 3)
            for j in range(KD):
                if i == 0:
                    e.wait_ge(x_hat, j + 1)
                x = e.transpose(ps[:, 2 + i % 4, j * P:(j + 1) * P], xcm[:, j, i * P:(i + 1) * P], core.ident[:])
            x.then_inc(turned, 1)
        decays(e, 0)
        for i in range(TT):
            e.wait_ge(added_odd if i % 2 else added, i // 2 + 1)
            x = e.matmul(ps[:, 4, :], onesn[:], t[:, i, :], start=(i == 0), stop=(i == TT - 1))
        x.then_inc(tot, 1)
        for i in range(TT):
            e.wait_ge(squared, i + 1)
            x = e.matmul(ps[:, 5, :], onesn[:], sq[:, i, :], start=(i == 0), stop=(i == TT - 1))
        x.then_inc(tot, 1)
        decays(e, 1)

    def decays(e, l):
        e.wait_ge(weights, l + 1)
        for i in range(TT):
            e.wait_ge(scaled if l else affine, i + 1)
            x = e.matmul(ps[0:H2, 6, :], wsel[:, l, i, :], xn[:, i, :], start=(i == 0), stop=(i == TT - 1))
        x.then_inc(dt_raw, 1)
        e.wait_ge(dec_low, l + 1)
        for i in range(TT):
            if i >= 4:
                e.wait_ge(scanned, l * TT + i - 3)
            for m, part in enumerate((dec_hi, dec_lo)):
                x = e.matmul(ps[:, i % 4, :], core.sel16[:, i, :], part[:], start=(m == 0), stop=(m == 1))
            x.then_inc(spread_d, 1)

    return dict(sp=sp, dve=dve, act=act, pe=pe, pool=pool, cx=cx, used=used)


MB_EPS = 1e-5
MB_DPROJ = 2 * DI + 2 * NS + H2
MB_CX, MB_CB, MB_CC, MB_CDT = DI, 2 * DI, 2 * DI + NS, 2 * DI + 2 * NS
MB_PIECES = 6
MB_ER = 2
MB_EG = 8
MB_LNW, MB_LNB, MB_CVW, MB_CVB, MB_BCW, MB_BCB, MB_DCOL, MB_RMSW, MB_DTB, MB_ALOG = 0, 4, 8, 40, 48, 56, 58, 66, 74, 106
MB_NPAR = 138


def stage_mamba(core, ps):
    nc, ins, t = core.nc, core.ins, core.t
    cx = ExitStack()
    sb = lambda n, s, d=F32: core.sb("mb_" + n, s, d, cx)
    used = []
    sem = lambda n: core.stage_sem("m_" + n, used)
    h = t
    kept = nc.dram_tensor("t_kept", [TOK, D], F32).ap().rearrange("(i p) f -> p i f", p=P)
    par = sb("par", [P, MB_NPAR])
    wi_hi, wi_lo = sb("wi_hi", [P, KD, MB_DPROJ], F16), sb("wi_lo", [P, KD, MB_DPROJ], F16)
    wo_hi, wo_lo = sb("wo_hi", [P, JD, D], F16), sb("wo_lo", [P, JD, D], F16)
    ring = sb("ring", [P, 2 * MB_DPROJ])
    raw = [ring[:, b * MB_DPROJ:(b + 1) * MB_DPROJ] for b in range(2)]
    u_hi, u_lo = sb("u_hi", [P, KD, TOK], F16), sb("u_lo", [P, KD, TOK], F16)
    stats, mv = sb("stats", [P, TT, 6]), sb("mv", [P, TT, 2])
    rstd = sb("rstd", [P, TT])
    nega = sb("nega", [P, H2])
    dtx, dtn, dte_ = sb("dtx", [P, TT, H2]), sb("dtn", [P, TT, H2]), sb("dte_", [P, TT, H2])
    dt, la, dend = sb("dt", [P, TT, H2]), sb("la", [P, TT, H2]), sb("dend", [P, TT, H2])
    edec, dte = sb("edec", [P, TT, H2]), sb("dte", [P, TT, H2])
    la_hi, la_lo = sb("la_hi", [P, TT, H2], F16), sb("la_lo", [P, TT, H2], F16)
    cum_hi, cum_lo = sb("cum_hi", [H2, TOK], F16), sb("cum_lo", [H2, TOK], F16)
    tri_th = sb("tri_th", [P, P, H2], F16)
    r_hi, r_lo = (ring[:, b * 2048:(b + 1) * 2048].bitcast(F16).rearrange("p (t h) -> p t h", h=H2) for b in range(2))
    E = sb("E", [P, MB_ER * 512])
    M = sb("M", [P, H2, P])
    uf = M[:].rearrange("p h t -> p (h t)").rearrange("p (i f) -> p i f", i=TT)
    xp, bcp = sb("xp", [P, JD, P + 3]), sb("bcp", [NS, 2, P + 3])
    ca, cbc = sb("ca", [P, JD, P]), sb("cbc", [NS, 2, P])
    th, thbc = sb("th", [P, JD, P]), sb("thbc", [NS, 2, P])
    xc, bcc = sb("xc", [P, JD, P]), sb("bcc", [NS, 2, P])
    thz, sz = th, sb("sz", [P, JD, P])
    xdt, xe = sb("xdt", [P, DI]), sb("xe", [P, DI])
    btok = sb("btok", [P, NS])
    gm = sb("gm", [P, P])
    S = sb("S", [NS, DI])
    quad = sb("quad", [P, 4, DI])
    un = quad[:].rearrange("p a b -> p (a b)").rearrange("p (i f) -> p i f", i=TT)
    ec, yi, dx, y = (quad[:, a, :].rearrange("p (j t) -> p j t", j=JD) for a in range(4))
    ysq = sb("ysq", [P, JD, P])
    y_hi, y_lo = sb("y_hi", [P, JD, P], F16), sb("y_lo", [P, JD, P], F16)
    rv, rs, mhalf = sb("rv", [P, 1]), sb("rs", [P, 1]), sb("mhalf", [P, 1])

    dve_own, act_own, pool_own = sem("dve_own"), sem("act_own"), sem("pool_own")
    layer_open = sem("layer_open")
    ring_free = sem("ring_free")
    par_in = sem("par_in")
    raw_in = [sem(f"raw_in{b}") for b in range(2)]
    w_hi, w_lo = sem("w_hi"), sem("w_lo")
    var_done, sd_done = sem("var_done"), sem("sd_done")
    un_done, turned, uf_done, uhi_done, ulo_done = (sem(n) for n in ("un_done", "turned", "uf_done", "uhi_done", "ulo_done"))
    dt_mm, dtn_done, dt_log, la_done, sums_mm, sums_exp, cum_ev, prep = (
        sem(n) for n in ("dt_mm", "dtn_done", "dt_log", "la_done", "sums_mm", "sums_exp", "cum_ev", "prep"))
    acc_bc, ysum_done = sem("acc_bc"), sem("ysum_done")
    stats_done = sem("stats_done")
    nega_done, split_la = sem("nega_done"), sem("split_la")
    zeroed = sem("zeroed")
    x_mm, bc_mm, z_mm = sem("x_mm"), sem("bc_mm"), sem("z_mm")
    x_ev, bc_ev = sem("x_ev"), sem("bc_ev")
    halo = sem("halo")
    acc, tanh, xc_done, bcc_done = sem("acc"), sem("tanh"), sem("xc_done"), sem("bcc_done")
    thz_done, sz_done = sem("thz_done"), sem("sz_done")
    rhi_done, rlo_done = sem("rhi_done"), sem("rlo_done")
    xtr, x_scaled, g_mm, gm_done, bt_done = (sem(n) for n in ("xtr", "x_scaled", "g_mm", "gm_done", "bt_done"))
    diff, exped, m_done = sem("diff"), sem("exped"), sem("m_done")
    ecum_mm, ec_done, inter_mm, yi_done, yid_done, dx_done = (
        sem(n) for n in ("ecum_mm", "ec_done", "inter_mm", "yi_done", "yid_done", "dx_done"))
    ds_mm, smul, s_done = sem("ds_mm"), sem("smul"), sem("s_done")
    intra_mm, ya_done, y_done, yhi_done, ylo_done, ysq_done = (
        sem(n) for n in ("intra_mm", "ya_done", "y_done", "yhi_done", "ylo_done", "ysq_done"))
    rms_mm, rv_done, pow_done, out_mm, h_done = (sem(n) for n in ("rms_mm", "rv_done", "pow_done", "out_mm", "h_done"))

    W_IN = ins["m_in_w"]
    W_OUT = ins["m_out_w"]

    def chunks(e, l, body):
        body(0, l * TT, True, False)
        with e.Fori(1, TT - 1) as i:
            body(i, l * TT + i, False, False)
        body(TT - 1, l * TT + TT - 1, False, True)

    def heads(x):
        return x.rearrange("p (h q) -> p h q", h=H2)

    def sp(e):
        e.dma_start(kept, t[:]).then_inc(t_kept, 16)
        with e.Fori(0, LAYERS) as l:
            e.wait_ge(ring_free, l + 1)
            for n in range(MB_PIECES):
                if n == 2:
                    e.wait_ge(layer_open, l + 1)
                    e.dma_start(par[:], ins["m_par"][l, :, :]).then_inc(par_in, 16)
                if n >= 2:
                    e.wait_ge(w_hi, l * MB_PIECES + n - 1)
                    e.wait_ge(w_lo, l * MB_PIECES + n - 1)
                if n < KD:
                    e.dma_start(raw[n % 2], W_IN[l, n * P:(n + 1) * P, :]).then_inc(raw_in[n % 2], 16)
                else:
                    e.dma_start(raw[n % 2][:, 0:4 * D].rearrange("p (j f) -> p j f", j=4),
                                W_OUT[l, (n - KD) * 512:(n - KD + 1) * 512, :].rearrange("(j p) f -> p j f", p=P))\
                        .then_inc(raw_in[n % 2], 16)

        e.wait_ge(intra_mm, LAYERS * TT)
        e.dma_start(uf, kept).then_inc(t_back, 16)

    def dve(e):
        own = Chain(e, dve_own)

        def aggregate():
            for i in range(TT):
                x = e.bn_aggr(mv[:, i, :], stats[:, i, :])
            own(x)
            e.tensor_scalar(rstd[:], mv[:, :, 1], MB_EPS, None, ALU.add).then_inc(var_done, 1)

        def lower(l, n):
            e.wait_ge(w_hi, l * MB_PIECES + (n + 1))
            if n < KD:
                e.tensor_tensor(wi_lo[:, n, :], raw[n % 2], wi_hi[:, n, :], ALU.subtract).then_inc(w_lo, 1)
            else:
                for q in range(4):
                    j = 4 * (n - KD) + q
                    x = e.scalar_tensor_tensor(out=wo_lo[:, j, :], in0=raw[n % 2][:, q * D:(q + 1) * D],
                                               scalar=par[:, MB_RMSW + j:MB_RMSW + j + 1], in1=wo_hi[:, j, :],
                                               op0=ALU.mult, op1=ALU.subtract)
                x.then_inc(w_lo, 1)

        def split_u(l, i):
            e.wait_ge(uf_done, l * TT + (i + 1))
            v, hi = uf[:, i, :].rearrange("p (k c) -> p k c", k=KD), u_hi[:, :, i * P:(i + 1) * P]
            if i % 2:
                own(e.tensor_copy(hi, v))
            else:
                e.wait_ge(uhi_done, l * (TT // 2) + (i // 2 + 1))
            e.tensor_tensor(u_lo[:, :, i * P:(i + 1) * P], v, hi, ALU.subtract).then_inc(ulo_done, 1)

        for i in range(TT):
            x = e.bn_stats(stats[:, i, :], t[:, i, :])
        own(x)
        aggregate()
        e.tensor_copy(tri_th[:], core.tri16[:].unsqueeze(2).to_broadcast([P, P, H2]))
        e.wait_ge(sd_done, 1)
        own(e.reciprocal(rstd[:], rstd[:]))
        e.wait_ge(t_kept, 16)
        for i in range(TT):
            x = e.tensor_scalar(h[:, i, :], t[:, i, :], mv[:, i, 0:1], rstd[:, i:i + 1], ALU.subtract, ALU.mult)
        own(x)
        own(e.tensor_tensor(rstd[:], rstd[:], rstd[:], ALU.mult))
        own(e.tensor_tensor(mv[:, :, 1], mv[:, :, 1], rstd[:], ALU.mult))
        own(e.memset(mv[:, :, 0], 0.0))
        e.tensor_scalar(rstd[:], mv[:, :, 1], MB_EPS, None, ALU.add).then_inc(var_done, 1)
        e.wait_ge(var_done, 2)
        e.tensor_copy(rv[:], mv[:, 0, 0:1]).then_inc(layer_open, 1)

        start = own.n
        with e.Fori(0, LAYERS) as l:
            own.n = start + l * OWN_PER_LAYER
            e.wait_ge(layer_open, l + 1)
            core.apart(e)
            e.wait_ge(sd_done, l + 2)
            own(e.reciprocal(rstd[:], rstd[:]))
            for i in range(TT):
                e.tensor_scalar(un[:, i, :], h[:, i, :], mv[:, i, 0:1], rstd[:, i:i + 1], ALU.subtract, ALU.mult)\
                    .then_inc(un_done, 1)
            lower(l, 0)
            lower(l, 1)
            e.wait_ge(par_in, (l + 1) * 16)
            core.apart(e)
            own(e.tensor_scalar(par[:, MB_CVW:MB_DCOL], par[:, MB_CVW:MB_DCOL], 0.5, None, ALU.mult))
            for i in range(TT):
                split_u(l, i)
                if i % 4 == 3:
                    lower(l, 2 + i // 4)
            lower(l, 4)
            e.wait_ge(dt_mm, l + 1)
            own(e.tensor_tensor(dtx[:], ps[:, 2, 0:TT * H2].rearrange("p (i h) -> p i h", i=TT),
                                par[:, MB_DTB:MB_DTB + H2].unsqueeze(1).to_broadcast([P, TT, H2]), ALU.add))
            e.scalar_tensor_tensor(out=dtn[:], in0=dtx[:], scalar=-1.0, in1=dtx[:], op0=ALU.mult, op1=ALU.min)\
                .then_inc(dtn_done, 1)
            lower(l, 5)
            e.wait_ge(dt_log, l + 1)
            own(e.scalar_tensor_tensor(out=dt[:], in0=dtx[:], scalar=0.0, in1=dte_[:], op0=ALU.max, op1=ALU.add))
            e.wait_ge(nega_done, l + 1)
            e.tensor_tensor(la[:], dt[:], nega[:].unsqueeze(1).to_broadcast([P, TT, H2]), ALU.mult).then_inc(la_done, 1)
            e.wait_ge(la_done, l + 1)
            own(e.tensor_copy(la_hi[:], la[:]))
            e.tensor_tensor(la_lo[:], la[:], la_hi[:], ALU.subtract).then_inc(split_la, 1)
            e.wait_ge(split_la, l + 1)
            def r_build(i):
                e.tensor_tensor(r_lo, la_lo[:, i, :].unsqueeze(1).to_broadcast([P, P, H2]), tri_th[:], ALU.mult)\
                    .then_inc(rlo_done, 1)

            def conv(g):
                for q in range(2):
                    e.wait_ge(x_ev, 2 * g + q + 1)
                    for k in range(TAPS - 1):
                        for j in range(4 * q, 4 * q + 4):
                            x = e.scalar_tensor_tensor(out=ca[:, j, :], in0=xp[:, j, k:k + P],
                                                       scalar=par[:, MB_CVW + 4 * j + k:MB_CVW + 4 * j + k + 1],
                                                       in1=ca[:, j, :], op0=ALU.mult, op1=ALU.add)
                        if k < TAPS - 2:
                            own(x)
                    x.then_inc(acc, 1)
                for q in range(2):
                    e.wait_ge(tanh, 3 * g + q + 1)
                    e.scalar_tensor_tensor(out=xc[:, 4 * q:4 * q + 4, :], in0=th[:, 4 * q:4 * q + 4, :], scalar=1.0,
                                           in1=ca[:, 4 * q:4 * q + 4, :], op0=ALU.add, op1=ALU.mult).then_inc(xc_done, 1)
                e.wait_ge(tanh, 3 * g + 3)
                e.scalar_tensor_tensor(out=bcc[:], in0=thbc[:], scalar=1.0, in1=cbc[:], op0=ALU.add, op1=ALU.mult)\
                    .then_inc(bcc_done, 1)

            def gate(g):
                for q in range(2):
                    e.wait_ge(thz_done, 2 * g + q + 1)
                    e.scalar_tensor_tensor(out=sz[:, 4 * q:4 * q + 4, :], in0=thz[:, 4 * q:4 * q + 4, :], scalar=1.0,
                                           in1=ps[:, 1 - q, :].rearrange("p (j t) -> p j t", j=4),
                                           op0=ALU.add, op1=ALU.mult).then_inc(sz_done, 1)

            def finish(i, g):
                e.wait_ge(rms_mm, g + 1)
                e.tensor_scalar(rv[:], ps[:, 2, 384:385], 1.0 / DI, 4 * MB_EPS, ALU.mult, ALU.add).then_inc(rv_done, 1)
                e.wait_ge(pow_done, g + 1)
                e.wait_ge(out_mm, g + 1)
                e.scalar_tensor_tensor(out=h[:, i, :], in0=ps[:, 7, :], scalar=rs[:], in1=h[:, i, :],
                                       op0=ALU.mult, op1=ALU.add).then_inc(h_done, 1)
                e.wait_ge(h_done, g + 1)
                core.apart(e)
                e.bn_stats(stats[:, i, :], h[:, i, :]).then_inc(stats_done, 1)

            def lower_y(g):
                e.wait_ge(yhi_done, g + 1)
                e.tensor_tensor(y_lo[:], y, y_hi[:], ALU.subtract).then_inc(ylo_done, 1)

            r_build(0)
            e.wait_ge(sums_exp, l + 1)
            e.tensor_tensor(cum_lo[:], ps[0:H2, 4:6, :].rearrange("p b n -> p (b n)"), cum_hi[:], ALU.subtract)
            e.tensor_tensor(dte[:], dend[:], dt[:], ALU.mult).then_inc(prep, 1)
            e.wait_ge(prep, l + 1)
            conv(l * TT)
            gate(l * TT)

            def body(i, g, is_first, is_last):
                e.wait_ge(g_mm, g + 1)
                e.tensor_tensor(gm[:], ps[:, 2, P:2 * P], core.tri[:], ALU.mult).then_inc(gm_done, 1)
                xt = heads(ps[:, 5:7, :].rearrange("p b n -> p (b n)"))
                e.wait_ge(gm_done, g + 1)
                for k in range(MB_EG):
                    e.wait_ge(exped, g * MB_EG + k + 1)
                    e.tensor_tensor(M[:].rearrange("p h t -> p t h")[:, 16 * k:16 * k + 16, :],
                                    E[:, 512 * (k % MB_ER):512 * (k % MB_ER + 1)].rearrange("p (t h) -> p t h", h=H2),
                                    gm[:, 16 * k:16 * k + 16].unsqueeze(2).to_broadcast([P, 16, H2]), ALU.mult)\
                        .then_inc(m_done, 1)
                    if k == 1 and not is_first:
                        lower_y(g - 1)
                    if k == 3:
                        e.wait_ge(xtr, g + 1)
                        e.tensor_tensor(heads(xdt[:]), xt, dt[:, i, :].unsqueeze(2).to_broadcast([P, H2, 32]), ALU.mult)
                    if k == 5:
                        e.tensor_tensor(heads(xe[:]), xt, dte[:, i, :].unsqueeze(2).to_broadcast([P, H2, 32]), ALU.mult)\
                            .then_inc(x_scaled, 1)
                if not is_last:
                    r_build(i + 1)
                if not is_first:
                    finish(i - 1, g - 1)
                e.wait_ge(inter_mm, g + 1)
                e.wait_ge(ec_done, g + 1)
                e.tensor_tensor(yi.rearrange("p j t -> p (j t)"), ps[:, 5:7, :].rearrange("p b n -> p (b n)"),
                                ec.rearrange("p j t -> p (j t)"), ALU.mult).then_inc(yi_done, 1)
                e.wait_ge(ds_mm, g + 1)
                e.wait_ge(smul, g + 1)
                e.tensor_tensor(S[:], S[:], ps[0:NS, 3:5, :].rearrange("p b n -> p (b n)"), ALU.add).then_inc(s_done, 1)
                if not is_last:
                    e.wait_ge(dx_done, g + 1)
                    conv(g + 1)
                e.wait_ge(intra_mm, g + 1)
                e.wait_ge(yid_done, g + 1)
                e.tensor_tensor(y[:, 0:4, :], ps[:, 7, :].rearrange("p (j t) -> p j t", j=4), yi[:, 0:4, :], ALU.add)
                e.tensor_tensor(y[:, 4:8, :], ps[:, 2, :].rearrange("p (j t) -> p j t", j=4), yi[:, 4:8, :], ALU.add)\
                    .then_inc(ya_done, 1)
                e.wait_ge(ya_done, g + 1)
                e.tensor_tensor(y, y, sz[:], ALU.mult).then_inc(y_done, 1)
                if not is_last:
                    e.wait_ge(y_done, g + 1)
                    gate(g + 1)

            own_before = own.n
            body(0, l * TT, True, False)
            per_chunk = OWN_PER_CONV
            own.n = own_before + per_chunk
            with e.Fori(1, TT - 1) as i:
                own.n = own_before + i * per_chunk
                body(i, l * TT + i, False, False)
            own.n = own_before + (TT - 1) * per_chunk
            body(TT - 1, l * TT + TT - 1, False, True)
            lower_y(l * TT + TT - 1)
            with e.If(l > LAYERS - 2):
                e.wait_ge(t_back, 16)
                e.wait_ge(stats_done, LAYERS * TT - 1)
                for i in range(TT - 1):
                    e.tensor_tensor(t[:, i, :], h[:, i, :], uf[:, i, :], ALU.add).then_inc(sum_done, 1)
                    if i:
                        e.wait_ge(sum_done, i)
                        e.bn_stats(core.stats[:, i - 1, :], t[:, i - 1, :])
            finish(TT - 1, l * TT + TT - 1)
            e.wait_ge(stats_done, (l + 1) * TT)
            core.apart(e)
            aggregate()
            e.wait_ge(var_done, l + 3)
            e.tensor_copy(rv[:], mv[:, 0, 0:1]).then_inc(layer_open, 1)
        e.wait_ge(layer_open, LAYERS + 1)
        e.tensor_tensor(t[:, TT - 1, :], h[:, TT - 1, :], uf[:, TT - 1, :], ALU.add).then_inc(sum_done, 1)
        for i in (TT - 2, TT - 1):
            e.wait_ge(sum_done, i + 1)
            e.bn_stats(core.stats[:, i, :], t[:, i, :])

    OWN_PER_CONV = 2 * (TAPS - 2)
    OWN_PER_LAYER = 1 + 1 + 1 + TT // 2 + 1 + 1 + 1 + TT * OWN_PER_CONV

    def act(e):
        own = Chain(e, act_own)

        def upper(l, n):
            e.wait_ge(raw_in[n % 2], l * (MB_PIECES // 2 * 16) + (n // 2 + 1) * 16)
            if n < KD:
                e.activation(wi_hi[:, n, :], raw[n % 2], ACT.Copy).then_inc(w_hi, 1)
            else:
                for q in range(4):
                    j = 4 * (n - KD) + q
                    x = e.activation(wo_hi[:, j, :], raw[n % 2][:, q * D:(q + 1) * D], ACT.Copy,
                                     scale=par[:, MB_RMSW + j:MB_RMSW + j + 1])
                x.then_inc(w_hi, 1)

        e.wait_ge(var_done, 1)
        e.activation(rstd[:], rstd[:], ACT.Sqrt).then_inc(sd_done, 1)
        with e.Fori(0, LAYERS) as l:
            e.wait_ge(var_done, l + 2)
            e.activation(rstd[:], rstd[:], ACT.Sqrt).then_inc(sd_done, 1)
            e.wait_ge(layer_open, l + 1)
            upper(l, 0)
            upper(l, 1)
            e.wait_ge(par_in, (l + 1) * 16)
            for i in range(TT):
                e.wait_ge(turned, l * TT + (i + 1))
                for k in range(KD):
                    x = e.activation(uf[:, i, k * P:(k + 1) * P], ps[:, i, k * P:(k + 1) * P], ACT.Identity,
                                     scale=par[:, MB_LNW + k:MB_LNW + k + 1], bias=par[:, MB_LNB + k:MB_LNB + k + 1])
                x.then_inc(uf_done, 1)
                if i % 4 == 3:
                    upper(l, 2 + i // 4)
            upper(l, 4)
            own.n = l * 4
            own(e.activation(nega[:], par[:, MB_ALOG:MB_ALOG + H2], ACT.Exp))
            e.mul(nega[:], nega[:], -1.0).then_inc(nega_done, 1)
            e.wait_ge(dtn_done, l + 1)
            own(e.activation(dte_[:], dtn[:], ACT.Exp))
            e.activation(dte_[:], dte_[:], ACT.Ln, bias=1.0).then_inc(dt_log, 1)
            upper(l, 5)

            def decay_sums():
                e.wait_ge(sums_mm, l + 1)
                own(e.activation(dend[:], ps[:, 3, 0:TT * H2].rearrange("p (i h) -> p i h", i=TT), ACT.Exp))
                own(e.activation(edec[:], ps[:, 3, TT * H2:2 * TT * H2].rearrange("p (i h) -> p i h", i=TT), ACT.Exp))
                e.activation(cum_hi[:], ps[0:H2, 4:6, :].rearrange("p b n -> p (b n)"), ACT.Copy).then_inc(sums_exp, 1)

            def project_x(g, is_first):
                if not is_first:
                    e.wait_ge(halo, g)
                    e.wait_ge(xc_done, 2 * g)
                for q in range(2):
                    e.wait_ge(x_mm, 2 * g + q + 1)
                    e.activation(xp[:, 4 * q:4 * q + 4, 3:P + 3], ps[:, q, :].rearrange("p (j t) -> p j t", j=4), ACT.Copy)
                    for j in range(4 * q, 4 * q + 4):
                        w = MB_CVW + 4 * j + TAPS - 1
                        x = e.activation(ca[:, j, :], ps[:, q, (j % 4) * P:(j % 4 + 1) * P], ACT.Identity,
                                         scale=par[:, w:w + 1], bias=par[:, MB_CVB + j:MB_CVB + j + 1])
                    x.then_inc(x_ev, 1)
                e.wait_ge(bc_mm, g + 1)
                e.activation(bcp[:, :, 3:P + 3], ps[0:NS, 0, 0:2 * P].rearrange("p (c t) -> p c t", c=2), ACT.Copy)
                if not is_first:
                    e.wait_ge(bcc_done, g)
                for c in range(2):
                    w = MB_BCW + 4 * c + TAPS - 1
                    x = e.activation(cbc[:, c, :], ps[0:NS, 0, c * P:(c + 1) * P], ACT.Identity,
                                     scale=par[0:NS, w:w + 1], bias=par[0:NS, MB_BCB + c:MB_BCB + c + 1])
                x.then_inc(bc_ev, 1)
                if is_first:
                    decay_sums()
                for q in range(2):
                    e.wait_ge(acc, 2 * g + q + 1)
                    e.activation(th[:, 4 * q:4 * q + 4, :], ca[:, 4 * q:4 * q + 4, :], ACT.Tanh).then_inc(tanh, 1)
                e.wait_ge(acc_bc, g + 1)
                e.activation(thbc[:], cbc[:], ACT.Tanh).then_inc(tanh, 1)

            def project_z(g):
                e.wait_ge(xc_done, 2 * g + 2)
                for q in range(2):
                    e.wait_ge(z_mm, 2 * g + q + 1)
                    e.activation(thz[:, 4 * q:4 * q + 4, :], ps[:, 1 - q, :].rearrange("p (j t) -> p j t", j=4),
                                 ACT.Tanh, scale=0.5).then_inc(thz_done, 1)

            def upper_y(g):
                e.wait_ge(y_done, g + 1)
                e.activation(y_hi[:], y, ACT.Copy).then_inc(yhi_done, 1)

            def square_y(g):
                e.activation(ysq[:], y, ACT.Square).then_inc(ysq_done, 1)

            e.wait_ge(zeroed, l + 1)
            project_x(l * TT, True)
            project_z(l * TT)

            def body(i, g, is_first, is_last):
                for k in range(MB_EG):
                    e.wait_ge(diff, MB_EG * g + k + 1)
                    if k >= MB_ER:
                        e.wait_ge(m_done, MB_EG * g + k - MB_ER + 1)
                    e.activation(E[:, 512 * (k % MB_ER):512 * (k % MB_ER + 1)], ps[:, 3 + k % 2, :], ACT.Exp).then_inc(exped, 1)
                    if k == 1:
                        e.wait_ge(gm_done, g + 1)
                        e.activation(btok[:], ps[:, 2, 0:NS], ACT.Copy).then_inc(bt_done, 1)
                        if not is_first:
                            upper_y(g - 1)
                    if not is_first and k == 3:
                        square_y(g - 1)
                e.wait_ge(ecum_mm, g + 1)
                e.activation(ec.rearrange("p j t -> p (j t)"), ps[:, 3:5, :].rearrange("p b n -> p (b n)"), ACT.Exp)\
                    .then_inc(ec_done, 1)
                if not is_last:
                    project_x(g + 1, False)
                    project_z(g + 1)

            chunks(e, l, body)
            upper_y(l * TT + TT - 1)
            square_y(l * TT + TT - 1)

    def pool(e):
        e.sem_inc(ring_free, 1)
        e.memset(mhalf[:], -0.5).then_inc(pool_own, 1)
        e.wait_ge(pool_own, 1)
        with e.Fori(0, LAYERS) as l:
            e.wait_ge(layer_open, l + 1)
            core.apart(e)
            e.memset(S[:], 0.0)
            e.memset(bcp[:, :, 0:3], 0.0)
            e.memset(xp[:, :, 0:3], 0.0).then_inc(zeroed, 1)
            for i in range(0, TT, 2):
                e.wait_ge(uf_done, l * TT + (i + 1))
                core.apart(e)
                e.tensor_copy(u_hi[:, :, i * P:(i + 1) * P], uf[:, i, :].rearrange("p (k c) -> p k c", k=KD))\
                    .then_inc(uhi_done, 1)
            e.wait_ge(w_lo, (l + 1) * MB_PIECES)
            e.wait_ge(split_la, l + 1)

            def r_build(i, half):
                t0 = slice(half * (P // 2), (half + 1) * (P // 2))
                e.tensor_tensor(r_hi[:, t0, :], la_hi[:, i, :].unsqueeze(1).to_broadcast([P, P // 2, H2]),
                                tri_th[:, t0, :], ALU.mult).then_inc(rhi_done, 1)

            def conv_bc(g):
                e.wait_ge(bc_ev, g + 1)
                core.apart(e)
                w = par[0:NS, MB_BCW:MB_BCB].rearrange("p (c k) -> p c k", c=2)
                part = [ysq[0:NS, 2 * k + 2:2 * k + 4, :] for k in range(TAPS - 1)]
                for k in range(TAPS - 1):
                    x = e.tensor_tensor(part[k], bcp[:, :, k:k + P], w[:, :, k].unsqueeze(2).to_broadcast([NS, 2, P]), ALU.mult)
                x.then_inc(pool_own, 1)
                e.wait_ge(pool_own, 2 * g + 2)
                core.apart(e)
                e.tensor_tensor(part[0], part[0], part[1], ALU.add)
                e.tensor_tensor(cbc[:], cbc[:], part[2], ALU.add).then_inc(pool_own, 1)
                e.wait_ge(pool_own, 2 * g + 3)
                core.apart(e)
                e.tensor_tensor(cbc[:], cbc[:], part[0], ALU.add).then_inc(acc_bc, 1)

            def sum_squares(g):
                e.wait_ge(ysq_done, g + 1)
                for k, half in enumerate((4, 2, 1)):
                    e.tensor_tensor(ysq[:, 0:half, :], ysq[:, 0:half, :], ysq[:, half:2 * half, :], ALU.add)\
                        .then_inc(ysum_done, 1)
                    e.wait_ge(ysum_done, 3 * g + (k + 1))

            def keep_halo(g):
                e.wait_ge(acc, 2 * (g + 1))
                e.wait_ge(acc_bc, g + 1)
                core.apart(e)
                e.tensor_copy(bcp[:, :, 0:3], bcp[:, :, P:P + 3])
                e.tensor_copy(xp[:, :, 0:3], xp[:, :, P:P + 3]).then_inc(halo, 1)

            def power(g):
                e.wait_ge(rv_done, g + 1)
                e.tensor_tensor(rs[:], rv[:], mhalf[:], ALU.pow).then_inc(pow_done, 1)

            conv_bc(l * TT)
            r_build(0, 0)
            r_build(0, 1)
            keep_halo(l * TT)
            e.wait_ge(prep, l + 1)

            def body(i, g, is_first, is_last):
                if not is_first:
                    sum_squares(g - 1)
                e.wait_ge(xc_done, 2 * (g + 1))
                e.tensor_tensor(dx, xc[:], par[:, MB_DCOL:MB_DCOL + JD].unsqueeze(2).to_broadcast([P, JD, P]), ALU.mult)\
                    .then_inc(dx_done, 1)
                if not is_first:
                    power(g - 1)
                    e.wait_ge(s_done, g)
                e.wait_ge(inter_mm, g + 1)
                if is_last:
                    e.sem_inc(ring_free, 1)
                e.tensor_tensor(heads(S[:]), heads(S[:]), edec[0:NS, i, :].unsqueeze(2).to_broadcast([NS, H2, 32]),
                                ALU.mult).then_inc(smul, 1)
                e.wait_ge(dx_done, g + 1)
                e.wait_ge(yi_done, g + 1)
                e.tensor_tensor(yi, yi, dx, ALU.add).then_inc(yid_done, 1)
                if not is_last:
                    e.wait_ge(diff, MB_EG * (g + 1))
                    r_build(i + 1, 0)
                    conv_bc(g + 1)
                    r_build(i + 1, 1)
                    keep_halo(g + 1)

            chunks(e, l, body)
            sum_squares(l * TT + TT - 1)
            power(l * TT + TT - 1)

    def pe(e):
        with e.Fori(0, LAYERS) as l:
            e.wait_ge(layer_open, l + 1)
            for i in range(TT):
                e.wait_ge(un_done, l * TT + i + 1)
                for k in range(KD):
                    x = e.transpose(ps[:, i, k * P:(k + 1) * P], un[:, i, k * P:(k + 1) * P], core.ident[:])
                x.then_inc(turned, 1)
            e.wait_ge(w_lo, l * MB_PIECES + KD)
            e.wait_ge(uf_done, (l + 1) * TT)
            e.wait_ge(ulo_done, (l + 1) * TT)
            core.apart(e)
            for i in range(TT):
                for k in range(KD):
                    for n, (a, b) in enumerate(((u_hi, wi_hi), (u_hi, wi_lo), (u_lo, wi_hi))):
                        x = e.matmul(ps[:, 2, i * H2:(i + 1) * H2], a[:, k, i * P:(i + 1) * P], b[:, k, MB_CDT:MB_CDT + H2],
                                     start=(k == 0 and n == 0), stop=(k == KD - 1 and n == 2))
            x.then_inc(dt_mm, 1)
            def project(i, bank, tiles, width, done):
                for n, f in enumerate(tiles):
                    for k in range(KD):
                        for m, (a, b) in enumerate(((wi_hi, u_hi), (wi_lo, u_hi), (wi_hi, u_lo))):
                            x = e.matmul(ps[0:width, bank, n * P:(n + 1) * P], a[:, k, f:f + width],
                                         b[:, k, ds(i * P, P)], start=(k == 0 and m == 0), stop=(k == KD - 1 and m == 2))
                x.then_inc(done, 1)

            def project_x(i, g, is_first):
                if not is_first:
                    e.wait_ge(sz_done, 2 * g)
                for q in range(2):
                    project(i, q, [MB_CX + P * j for j in range(4 * q, 4 * q + 4)], P, x_mm)
                e.wait_ge(x_ev, 2 * g + 1)
                core.apart(e)
                project(i, 0, [MB_CB, MB_CC], NS, bc_mm)

            def project_z(i, g):
                e.wait_ge(x_ev, 2 * g + 2)
                project(i, 1, [P * j for j in range(4)], P, z_mm)
                e.wait_ge(bc_ev, g + 1)
                project(i, 0, [P * j for j in range(4, 8)], P, z_mm)

            def out_project(g, first, end):
                e.wait_ge(ylo_done, g + 1)
                for j in range(first, end):
                    for m, (a, b) in enumerate(((y_hi, wo_hi), (y_hi, wo_lo), (y_lo, wo_hi))):
                        x = e.matmul(ps[:, 7, :], a[:, j, :], b[:, j, :], start=(j == 0 and m == 0),
                                     stop=(j == JD - 1 and m == 2))
                if end == JD:
                    x.then_inc(out_mm, 1)

            def sum_rows(g):
                e.wait_ge(ysum_done, 3 * g + 3)
                e.matmul(ps[:, 2, 384:385], ysq[:, 0, :], core.ones[:, 0:1], start=True, stop=True).then_inc(rms_mm, 1)

            project_x(0, l * TT, True)
            e.wait_ge(la_done, l + 1)
            la2 = la[:].rearrange("p i h -> p (i h)")
            e.matmul(ps[:, 3, 0:TT * H2], core.after[:], la2, start=True, stop=True)
            e.matmul(ps[:, 3, TT * H2:2 * TT * H2], core.ones[:], la2, start=True, stop=True)
            for i in range(TT):
                x = e.matmul(ps[0:H2, 4 + i // 4, (i % 4) * P:(i % 4 + 1) * P], la[:, i, :], core.tri[:], start=True, stop=True)
            x.then_inc(sums_mm, 1)
            project_z(0, l * TT)
            e.wait_ge(prep, l + 1)
            e.wait_ge(w_lo, (l + 1) * MB_PIECES)

            def body(i, g, is_first, is_last):
                e.wait_ge(xc_done, 2 * (g + 1))
                if not is_first:
                    e.wait_ge(yi_done, g)
                core.apart(e)
                for j in range(JD):
                    x = e.transpose(ps[:, 5 + j // 4, (j % 4) * P:(j % 4 + 1) * P], xc[:, j, :], core.ident[:])
                x.then_inc(xtr, 1)
                e.wait_ge(rhi_done, 2 * g + 1)
                e.wait_ge(rlo_done, g + 1)
                if not is_first:
                    e.wait_ge(s_done, g)
                for k in range(MB_EG):
                    if k >= 2:
                        e.wait_ge(exped, MB_EG * g + k - 1)
                    if k == MB_EG // 2:
                        e.wait_ge(rhi_done, 2 * g + 2)
                    for m, r in enumerate((r_hi, r_lo)):
                        x = e.matmul(ps[:, 3 + k % 2, :], core.after16[:], r[:, 16 * k:16 * k + 16, :].rearrange("p t h -> p (t h)"),
                                     start=(m == 0), stop=(m == 1))
                    x.then_inc(diff, 1)
                    if k == 1:
                        e.wait_ge(bcc_done, g + 1)
                        if not is_first:
                            e.wait_ge(ya_done, g)
                        core.apart(e)
                        e.transpose(ps[:, 2, 0:NS], bcc[:, 0, :], core.ident[0:NS, 0:NS])
                        e.matmul(ps[:, 2, P:2 * P], bcc[:, 0, :], bcc[:, 1, :], start=True, stop=True).then_inc(g_mm, 1)
                    if k >= 4 and not is_first:
                        out_project(g - 1, 2 * (k - 4), 2 * (k - 3))
                e.wait_ge(gm_done, g + 1)
                e.wait_ge(bt_done, g + 1)
                if not is_first:
                    sum_rows(g - 1)
                e.wait_ge(exped, MB_EG * (g + 1))
                for j in range(JD):
                    for m, c in enumerate((cum_hi, cum_lo)):
                        x = e.matmul(ps[:, 3 + j // 4, (j % 4) * P:(j % 4 + 1) * P], core.sel16[:, j, :], c[:, ds(i * P, P)],
                                     start=(m == 0), stop=(m == 1))
                x.then_inc(ecum_mm, 1)
                e.wait_ge(x_scaled, g + 1)
                for j in range(JD):
                    x = e.matmul(ps[:, 5 + j // 4, (j % 4) * P:(j % 4 + 1) * P], S[:, j * P:(j + 1) * P], bcc[:, 1, :],
                                 start=True, stop=True)
                x.then_inc(inter_mm, 1)
                e.wait_ge(ec_done, g + 1)
                for q in range(2):
                    x = e.matmul(ps[0:NS, 3 + q, :], btok[:], xe[:, q * 512:(q + 1) * 512], start=True, stop=True)
                x.then_inc(ds_mm, 1)
                if not is_last:
                    project_x(i + 1, g + 1, False)
                e.wait_ge(m_done, MB_EG * (g + 1))
                if not is_first:
                    e.wait_ge(h_done, g)
                for hh in range(H2):
                    bank = 7 if hh < 16 else 2
                    c = (hh // 4) % 4
                    x = e.matmul(ps[32 * (hh % 4):32 * (hh % 4) + 32, bank, c * P:(c + 1) * P],
                                 xdt[:, 32 * hh:32 * hh + 32], M[:, hh, :], start=True, stop=True)
                x.then_inc(intra_mm, 1)
                if not is_last:
                    project_z(i + 1, g + 1)

            chunks(e, l, body)
            out_project(l * TT + TT - 1, 0, JD)
            sum_rows(l * TT + TT - 1)

    t_kept, t_back, sum_done = sem("t_kept"), sem("t_back"), sem("sum_done")
    return dict(sp=sp, dve=dve, act=act, pe=pe, pool=pool, cx=cx, used=used)


FF_QEPS = 1e-5
FF_MAGIC = 1.5 * 2.0 ** 23
FF_RSQ = float(np.float32(1 / np.sqrt(D)))


def stage_ffn(core, ps):
    nc, ins, t = core.nc, core.ins, core.t
    cx = ExitStack()
    sb = lambda n, s, d=F32: core.sb("f_" + n, s, d, cx)
    used = []
    sem = lambda n: core.stage_sem("f_" + n, used)
    wn = sb("wn", [P, KD, D])
    low = sb("low", [P, KD, D])
    tern = sb("tern", [P, KD, D])
    ternT = sb("ternT", [P, KD, D], F16)
    had = sb("had", [P, KD, D], F16)
    asum, scale, half, nhalf = (sb(n, [P, KD]) for n in ("asum", "scale", "half", "nhalf"))
    diag = sb("diag", [P, KD, P])
    wscale = sb("wscale", [P, D])
    mv, rstd = sb("mv", [P, TT, 2]), sb("rstd", [P, TT])
    un = sb("un", [P, 2, D])
    u_hi, u_lo = sb("u_hi", [P, 2, D], F16), sb("u_lo", [P, 2, D], F16)
    amax, tscale, inv, mult = (sb(n, [P, TT]) for n in ("amax", "tscale", "inv", "mult"))
    minus_magic = sb("minus_magic", [P, 1])
    qa, qc = sb("qa", [P, D]), sb("qc", [P, 2, D])
    qT = sb("qT", [P, 2, D], F16)
    upd = sb("upd", [P, 2, D])

    w_in, had_in = sem("w_in"), sem("had_in")
    dve_own = sem("dve_own")
    var_done, sd_done, magic_set = sem("var_done"), sem("sd_done"), sem("magic_set")
    tern_done, wsc_done = sem("tern_done"), sem("wsc_done")
    w_tr, w_ev, wsc_mm = sem("w_tr"), sem("w_ev"), sem("wsc_mm")
    un_done, turned, hi_done, lo_done = (sem(n) for n in ("un_done", "turned", "hi_done", "lo_done"))
    h_mm, qa_done, q_done, q_tr, q_ev, o_mm, o_done, t_done = (
        sem(n) for n in ("h_mm", "qa_done", "q_done", "q_tr", "q_ev", "o_mm", "o_done", "t_done"))

    def rounds(*steps):
        for r in range(TT + max(lag for lag, _ in steps)):
            for lag, step in steps:
                if 0 <= r - lag < TT:
                    step(r - lag)

    def sp(e):
        e.dma_start(wn[:], ins["f_w"].rearrange("(j p) i -> p j i", p=P)).then_inc(w_in, 16)
        e.dma_start(had[:], ins["c_had"].rearrange("(k p) n -> p k n", p=P)).then_inc(had_in, 16)

    def dve(e):
        own = Chain(e, dve_own)
        for i in range(TT):
            x = e.bn_aggr(mv[:, i, :], core.stats[:, i, :])
        own(x)
        e.tensor_scalar(rstd[:], mv[:, :, 1], 1e-5, None, ALU.add).then_inc(var_done, 1)
        e.wait_ge(w_in, 16)
        own(e.tensor_reduce(asum[:], wn[:], AX.X, ALU.add, apply_absolute_value=True))
        own(e.tensor_scalar(scale[:], asum[:], 1.0 / D, FF_QEPS, ALU.mult, ALU.max))
        e.tensor_scalar(half[:], scale[:], 0.5, None, ALU.mult)
        own(e.tensor_scalar(nhalf[:], scale[:], -0.5, None, ALU.mult))
        e.wait_ge(sd_done, 1)
        own(e.reciprocal(rstd[:], rstd[:]))

        def weights(j):
            e.tensor_scalar(diag[:, j, :], core.ident[:], scale[:, j:j + 1], None, ALU.mult)
            own(e.tensor_scalar(low[:, j, :], wn[:, j, :], nhalf[:, j:j + 1], None, ALU.is_lt))
            e.scalar_tensor_tensor(out=tern[:, j, :], in0=wn[:, j, :], scalar=half[:, j:j + 1], in1=low[:, j, :],
                                   op0=ALU.is_gt, op1=ALU.subtract).then_inc(tern_done, 1)

        def normalise(i):
            if i >= 2:
                e.wait_ge(turned, i - 1)
            e.tensor_scalar(un[:, i % 2, :], t[:, i, :], mv[:, i, 0:1], rstd[:, i:i + 1], ALU.subtract, ALU.mult)\
                .then_inc(un_done, 1)
            if i < 2:
                weights(2 * i)
                weights(2 * i + 1)

        def low_part(i):
            e.wait_ge(hi_done, i + 1)
            if i >= 2:
                e.wait_ge(h_mm, i - 1)
            e.tensor_tensor(u_lo[:, i % 2, :], ps[:, i % 2, :], u_hi[:, i % 2, :], ALU.subtract).then_inc(lo_done, 1)

        def quantise(i):
            e.wait_ge(h_mm, i + 1)
            c = slice(i, i + 1)
            h = ps[:, 2 + i % 2, :]
            own(e.tensor_reduce(amax[:, c], h, AX.X, ALU.max, apply_absolute_value=True))
            own(e.tensor_scalar(tscale[:, c], amax[:, c], FF_RSQ, FF_QEPS, ALU.mult, ALU.max))
            own(e.tensor_scalar(tscale[:, c], tscale[:, c], 1.0 / 7, None, ALU.mult))
            own(e.reciprocal(inv[:, c], tscale[:, c]))
            own(e.tensor_scalar(mult[:, c], inv[:, c], FF_RSQ, None, ALU.mult))
            e.tensor_scalar(qa[:], h, mult[:, c], FF_MAGIC, ALU.mult, ALU.add).then_inc(qa_done, 1)
            e.wait_ge(qa_done, i + 1)
            if i >= 2:
                e.wait_ge(q_tr, i - 1)
            e.tensor_scalar(qc[:, i % 2, :], qa[:], FF_MAGIC - 8, FF_MAGIC + 7, ALU.max, ALU.min).then_inc(q_done, 1)

        def update(i):
            e.wait_ge(o_mm, i + 1)
            if i == 0:
                e.wait_ge(wsc_done, 1)
            if i >= 2:
                e.wait_ge(t_done, i - 1)
            e.scalar_tensor_tensor(out=upd[:, i % 2, :], in0=ps[:, 6 + i % 2, :], scalar=tscale[:, i:i + 1],
                                   in1=wscale[:], op0=ALU.mult, op1=ALU.mult).then_inc(o_done, 1)

        def statistics(i):
            e.wait_ge(t_done, i + 1)
            e.bn_stats(core.stats[:, i, :], t[:, i, :])

        rounds((0, normalise), (1, low_part), (2, quantise), (3, update), (4, statistics))

    def act(e):
        e.wait_ge(var_done, 1)
        e.activation(rstd[:], rstd[:], ACT.Sqrt).then_inc(sd_done, 1)
        e.wait_ge(magic_set, 1)

        def high_part(i):
            e.wait_ge(turned, i + 1)
            if i >= 2:
                e.wait_ge(h_mm, i - 1)
            e.activation(u_hi[:, i % 2, :], ps[:, i % 2, :], ACT.Copy).then_inc(hi_done, 1)
            if i == 0:
                for k in range(KD):
                    e.wait_ge(w_tr, k + 1)
                    e.activation(ternT[:, k, :], ps[:, 4 + k, :], ACT.Copy).then_inc(w_ev, 1)
                e.wait_ge(wsc_mm, 1)
                e.activation(wscale[:], ps[:, 2, :], ACT.Copy).then_inc(wsc_done, 1)

        def quantised(i):
            e.wait_ge(q_tr, i + 1)
            if i >= 2:
                e.wait_ge(o_mm, i - 1)
            e.activation(qT[:, i % 2, :], ps[:, 4 + i % 2, :], ACT.Identity, bias=minus_magic[:]).then_inc(q_ev, 1)

        rounds((0, high_part), (2, quantised))

    def pool(e):
        e.memset(minus_magic[:], -FF_MAGIC).then_inc(magic_set, 1)
        for i in range(TT):
            e.wait_ge(o_done, i + 1)
            e.tensor_tensor(t[:, i, :], t[:, i, :], upd[:, i % 2, :], ALU.add).then_inc(t_done, 1)

    def pe(e):
        def turn(i):
            e.wait_ge(un_done, i + 1)
            if i >= 2:
                e.wait_ge(lo_done, i - 1)
            for k in range(KD):
                x = e.transpose(ps[:, i % 2, k * P:(k + 1) * P], un[:, i % 2, k * P:(k + 1) * P], core.ident[:])
            x.then_inc(turned, 1)
            if i == 1:
                for k in range(KD):
                    for j in range(KD):
                        e.wait_ge(tern_done, j + 1)
                        x = e.transpose(ps[:, 4 + k, j * P:(j + 1) * P], tern[:, j, k * P:(k + 1) * P], core.ident[:])
                    x.then_inc(w_tr, 1)
                for j in range(KD):
                    x = e.matmul(ps[:, 2, j * P:(j + 1) * P], core.ones[:], diag[:, j, :], start=True, stop=True)
                x.then_inc(wsc_mm, 1)

        def rotate(i):
            e.wait_ge(lo_done, i + 1)
            if i == 0:
                e.wait_ge(had_in, 16)
                e.wait_ge(wsc_done, 1)
            if i >= 2:
                e.wait_ge(q_done, i - 1)
            for k in range(KD):
                for m, a in enumerate((u_hi, u_lo)):
                    x = e.matmul(ps[:, 2 + i % 2, :], a[:, i % 2, k * P:(k + 1) * P], had[:, k, :],
                                 start=(k == 0 and m == 0), stop=(k == KD - 1 and m == 1))
            x.then_inc(h_mm, 1)

        def turn_back(i):
            e.wait_ge(q_done, i + 1)
            if i >= 2:
                e.wait_ge(q_ev, i - 1)
            for k in range(KD):
                x = e.transpose(ps[:, 4 + i % 2, k * P:(k + 1) * P], qc[:, i % 2, k * P:(k + 1) * P], core.ident[:])
            x.then_inc(q_tr, 1)

        def multiply(i):
            e.wait_ge(q_ev, i + 1)
            if i >= 2:
                e.wait_ge(o_done, i - 1)
            for k in range(KD):
                x = e.matmul(ps[:, 6 + i % 2, :], qT[:, i % 2, k * P:(k + 1) * P], ternT[:, k, :], start=(k == 0),
                             stop=(k == KD - 1))
            x.then_inc(o_mm, 1)

        rounds((0, turn), (3, multiply), (1, rotate), (2, turn_back))

    return dict(sp=sp, dve=dve, act=act, pe=pe, pool=pool, cx=cx, used=used)


AT_RMS_EPS = 1.1920929e-07
AT_LN_EPS = 1e-5
AT_HN = 4
AT_HW = DI // AT_HN
AT_DPROJ = 2 * DI + AT_HN + 2 * AT_HN * NS
AT_CX, AT_CDT, AT_CBC = DI, 2 * DI, 2 * DI + AT_HN
AT_PIECES = 6
AT_RAWS = 4


def stage_l3(core, ps):
    nc, ins, t = core.nc, core.ins, core.t
    cx = ExitStack()
    sb = lambda n, s, d=F32: core.sb("ab_" + n, s, d, cx)
    used = []
    sem = lambda n: core.stage_sem("a_" + n, used)
    wi_hi, wi_lo = sb("wi_hi", [P, KD, AT_DPROJ], F16), sb("wi_lo", [P, KD, AT_DPROJ], F16)
    wo_hi, wo_lo = sb("wo_hi", [P, JD, D], F16), sb("wo_lo", [P, JD, D], F16)
    inb, outb = sb("inb", [P, AT_DPROJ]), sb("outb", [P, D])
    raw = [sb(f"raw{b}", [P, AT_DPROJ]) for b in range(AT_RAWS)]
    nw = sb("nw", [P, KD])
    alog, dpar, dtb = sb("alog", [P, AT_HN]), sb("dpar", [P, AT_HN]), sb("dtb", [P, AT_HN])
    nega, dtbb = sb("nega", [P, AT_HN]), sb("dtbb", [P, AT_HN])
    mv = sb("mv", [P, TT, 2])
    rstd, v2, r2, shift = (sb(n, [P, TT]) for n in ("rstd", "v2", "r2", "shift"))
    un = sb("un", [P, 2, D])
    u_hi, u_lo = sb("u_hi", [P, KD, TOK], F16), sb("u_lo", [P, KD, TOK], F16)
    small = lambda n, d=F32: sb(n, [P, TT, AT_HN], d)
    dtx, dtn, dtl, dt, la, dend, ecum, edec, dte = (small(n) for n in "dtx dtn dtl dt la dend ecum edec dte".split())
    la_hi, la_lo = small("la_hi", F16), small("la_lo", F16)
    bc = sb("bc", [P, 2 * AT_HN * NS])
    bct = sb("bct", [NS, 2 * AT_HN, P])
    r_hi, r_lo = sb("r_hi", [P, AT_HN, P], F16), sb("r_lo", [P, AT_HN, P], F16)
    E, gm, M = sb("E", [P, AT_HN, P]), sb("gm", [P, AT_HN, P]), sb("M", [P, AT_HN, P])
    xs, xdt, xe, dx = (sb(n, [P, DI]) for n in ("xs", "xdt", "xe", "dx"))
    zt, th, sz, y1, y = (sb(n, [P, DI]) for n in ("zt", "th", "sz", "y1", "y"))
    S = sb("S", [NS, DI])
    yT_hi, yT_lo = sb("yT_hi", [P, DI], F16), sb("yT_lo", [P, DI], F16)

    dve_own, act_own = sem("dve_own"), sem("act_own")
    par_in, rstd_done = sem("par_in"), sem("rstd_done")
    nw_in = core.sem("a_nw_in")
    raw_in = [core.sem(f"a_raw_in{b}") for b in range(AT_RAWS)]
    names = """w_hi w_lo var_done sd_done un_done turned hi_done lo_done dt_mm dtn_done dt_log nega_done la_done sums_mm
        sums_exp prep bias_added zeroed bc_mm x_mm z_mm bc_done x_done z_ev thz_done sz_done bct_mm bct_done g_mm
        r_done diff gm_done exped m_done inter_mm y1_done smul ds_mm s_done intra_mm xdt_done xe_done dx_done y2_done
        y3_done y_done yt_mm yhi_done ylo_done out_mm t_done""".split()
    s = {n: sem(n) for n in names}
    (w_hi, w_lo, var_done, sd_done, un_done, turned, hi_done, lo_done, dt_mm, dtn_done, dt_log, nega_done, la_done,
     sums_mm, sums_exp, prep, bias_added, zeroed, bc_mm, x_mm, z_mm, bc_done, x_done, z_ev, thz_done, sz_done, bct_mm,
     bct_done, g_mm, r_done, diff, gm_done, exped, m_done, inter_mm, y1_done, smul, ds_mm, s_done, intra_mm, xdt_done,
     xe_done, dx_done, y2_done, y3_done, y_done, yt_mm, yhi_done, ylo_done, out_mm, t_done) = (s[n] for n in names)

    def chunks(e, body):
        body(0, True, False)
        with e.Fori(1, TT - 1) as i:
            body(i, False, False)
        body(TT - 1, False, True)

    def two(a, b):
        return ps[:, a:b, :].rearrange("p b n -> p (b n)")

    def per_head(x, i):
        return x[:, i, :].unsqueeze(2).to_broadcast([P, AT_HN, AT_HW])

    def hv(x):
        return x.rearrange("p (h q) -> p h q", h=AT_HN)

    PARS = ("a_in_b", "a_out_b", "a_alog", "a_D", "a_dtb")

    def sp_ahead(e):
        e.dma_start(nw[:], ins["a_nw"]).then_inc(nw_in, 16)
        for n in range(KD):
            e.dma_start(raw[n][:], ins["a_in_w"][n * P:(n + 1) * P, :]).then_inc(raw_in[n], 16)

    def sp(e):
        for dst, name in zip((inb, outb, alog, dpar, dtb), PARS):
            e.dma_start(dst[:], ins[name].partition_broadcast(P)).then_inc(par_in, 16)
        for n in range(KD, AT_PIECES):
            e.wait_ge(w_hi, n - AT_RAWS + 1)
            e.wait_ge(w_lo, n - AT_RAWS + 1)
            e.dma_start(raw[n % AT_RAWS][:, 0:4 * D].rearrange("p (j f) -> p j f", j=4),
                        ins["a_out_w"][(n - KD) * 512:(n - KD + 1) * 512, :].rearrange("(j p) f -> p j f", p=P))\
                .then_inc(raw_in[n % AT_RAWS], 16)
        e.wait_ge(w_hi, AT_PIECES)
        e.wait_ge(w_lo, AT_PIECES)

    PAR = 16 * len(PARS)

    def dve(e):
        own = Chain(e, dve_own)
        for i in range(TT):
            x = e.bn_aggr(mv[:, i, :], core.stats[:, i, :])
        own(x)
        e.tensor_scalar(rstd[:], mv[:, :, 1], AT_LN_EPS, None, ALU.add).then_inc(var_done, 1)
        e.wait_ge(sd_done, 1)
        own(e.reciprocal(rstd[:], rstd[:]))
        own(e.tensor_tensor(v2[:], rstd[:], rstd[:], ALU.mult))
        own(e.tensor_tensor(v2[:], v2[:], mv[:, :, 1], ALU.mult))
        e.tensor_scalar(r2[:], v2[:], AT_RMS_EPS, None, ALU.add).then_inc(var_done, 1)
        e.wait_ge(sd_done, 2)
        own(e.reciprocal(r2[:], r2[:]))
        own(e.tensor_tensor(rstd[:], rstd[:], r2[:], ALU.mult))
        e.scalar_tensor_tensor(out=shift[:], in0=mv[:, :, 0], scalar=-1.0, in1=rstd[:], op0=ALU.mult, op1=ALU.mult)\
            .then_inc(rstd_done, 1)
        lower(e, 0)
        for i in range(TT):
            low_part(e, i)
            if i in (1, 3, 6):
                lower(e, (i + 1) // 2)
        e.wait_ge(par_in, PAR)
        e.wait_ge(dt_mm, 1)
        own(e.tensor_tensor(dtbb[:], dtb[:], inb[:, AT_CDT:AT_CDT + AT_HN], ALU.add))
        own(e.tensor_tensor(dtx[:], ps[:, 6, 0:TT * AT_HN].rearrange("p (i h) -> p i h", i=TT),
                            dtbb[:].unsqueeze(1).to_broadcast([P, TT, AT_HN]), ALU.add))
        e.scalar_tensor_tensor(out=dtn[:], in0=dtx[:], scalar=-1.0, in1=dtx[:], op0=ALU.mult, op1=ALU.min)\
            .then_inc(dtn_done, 1)
        e.wait_ge(dt_log, 1)
        own(e.scalar_tensor_tensor(out=dt[:], in0=dtx[:], scalar=0.0, in1=dtl[:], op0=ALU.max, op1=ALU.add))
        e.wait_ge(nega_done, 1)
        e.tensor_tensor(la[:], dt[:], nega[:].unsqueeze(1).to_broadcast([P, TT, AT_HN]), ALU.mult).then_inc(la_done, 1)
        e.wait_ge(la_done, 1)
        own(e.tensor_copy(la_hi[:], la[:]))
        own(e.tensor_tensor(la_lo[:], la[:], la_hi[:], ALU.subtract))
        lower(e, 4)
        lower(e, 5)

        def take_bc(g):
            e.wait_ge(bc_mm, g + 1)
            e.tensor_tensor(bc[:], ps[:, 1, 0:2 * AT_HN * NS], inb[:, AT_CBC:AT_DPROJ], ALU.add).then_inc(bc_done, 1)

        def take_z(g):
            e.wait_ge(z_mm, g + 1)
            e.tensor_tensor(zt[:], two(4, 6), inb[:, 0:DI], ALU.add).then_inc(z_ev, 1)

        def gate(g):
            e.wait_ge(thz_done, g + 1)
            e.scalar_tensor_tensor(out=sz[:], in0=th[:], scalar=1.0, in1=zt[:], op0=ALU.add, op1=ALU.mult)\
                .then_inc(sz_done, 1)

        def take_x(i, g):
            e.wait_ge(x_mm, g + 1)
            e.tensor_tensor(xs[:], two(2, 4), inb[:, AT_CX:AT_CX + DI], ALU.add).then_inc(x_done, 1)
            e.wait_ge(x_done, g + 1)
            e.tensor_tensor(hv(xdt[:]), hv(xs[:]), per_head(dt, i), ALU.mult).then_inc(xdt_done, 1)

        def decays(i):
            for r, l in ((r_hi, la_hi), (r_lo, la_lo)):
                x = e.tensor_tensor(r[:], l[:, i, :].unsqueeze(2).to_broadcast([P, AT_HN, P]),
                                    core.tri16[:].unsqueeze(1).to_broadcast([P, AT_HN, P]), ALU.mult)
            x.then_inc(r_done, 1)

        take_bc(0)
        decays(0)
        take_z(0)
        gate(0)
        take_x(0, 0)
        e.wait_ge(sums_exp, 1)
        e.tensor_tensor(dte[:], dend[:], dt[:], ALU.mult).then_inc(prep, 1)

        def statistics(i, g):
            e.wait_ge(t_done, g + 1)
            core.apart(e)
            e.bn_stats(core.stats[:, i, :], t[:, i, :])

        def body(i, first, last):
            g = i
            e.wait_ge(g_mm, g + 1)
            e.tensor_tensor(gm[:], ps[:, 6, :].rearrange("p (h t) -> p h t", h=AT_HN),
                            core.tri[:].unsqueeze(1).to_broadcast([P, AT_HN, P]), ALU.mult).then_inc(gm_done, 1)
            e.wait_ge(gm_done, g + 1)
            e.wait_ge(exped, g + 1)
            e.tensor_tensor(M[:], E[:], gm[:], ALU.mult).then_inc(m_done, 1)
            e.wait_ge(inter_mm, g + 1)
            e.tensor_tensor(hv(y1[:]), hv(two(4, 6)), per_head(ecum, i), ALU.mult).then_inc(y1_done, 1)
            if not first:
                statistics(i - 1, g - 1)
            e.wait_ge(intra_mm, g + 1)
            e.wait_ge(y3_done, g + 1)
            e.tensor_tensor(y1[:], y1[:], two(2, 4), ALU.add).then_inc(y2_done, 1)
            e.wait_ge(y2_done, g + 1)
            e.tensor_tensor(y[:], y1[:], sz[:], ALU.mult).then_inc(y_done, 1)
            e.wait_ge(ds_mm, g + 1)
            e.wait_ge(smul, g + 1)
            e.tensor_tensor(S[:], S[:], ps[0:NS, 6:8, :].rearrange("p b n -> p (b n)"), ALU.add).then_inc(s_done, 1)
            if not last:
                take_bc(g + 1)
            e.wait_ge(yhi_done, g + 1)
            e.tensor_tensor(yT_lo[:], two(2, 4), yT_hi[:], ALU.subtract).then_inc(ylo_done, 1)
            if not last:
                e.wait_ge(y_done, g + 1)
                take_z(g + 1)
                gate(g + 1)
            if not last:
                e.wait_ge(diff, g + 1)
                decays(i + 1)
                e.wait_ge(dx_done, g + 1)
                e.wait_ge(xe_done, g + 1)
                take_x(i + 1, g + 1)
            e.wait_ge(out_mm, g + 1)
            e.scalar_tensor_tensor(out=t[:, i, :], in0=ps[:, 0, :], scalar=0.5, in1=t[:, i, :], op0=ALU.mult,
                                   op1=ALU.add).then_inc(t_done, 1)

        e.wait_ge(bias_added, 1)
        chunks(e, body)
        statistics(TT - 1, TT - 1)

    def upper(e, n):
        e.wait_ge(raw_in[n % AT_RAWS], (n // AT_RAWS + 1) * 16)
        if n < KD:
            e.activation(wi_hi[:, n, :], raw[n % AT_RAWS][:], ACT.Copy, scale=nw[:, n:n + 1]).then_inc(w_hi, 1)
        else:
            j = 4 * (n - KD)
            e.activation(wo_hi[:, j:j + 4, :], raw[n % AT_RAWS][:, 0:4 * D].rearrange("p (j f) -> p j f", j=4), ACT.Copy)\
                .then_inc(w_hi, 1)

    def lower(e, n):
        e.wait_ge(w_hi, n + 1)
        if n < KD:
            e.scalar_tensor_tensor(out=wi_lo[:, n, :], in0=raw[n % AT_RAWS][:], scalar=nw[:, n:n + 1], in1=wi_hi[:, n, :],
                                   op0=ALU.mult, op1=ALU.subtract).then_inc(w_lo, 1)
        else:
            j = 4 * (n - KD)
            e.tensor_tensor(wo_lo[:, j:j + 4, :], raw[n % AT_RAWS][:, 0:4 * D].rearrange("p (j f) -> p j f", j=4),
                            wo_hi[:, j:j + 4, :], ALU.subtract).then_inc(w_lo, 1)

    def low_part(e, i):
        e.wait_ge(hi_done, i + 1)
        e.tensor_tensor(u_lo[:, :, i * P:(i + 1) * P], ps[:, i % 4, :].rearrange("p (k c) -> p k c", k=KD),
                        u_hi[:, :, i * P:(i + 1) * P], ALU.subtract).then_inc(lo_done, 1)

    def act(e):
        own = Chain(e, act_own)
        e.wait_ge(nw_in, 16)
        e.wait_ge(var_done, 1)
        e.activation(rstd[:], rstd[:], ACT.Sqrt).then_inc(sd_done, 1)
        e.wait_ge(var_done, 2)
        e.activation(r2[:], r2[:], ACT.Sqrt).then_inc(sd_done, 1)
        upper(e, 0)
        e.wait_ge(rstd_done, 1)

        def normalise(i):
            if i >= 2:
                e.wait_ge(turned, i - 1)
            e.activation(un[:, i % 2, :], t[:, i, :], ACT.Identity, bias=shift[:, i:i + 1], scale=rstd[:, i:i + 1])\
                .then_inc(un_done, 1)

        normalise(0)
        for i in range(TT):
            if i < TT - 1:
                normalise(i + 1)
            if i == 0:
                upper(e, 1)
            e.wait_ge(turned, i + 1)
            e.activation(u_hi[:, :, i * P:(i + 1) * P], ps[:, i % 4, :].rearrange("p (k c) -> p k c", k=KD), ACT.Copy)\
                .then_inc(hi_done, 1)
            if i in (1, 3):
                upper(e, (i + 3) // 2)
        e.wait_ge(par_in, PAR)
        own(e.activation(nega[:], alog[:], ACT.Exp))
        e.mul(nega[:], nega[:], -1.0).then_inc(nega_done, 1)
        e.wait_ge(dtn_done, 1)
        own(e.activation(dtl[:], dtn[:], ACT.Exp))
        e.activation(dtl[:], dtl[:], ACT.Ln, bias=1.0).then_inc(dt_log, 1)
        upper(e, 4)
        upper(e, 5)

        def tanh_z(g):
            e.wait_ge(z_ev, g + 1)
            e.activation(th[:], zt[:], ACT.Tanh, scale=0.5).then_inc(thz_done, 1)

        tanh_z(0)
        e.wait_ge(sums_mm, 1)
        for n, d in enumerate((dend, ecum, edec)):
            x = e.activation(d[:], ps[:, 7, 32 * n:32 * n + 32].rearrange("p (i h) -> p i h", i=TT), ACT.Exp)
        x.then_inc(sums_exp, 1)

        def body(i, first, last):
            g = i
            e.wait_ge(bct_mm, g + 1)
            e.activation(bct[:], ps[0:NS, 6:8, :].rearrange("p b (c t) -> p (b c) t", t=P), ACT.Copy).then_inc(bct_done, 1)
            e.wait_ge(diff, g + 1)
            e.activation(E[:], ps[:, 1, :].rearrange("p (h t) -> p h t", h=AT_HN), ACT.Exp).then_inc(exped, 1)
            e.wait_ge(yt_mm, g + 1)
            e.activation(yT_hi[:], two(2, 4), ACT.Copy).then_inc(yhi_done, 1)
            if not last:
                tanh_z(g + 1)

        chunks(e, body)

    def pool(e):
        e.memset(S[:], 0.0).then_inc(zeroed, 1)
        e.wait_ge(zeroed, 1)
        e.wait_ge(un_done, TT)
        e.wait_ge(par_in, PAR)
        e.tensor_tensor(t[:], t[:], outb[:].unsqueeze(1).to_broadcast([P, TT, D]), ALU.add).then_inc(bias_added, 1)
        e.wait_ge(prep, 1)

        def body(i, first, last):
            g = i
            e.wait_ge(x_done, g + 1)
            e.tensor_tensor(hv(xe[:]), hv(xs[:]), per_head(dte, i), ALU.mult).then_inc(xe_done, 1)
            e.tensor_tensor(hv(dx[:]), hv(xs[:]), dpar[:].unsqueeze(2).to_broadcast([P, AT_HN, AT_HW]), ALU.mult)\
                .then_inc(dx_done, 1)
            e.wait_ge(y1_done, g + 1)
            e.wait_ge(dx_done, g + 1)
            e.tensor_tensor(y1[:], y1[:], dx[:], ALU.add).then_inc(y3_done, 1)
            if not first:
                e.wait_ge(s_done, g)
            e.tensor_tensor(hv(S[:]), hv(S[:]), edec[0:NS, i, :].unsqueeze(2).to_broadcast([NS, AT_HN, AT_HW]), ALU.mult)\
                .then_inc(smul, 1)

        chunks(e, body)

    def pe(e):
        for i in range(TT):
            e.wait_ge(un_done, i + 1)
            if i >= 4:
                e.wait_ge(lo_done, i - 3)
            for k in range(KD):
                x = e.transpose(ps[:, i % 4, k * P:(k + 1) * P], un[:, i % 2, k * P:(k + 1) * P], core.ident[:])
            x.then_inc(turned, 1)
        e.wait_ge(w_lo, KD)
        e.wait_ge(lo_done, TT)
        for i in range(TT):
            for k in range(KD):
                for m, (a, b) in enumerate(((u_hi, wi_hi), (u_hi, wi_lo), (u_lo, wi_hi))):
                    x = e.matmul(ps[:, 6, i * AT_HN:(i + 1) * AT_HN], a[:, k, i * P:(i + 1) * P], b[:, k, AT_CDT:AT_CDT + AT_HN],
                                 start=(k == 0 and m == 0), stop=(k == KD - 1 and m == 2))
        x.then_inc(dt_mm, 1)
        def project(i, out, col, width):
            for k in range(KD):
                for m, (a, b) in enumerate(((u_hi, wi_hi), (u_hi, wi_lo), (u_lo, wi_hi))):
                    x = e.matmul(out, a[:, k, ds(i * P, P)], b[:, k, col:col + width],
                                 start=(k == 0 and m == 0), stop=(k == KD - 1 and m == 2))
            return x

        def project_bc(i):
            project(i, ps[:, 1, 0:2 * AT_HN * NS], AT_CBC, 2 * AT_HN * NS).then_inc(bc_mm, 1)

        def project_z(i, half):
            x = project(i, ps[:, 4 + half, :], 512 * half, 512)
            if half:
                x.then_inc(z_mm, 1)

        def project_x(i):
            project(i, ps[:, 2, :], AT_CX, 512)
            project(i, ps[:, 3, :], AT_CX + 512, 512).then_inc(x_mm, 1)

        project_bc(0)
        for half in range(2):
            project_z(0, half)
        project_x(0)
        e.wait_ge(la_done, 1)
        la2 = la[:].rearrange("p i h -> p (i h)")
        for n, w in enumerate((core.after, core.tri, core.ones)):
            x = e.matmul(ps[:, 7, 32 * n:32 * n + 32], w[:], la2, start=True, stop=True)
        x.then_inc(sums_mm, 1)

        def body(i, first, last):
            g = i
            e.wait_ge(bc_done, g + 1)
            if first:
                e.wait_ge(sums_exp, 1)
                e.wait_ge(zeroed, 1)
            else:
                e.wait_ge(s_done, g)
            for c in range(2 * AT_HN):
                x = e.transpose(ps[0:NS, 6 + c // 4, (c % 4) * P:(c % 4 + 1) * P], bc[:, c * NS:(c + 1) * NS], core.ident[:])
            x.then_inc(bct_mm, 1)
            e.wait_ge(r_done, g + 1)
            for m, r in enumerate((r_hi, r_lo)):
                x = e.matmul(ps[:, 1, :], core.after16[:], r[:].rearrange("p h t -> p (h t)"), start=(m == 0), stop=(m == 1))
            x.then_inc(diff, 1)
            e.wait_ge(bct_done, g + 1)
            for h in range(AT_HN):
                x = e.matmul(ps[:, 6, h * P:(h + 1) * P], bct[:, 2 * h, :], bct[:, 2 * h + 1, :], start=True, stop=True)
            x.then_inc(g_mm, 1)
            e.wait_ge(z_ev, g + 1)
            for h in range(AT_HN):
                x = e.matmul(ps[:, 4 + h // 2, (h % 2) * AT_HW:(h % 2 + 1) * AT_HW], bct[:, 2 * h + 1, :], S[:, h * AT_HW:(h + 1) * AT_HW],
                             start=True, stop=True)
            x.then_inc(inter_mm, 1)
            e.wait_ge(xdt_done, g + 1)
            e.wait_ge(m_done, g + 1)
            for h in range(AT_HN):
                x = e.matmul(ps[:, 2 + h // 2, (h % 2) * AT_HW:(h % 2 + 1) * AT_HW], M[:, h, :], xdt[:, h * AT_HW:(h + 1) * AT_HW],
                             start=True, stop=True)
            x.then_inc(intra_mm, 1)
            e.wait_ge(xe_done, g + 1)
            for h in range(AT_HN):
                x = e.matmul(ps[0:NS, 6 + h // 2, (h % 2) * AT_HW:(h % 2 + 1) * AT_HW], bc[:, 2 * h * NS:(2 * h + 1) * NS],
                             xe[:, h * AT_HW:(h + 1) * AT_HW], start=True, stop=True)
            x.then_inc(ds_mm, 1)
            if not last:
                project_bc(i + 1)
                e.wait_ge(y1_done, g + 1)
                project_z(i + 1, 0)
            e.wait_ge(y_done, g + 1)
            core.apart(e)
            for j in range(JD):
                x = e.transpose(ps[:, 2 + j // 4, (j % 4) * P:(j % 4 + 1) * P], y[:, j * P:(j + 1) * P], core.ident[:])
            x.then_inc(yt_mm, 1)
            if not last:
                project_z(i + 1, 1)
            e.wait_ge(ylo_done, g + 1)
            if not first:
                e.wait_ge(t_done, g)
            for j in range(JD):
                for m, (a, b) in enumerate(((yT_hi, wo_hi), (yT_hi, wo_lo), (yT_lo, wo_hi))):
                    x = e.matmul(ps[:, 0, :], a[:, j * P:(j + 1) * P], b[:, j, :], start=(j == 0 and m == 0),
                                 stop=(j == JD - 1 and m == 2))
            x.then_inc(out_mm, 1)
            if not last:
                project_x(i + 1)

        chunks(e, body)

    return dict(sp_ahead=sp_ahead, sp=sp, dve=dve, act=act, pe=pe, pool=pool, cx=cx, used=used)


EX_F = 2048
EX_FB = EX_F // P
EX_GB = 4
EX_FG = EX_FB // EX_GB
EX_PIECES = 8
EX_MAGIC = 1.5 * 2.0 ** 23
EX_LN_EPS = 1e-5
EX_FIRST_AT = (1, 2, 5, 6)
EX_MIX_AT = 6
EX_RAWS = 4


def stage_moe(core, ps):
    nc, ins, t = core.nc, core.ins, core.t
    cx = ExitStack()
    sb = lambda n, s, d=F32: core.sb("eb_" + n, s, d, cx)
    used = []
    sem = lambda n: core.stage_sem("e_" + n, used)
    w_hi, w_lo = [sb("w_hi0", [P, EX_PIECES, EX_F], F16)], [sb("w_lo0", [P, EX_PIECES, EX_F], F16)]
    raw = [sb(f"raw{b}", [P, EX_F])[:] for b in range(2)]
    un = sb("un", [P, TT, D])
    room = un[:].rearrange("p i f -> p (i f)")
    raw += [room[:, b * EX_F:(b + 1) * EX_F] for b in range(2)]
    w_hi.append(sb("w_hi1", [P, EX_PIECES, EX_F], F16))
    w_lo.append(sb("w_lo1", [P, EX_PIECES, EX_F], F16))
    gw = sb("gw", [P, KD, E])
    b1, b2 = sb("b1", [P, E, EX_FB]), sb("b2", [E, D])
    iota = sb("iota", [P, E])
    mv, rstd = sb("mv", [P, TT, 2]), sb("rstd", [P, TT])
    lg, pr, top, pos, pk = (sb(n, [P, TT, E]) for n in ("lg", "pr", "top", "pos", "pk"))
    pick = [sb(f"pick{k}", [P, TT, E]) for k in range(TOPK)]
    mask, tot = sb("mask", [P, TT, E]), sb("tot", [P, TT, E])
    topi, topf = sb("topi", [P, TT, E], U32), sb("topf", [P, TT, E])
    red, inv = sb("red", [P, TT]), sb("inv", [P, TT])
    before = sb("before", [P, TT + 1, E])
    nb, cum, first, first_slot = (sb(n, [P, E]) for n in ("nb", "cum", "first", "first_slot"))
    plan = sb("plan", [P, 2 * E + 1], U32)
    slotf, slot = sb("slotf", [P, TOPK, TT]), sb("slot", [P, TOPK, TT], U32)
    xg, x_hi, x_lo = sb("xg", [P, D]), sb("x_hi", [P, KD, P], F16), sb("x_lo", [P, KD, P], F16)
    hb = sb("hb", [P, 2, EX_GB * P])
    h_hi, h_lo = sb("h_hi", [P, EX_FG, EX_GB * P], F16), sb("h_lo", [P, EX_FG, EX_GB * P], F16)
    y = sb("y", [P, D])
    xs_dram, ys_dram = core.xs_dram, core.ys_dram

    names = """par_in var_done sd_done un_done turned0 copied0 logits max_done exp_done mask_done ranks table_done
         scattered xg_in turned xhi_done xlo_done whi_done wlo_done h_mm h_taken silu_done hhi_done
        hlo_done y_mm y_ev y_out expert_done t_done y_sent out_sent mix_done mix_turned mix_ev b2_mm b2_done dve_own act_own""".split()
    s_ = {n: sem(n) for n in names}
    (par_in, var_done, sd_done, un_done, turned0, copied0, logits, max_done, exp_done, mask_done, ranks, table_done,
     scattered, xg_in, turned, xhi_done, xlo_done, whi_done, wlo_done, h_mm, h_taken, silu_done,
     hhi_done, hlo_done, y_mm, y_ev, y_out, expert_done, t_done, y_sent, out_sent, mix_done, mix_turned, mix_ev, b2_mm, b2_done, dve_own, act_own) = \
        (s_[n] for n in names)
    raw_in = [core.sem(f"e_raw_in{b}") for b in range(EX_RAWS)]
    back = [sem(f"back{b}") for b in range(TT)]

    PARS = ((gw, "e_gw"), (b1, "e_b1"), (b2, "e_b2"), (iota, "c_iota"))
    PAR = 16 * len(PARS)
    H_TAKEN0, HLO0, YMM0, YEV0, YSENT0, EXPERT0 = EX_FG, 2, 1, 1, 1, 1

    def experts(e, piece, block, end):
        def body(x, side, last):
            count = e.value_load(plan[0:1, ds(x, 1)], min_val=0, max_val=BLOCKS)
            start = e.value_load(plan[0:1, ds(x + E, 1)], min_val=0, max_val=FILLED - 2)
            with e.Fori(0, EX_PIECES // EX_RAWS) as i:
                for q in range(2):
                    if piece and not last:
                        for n in (2 * q, 2 * q + 1):
                            piece(x + 1, 1 - side, i * EX_RAWS + n, n, x * (EX_PIECES // EX_RAWS) + i)
                    with e.If(i * 2 + q < count):
                        block(x, side, start + (i * 2 + q))
            with e.Fori(EX_PIECES // 2, BLOCKS) as b:
                with e.If(b < count):
                    block(x, side, start + b)
            if end:
                end(x)

        with e.Fori(0, E // 2 - 1) as i:
            body(i * 2, 0, False)
            body(i * 2 + 1, 1, False)
        body(E - 2, 0, False)
        body(E - 1, 1, True)

    def load(e, m, q):
        e.dma_start(raw[q], ins["e_w"][ds(m * P, P), :]).then_inc(raw_in[q], 16)

    def sp_ahead(e):
        for m in range(2):
            load(e, m, m)

    def sp(e):
        for dst, name in PARS:
            e.dma_start(dst[:], ins[name]).then_inc(par_in, 16)
        for m in range(2, EX_PIECES):
            e.wait_ge(wlo_done, m - 1)
            load(e, m, m % 2)
        for q in range(EX_RAWS):
            if q < 2:
                e.wait_ge(wlo_done, EX_PIECES - 1 + q)
            if q == 0:
                e.wait_ge(scattered, 16 * TT * TOPK)
                e.wait_ge(xg_in, 16)
            load(e, EX_PIECES + q, q)
        with e.Fori(EX_PIECES // EX_RAWS + 1, E * EX_PIECES // EX_RAWS) as i:
            for q in range(EX_RAWS):
                e.wait_ge(wlo_done, i * EX_RAWS + (q - EX_RAWS + 1))
                load(e, i * EX_RAWS + q, q)
        for i in range(TT):
            e.wait_ge(t_done, TOPK * (i + 1))
            e.dma_start(core.out[i * P:(i + 1) * P, :], t[:, i, :]).then_inc(out_sent, 16)
        e.wait_ge(out_sent, 16 * TT)

    def dve(e):
        own = Chain(e, dve_own)
        e.sem_inc(hlo_done, HLO0)
        e.sem_inc(y_ev, YEV0)
        for i in range(TT):
            x = e.bn_aggr(mv[:, i, :], core.stats[:, i, :])
        own(x)
        e.tensor_scalar(rstd[:], mv[:, :, 1], EX_LN_EPS, None, ALU.add).then_inc(var_done, 1)
        e.wait_ge(sd_done, 1)
        own(e.reciprocal(rstd[:], rstd[:]))
        for i in range(TT):
            e.tensor_scalar(un[:, i, :], t[:, i, :], mv[:, i, 0:1], rstd[:, i:i + 1], ALU.subtract, ALU.mult)\
                .then_inc(un_done, 1)
        for n in range(len(EX_FIRST_AT)):
            lower(e, 0, 0, n, n % 2)
        wide = lambda x: x.unsqueeze(2).to_broadcast([P, TT, E])
        e.wait_ge(logits, 1)
        own(e.tensor_copy(lg[:], ps[:, 7, 0:TT * E].rearrange("p (i x) -> p i x", i=TT)))
        own(e.tensor_reduce(red[:], lg[:], AX.X, ALU.max))
        e.tensor_tensor(lg[:], lg[:], wide(red[:]), ALU.subtract).then_inc(max_done, 1)
        e.wait_ge(exp_done, 1)
        own(e.tensor_reduce(inv[:], pr[:], AX.X, ALU.add))
        own(e.reciprocal(inv[:], inv[:]))
        own(e.tensor_tensor(pr[:], pr[:], wide(inv[:]), ALU.mult))
        for i in range(TT):
            x = e.max(top[:, i, :], pr[:, i, :])
        own(x)
        for i in range(TT):
            x = e.max_index(topi[:, i, :], top[:, i, :], pr[:, i, :])
        own(x)
        own(e.tensor_copy(topf[:], topi[:]))
        e.wait_ge(par_in, PAR)
        for k in range(TOPK):
            x = e.tensor_tensor(pick[k][:], iota[:].unsqueeze(1).to_broadcast([P, TT, E]), wide(topf[:, :, k]), ALU.is_equal)
        own(x)
        e.tensor_tensor(mask[:], pick[0][:], pick[1][:], ALU.add).then_inc(mask_done, 1)
        own(e.memset(before[:, 0, :], 0.0))
        e.wait_ge(ranks, 1)
        own(e.tensor_copy(tot[:], ps[:, 6, 0:TT * E].rearrange("p (i x) -> p i x", i=TT)))
        for i in range(TT):
            own(e.tensor_tensor(before[:, i + 1, :], before[:, i, :], tot[:, i, :], ALU.add))
        own(e.tensor_scalar(nb[:], before[:, TT, :], 1.0 / P, 0.5 - 0.5 / P, ALU.mult, ALU.add))
        own(e.tensor_scalar(nb[:], nb[:], EX_MAGIC, None, ALU.add))
        own(e.tensor_scalar(nb[:], nb[:], EX_MAGIC, None, ALU.subtract))
        own(e.tensor_tensor_scan(cum[:], core.ones[:, 0:E], nb[:], 0.0, ALU.mult, ALU.add))
        own(e.tensor_tensor(first[:], cum[:], nb[:], ALU.subtract))
        e.tensor_copy(plan[:, 0:E], nb[:])
        e.tensor_copy(plan[:, E:2 * E], first[:])
        own(e.tensor_copy(plan[:, 2 * E:], cum[:, E - 1:E]))
        own(e.tensor_scalar(first_slot[:], first[:], float(P), None, ALU.mult))
        own(e.tensor_tensor(pos[:], ps[:, 7, TT * E:2 * TT * E].rearrange("p (i x) -> p i x", i=TT), mask[:], ALU.subtract))
        own(e.tensor_tensor(pos[:], pos[:], before[:, 0:TT, :], ALU.add))
        own(e.tensor_tensor(pos[:], pos[:], first_slot[:].unsqueeze(1).to_broadcast([P, TT, E]), ALU.add))
        for k in range(TOPK):
            own(e.tensor_tensor(pk[:], pick[k][:], pos[:], ALU.mult))
            own(e.tensor_reduce(slotf[:, k, :], pk[:], AX.X, ALU.add))
        e.tensor_copy(slot[:], slotf[:]).then_inc(table_done, 1)
        e.wait_ge(table_done, 1)
        e.tensor_tensor(pick[0][:], pick[0][:], wide(top[:, :, 0]), ALU.mult)
        own(e.tensor_tensor(pick[1][:], pick[1][:], wide(top[:, :, 1]), ALU.mult))
        e.tensor_tensor(mask[:], pick[0][:], pick[1][:], ALU.add).then_inc(mix_done, 1)

        def add_bias(tiles):
            for i in tiles:
                e.wait_ge(b2_mm, i + 1)
                e.tensor_tensor(t[:, i, :], t[:, i, :], ps[:, i % 4, :], ALU.add).then_inc(b2_done, 1)

        for n in range(len(EX_FIRST_AT), EX_MIX_AT):
            lower(e, 0, 0, n, n % 2)
        add_bias(range(TT // 2))
        lower(e, 0, 0, EX_PIECES - 2, 0)
        add_bias(range(TT // 2, TT - 1))
        lower(e, 0, 0, EX_PIECES - 1, 1)
        add_bias((TT - 1,))
        e.wait_ge(b2_done, TT)
        e.sem_inc(h_taken, H_TAKEN0)
        lower_x(e, 0)

        def bias(x, s, j):
            e.wait_ge(h_mm, s * EX_FG + (j + 1))
            e.wait_ge(hlo_done, s * EX_FG + (j + 1))
            e.tensor_tensor(hb[:, j % 2, :].rearrange("p (c n) -> p c n", c=EX_GB),
                            ps[:, j, :].rearrange("p (c n) -> p c n", c=EX_GB),
                            b1[:, ds(x, 1), j * EX_GB:(j + 1) * EX_GB].rearrange("p o c -> p (o c)").unsqueeze(2)
                            .to_broadcast([P, EX_GB, P]), ALU.add).then_inc(h_taken, 1)

        def low(s, j):
            e.wait_ge(hhi_done, s * EX_FG + (j + 1))
            e.tensor_tensor(h_lo[:, j, :], hb[:, j % 2, :], h_hi[:, j, :], ALU.subtract).then_inc(hlo_done, 1)

        def block(x, side, s):
            for j in range(EX_FG):
                bias(x, s, j)
                if j:
                    low(s, j - 1)
            low(s, EX_FG - 1)
            lower_x(e, s + 1)
            e.wait_ge(y_mm, s + 1 + YMM0)
            e.wait_ge(y_sent, s + YSENT0)
            core.apart(e)
            e.tensor_copy(y[:], ps[:, 5, :]).then_inc(y_ev, 1)

        experts(e, lambda x, side, n, q, m: lower(e, x, side, n, q), block, None)
        for n in range(TOPK * TT):
            i, k = n // TOPK, n % TOPK
            e.wait_ge(back[n % TT], 16 * (n // TT + 1))
            if k:
                e.wait_ge(t_done, n)
            e.scalar_tensor_tensor(out=t[:, i, :], in0=un[:, n % TT, :], scalar=top[:, i, k:k + 1], in1=t[:, i, :],
                                   op0=ALU.mult, op1=ALU.add).then_inc(t_done, 1)

    def lower(e, x, side, n, q):
        e.wait_ge(whi_done, x * EX_PIECES + (n + 1))
        e.tensor_tensor(w_lo[side][:, n, :], raw[q], w_hi[side][:, n, :], ALU.subtract).then_inc(wlo_done, 1)

    def upper(e, x, side, n, q, m):
        e.wait_ge(raw_in[q], (m + 1 + (EX_PIECES // 2 if q < 2 else 0)) * 16)
        e.wait_ge(expert_done, x)
        e.copy(w_hi[side][:, n, :], raw[q]).then_inc(whi_done, 1)

    def lower_x(e, s):
        e.wait_ge(xhi_done, s + 1)
        e.tensor_tensor(x_lo[:], ps[:, 4, :].rearrange("p (k n) -> p k n", k=KD), x_hi[:], ALU.subtract)\
            .then_inc(xlo_done, 1)

    def upper_x(e, s):
        e.wait_ge(turned, s + 1)
        e.copy(x_hi[:], ps[:, 4, :].rearrange("p (k n) -> p k n", k=KD)).then_inc(xhi_done, 1)

    def act(e):
        own = Chain(e, act_own)

        def first_upper(n):
            e.wait_ge(raw_in[n % 2], 16 * (n // 2 + 1))
            e.copy(w_hi[0][:, n, :], raw[n % 2]).then_inc(whi_done, 1)

        e.wait_ge(var_done, 1)
        e.activation(rstd[:], rstd[:], ACT.Sqrt).then_inc(sd_done, 1)
        for i in range(TT):
            e.wait_ge(turned0, i + 1)
            e.copy(hb[:, i % 2, :], ps[:, i % 2, :]).then_inc(copied0, 1)
            if i in EX_FIRST_AT:
                first_upper(EX_FIRST_AT.index(i))
        e.wait_ge(max_done, 1)
        e.activation(pr[:], lg[:], ACT.Exp).then_inc(exp_done, 1)
        for n in range(len(EX_FIRST_AT), EX_PIECES):
            if n == EX_MIX_AT:
                e.wait_ge(mix_turned, 1)
                e.copy(hb[0:E, :, :], ps[0:E, 6:8, :]).then_inc(mix_ev, 1)
            first_upper(n)
        upper_x(e, 0)
        e.wait_ge(table_done, 1)

        def block(x, side, s):
            for j in range(EX_FG):
                e.wait_ge(h_taken, s * EX_FG + (j + 1 + H_TAKEN0))
                if j == 0:
                    e.wait_ge(y_mm, s + YMM0)
                e.activation(hb[:, j % 2, :], hb[:, j % 2, :], ACT.Silu).then_inc(silu_done, 1)
                e.wait_ge(silu_done, s * EX_FG + (j + 1))
                e.copy(h_hi[:, j, :], hb[:, j % 2, :]).then_inc(hhi_done, 1)
            upper_x(e, s + 1)

        experts(e, lambda x, side, n, q, m: upper(e, x, side, n, q, m), block, None)

    def pe(e):
        for i in range(TT + 1):
            if i < TT:
                e.wait_ge(un_done, i + 1)
                if i >= 2:
                    e.wait_ge(copied0, i - 1)
                for k in range(KD):
                    x = e.transpose(ps[:, i % 2, k * P:(k + 1) * P], un[:, i, k * P:(k + 1) * P], core.ident[:])
                x.then_inc(turned0, 1)
            if i == 1:
                e.wait_ge(par_in, PAR)
            if i >= 1:
                e.wait_ge(copied0, i)
                for k in range(KD):
                    x = e.matmul(ps[:, 7, (i - 1) * E:i * E], hb[:, (i - 1) % 2, k * P:(k + 1) * P], gw[:, k, :],
                                 start=(k == 0), stop=(k == KD - 1))
        x.then_inc(logits, 1)
        e.wait_ge(mask_done, 1)
        m2 = mask[:].rearrange("p i x -> p (i x)")
        e.matmul(ps[:, 7, TT * E:2 * TT * E], core.tri[:], m2, start=True, stop=True)
        e.matmul(ps[:, 6, 0:TT * E], core.ones[:], m2, start=True, stop=True).then_inc(ranks, 1)
        e.wait_ge(mix_done, 1)
        for i in range(TT):
            x = e.transpose(ps[0:E, 6 + i // 4, (i % 4) * P:(i % 4 + 1) * P], mask[:, i, :], core.ident[:])
        x.then_inc(mix_turned, 1)
        e.wait_ge(mix_ev, 1)
        for i in range(TT):
            if i >= 4:
                e.wait_ge(b2_done, i - 3)
            e.matmul(ps[:, i % 4, :], hb[0:E, i // 4, (i % 4) * P:(i % 4 + 1) * P], b2[:], start=True, stop=True)\
                .then_inc(b2_mm, 1)
        e.sem_inc(y_mm, YMM0)
        e.sem_inc(expert_done, EXPERT0)

        def turn(s):
            e.wait_ge(xg_in, s * 16 + 16)
            core.apart(e)
            for k in range(KD):
                x = e.transpose(ps[:, 4, k * P:(k + 1) * P], xg[:, k * P:(k + 1) * P], core.ident[:])
            x.then_inc(turned, 1)

        turn(0)
        e.wait_ge(table_done, 1)

        def block(x, side, s):
            e.wait_ge(wlo_done, x * EX_PIECES + KD)
            e.wait_ge(xlo_done, s + 1)
            for j in range(EX_FG):
                e.wait_ge(h_taken, s * EX_FG + (j + 1))
                for c in range(EX_GB):
                    f = j * EX_GB + c
                    for k in range(KD):
                        for m, (a, b) in enumerate(((w_hi, x_hi), (w_hi, x_lo), (w_lo, x_hi))):
                            o = e.matmul(ps[:, j, c * P:(c + 1) * P], a[side][:, k, f * P:(f + 1) * P], b[:, k, :],
                                         start=(k == 0 and m == 0), stop=(k == KD - 1 and m == 2))
                o.then_inc(h_mm, 1)
            turn(s + 1)
            e.wait_ge(wlo_done, x * EX_PIECES + EX_PIECES)
            for j in range(EX_FG):
                e.wait_ge(hlo_done, s * EX_FG + (j + 1 + HLO0))
                if j == 0:
                    e.wait_ge(y_ev, s + YEV0)
                for c in range(EX_GB):
                    for m, (a, b) in enumerate(((h_hi, w_hi), (h_hi, w_lo), (h_lo, w_hi))):
                        o = e.matmul(ps[:, 5, :], a[:, j, c * P:(c + 1) * P], b[side][:, KD + j, c * D:(c + 1) * D],
                                     start=(j == 0 and c == 0 and m == 0), stop=(j == EX_FG - 1 and c == EX_GB - 1 and m == 2))
            o.then_inc(y_mm, 1)

        experts(e, None, block, lambda x: e.drain().then_inc(expert_done, 1))

    def pool(e):
        e.wait_ge(un_done, TT)
        e.wait_ge(table_done, 1)
        for i in range(TT):
            for k in range(TOPK):
                e.indirect_dma_start(out=xs_dram, out_offset=bass.IndirectOffsetOnAxis(ap=slot[:, k, i:i + 1], axis=0),
                                     in_=un[:, i, :], in_offset=None).then_inc(scattered, 16)
        e.wait_ge(scattered, 16 * TT * TOPK)

        def fetch(s):
            e.dma_start(xg[:], xs_dram[ds(s * P, P), :]).then_inc(xg_in, 16)

        fetch(0)
        e.wait_ge(turned, 1)
        fetch(1)
        e.sem_inc(y_sent, YSENT0)

        def block(x, side, s):
            e.wait_ge(turned, s + 2)
            core.apart(e)
            fetch(s + 2)
            e.wait_ge(y_ev, s + 1 + YEV0)
            core.apart(e)
            e.dma_start(ys_dram[ds(s * P, P), :], y[:]).then_inc(y_out, 16)
            e.wait_ge(y_out, s * 16 + 16)
            e.sem_inc(y_sent, 1)

        experts(e, None, block, None)
        total = e.value_load(plan[0:1, 2 * E:2 * E + 1], min_val=TOPK * TT, max_val=FILLED - 2)
        e.wait_ge(y_out, total * 16)
        e.wait_ge(xg_in, total * 16 + 32)
        e.wait_ge(wlo_done, E * EX_PIECES)
        core.apart(e)
        for n in range(TOPK * TT):
            i, k = n // TOPK, n % TOPK
            if n >= TT:
                e.wait_ge(t_done, n - TT + 1)
            e.indirect_dma_start(out=un[:, n % TT, :], out_offset=None, in_=ys_dram[0:(FILLED - 2) * P, :],
                                 in_offset=bass.IndirectOffsetOnAxis(ap=slot[:, k, i:i + 1], axis=0)).then_inc(back[n % TT], 16)

    return dict(sp_ahead=sp_ahead, sp=sp, dve=dve, act=act, pe=pe, pool=pool, cx=cx, used=used)


ENGINES = 5


def program(nc, ins, out):
    with ExitStack() as ctx:
        core = Core(nc, ctx, ins, out)
        ps = ctx.enter_context(nc.psum_tensor("banks", [P, 8, 512], F32))
        stages = []
        before = ctx.enter_context(ExitStack())
        for make in (stage_l01, stage_mamba, stage_ffn, stage_l3, stage_moe):
            core.stage_sems = ctx.enter_context(ExitStack())
            stage = make(core, ps)
            stage["cx"].close()
            before.close()
            before = core.stage_sems
            stages.append(stage)

        def open_stage(e, k):
            if k:
                e.wait_ge(core.stage_end, k * ENGINES)
            if k == 1:
                e.wait_ge(core.consts_in, core.CONSTS)

        block = ctx.enter_context(nc.Block())

        @block.sync
        def _(sp):
            for k, stage in enumerate(stages):
                open_stage(sp, k)
                stage["sp"](sp)
                if k + 1 < len(stages) and "sp_ahead" in stages[k + 1]:
                    stages[k + 1]["sp_ahead"](sp)
                sp.sem_inc(core.stage_end, 1)

        @block.scalar
        def _(act):
            for k, stage in enumerate(stages):
                open_stage(act, k)
                stage["act"](act)
                act.drain().then_inc(core.stage_end, 1)

        @block.vector
        def _(dve):
            for k, stage in enumerate(stages):
                open_stage(dve, k)
                stage["dve"](dve)
                dve.drain().then_inc(core.stage_end, 1)

        @block.gpsimd
        def _(pool):
            for k, stage in enumerate(stages):
                open_stage(pool, k)
                if k:
                    for number in sorted(s.num for s in stages[k - 1]["used"]):
                        pool.sem_clear(range(number, number + 1))
                if stage["pool"]:
                    stage["pool"](pool)
                pool.drain().then_inc(core.stage_end, 1)

        @block.tensor
        def _(pe):
            for k, stage in enumerate(stages):
                open_stage(pe, k)
                stage["pe"](pe)
                pe.drain().then_inc(core.stage_end, 1)


def shape_constants():
    k = np.arange(P)
    c = {"c_ident": np.eye(P, dtype=np.float32),
         "c_tri": (k[:, None] <= k[None, :]).astype(np.float32),
         "c_after": (k[:, None] > k[None, :]).astype(np.float32)}
    c["c_tri16"] = c["c_tri"].astype(np.float16)
    c["c_after16"] = c["c_after"].astype(np.float16)
    c["c_ones"] = np.ones((P, P), np.float32)
    r, j, p = np.arange(H2)[:, None, None], np.arange(JD)[None, :, None], k[None, None, :]
    c["c_sel16"] = (r == 4 * j + p // 32).astype(np.float16)
    c["c_selT"] = (np.arange(H2)[None, None, :] == 4 * j + k[:, None, None] // 32).astype(np.float32)
    per_group = SEQ // GROUPS
    c["c_g16"] = ((k[:, None] // per_group == k[None, :] // per_group) / per_group).astype(np.float32)
    c["c_onesn"] = np.full((P, P), 1 / (per_group * TOK), np.float32)
    signs = np.ones((1, 1))
    while signs.shape[0] < D:
        signs = np.block([[signs, signs], [signs, -signs]])
    c["c_had"] = signs.astype(np.float16)
    c["c_iota"] = np.tile(np.arange(E, dtype=np.float32), (P, 1))
    return c


def laid_out(i):
    x = i["x"].reshape(SEQ, TOK)
    columns = lambda a: a.reshape(LAYERS, -1, P).transpose(0, 2, 1)
    par = np.zeros((LAYERS, P, MB_NPAR), np.float32)
    conv_w, conv_b = i["L2_attn_conv_w"], i["L2_attn_conv_b"]
    par[:, :, MB_LNW:MB_LNW + KD] = columns(i["L2_attn_ln_w"])
    par[:, :, MB_LNB:MB_LNB + KD] = columns(i["L2_attn_ln_b"])
    par[:, :, MB_CVW:MB_CVB] = conv_w[:, :DI].reshape(LAYERS, JD, P, TAPS).transpose(0, 2, 1, 3).reshape(LAYERS, P, -1)
    par[:, :, MB_CVB:MB_BCW] = columns(conv_b[:, :DI])
    par[:, :NS, MB_BCW:MB_BCB] = conv_w[:, DI:].reshape(LAYERS, 2, NS, TAPS).transpose(0, 2, 1, 3).reshape(LAYERS, NS, -1)
    par[:, :NS, MB_BCB:MB_DCOL] = conv_b[:, DI:].reshape(LAYERS, 2, NS).transpose(0, 2, 1)
    par[:, :, MB_DCOL:MB_RMSW] = columns(np.repeat(i["L2_attn_D"], DI // H2, axis=1))
    par[:, :, MB_RMSW:MB_DTB] = columns(i["L2_attn_rms_w"])
    par[:, :, MB_DTB:MB_ALOG] = i["L2_attn_dt_bias"][:, None, :]
    par[:, :, MB_ALOG:] = i["L2_attn_A_log"][:, None, :]
    w1 = i["L3_ffn_w1"].reshape(E, KD, P, EX_F)
    w2 = i["L3_ffn_w2"].reshape(E, EX_FG, EX_GB, P, D).transpose(0, 1, 3, 2, 4).reshape(E, EX_FG, P, EX_F)
    return {
        "x_cm": x, "x_tm": x.T,
        "ln2d_w": i["L0_conv_ln_w"].reshape(TT, P).T, "ln2d_b": i["L0_conv_ln_b"].reshape(TT, P).T,
        "dt_w01": np.stack([np.tile(i["L0_conv_dt_w"][0], 4), np.tile(i["L1_conv_w_dt"][0], 4)], 1),
        "dt_b01": np.stack([np.tile(i["L0_conv_dt_b"], SIDE), np.tile(i["L1_conv_b_dt"], SIDE)], 1),
        "log_A01": np.stack([i["L0_conv_log_A"], i["L1_conv_log_A"]], 1),
        "m_par": par,
        "m_in_w": i["L2_attn_in_proj_w"].transpose(0, 2, 1), "m_out_w": i["L2_attn_out_proj_w"].transpose(0, 2, 1),
        "f_w": i["L2_ffn_weight"],
        "a_nw": i["L3_attn_norm_w"].reshape(KD, P).T, "a_in_b": i["L3_attn_in_proj_b"],
        "a_out_b": i["L3_attn_out_proj_b"], "a_alog": i["L3_attn_A_log"], "a_D": i["L3_attn_D"],
        "a_dtb": i["L3_attn_dt_bias"], "a_in_w": i["L3_attn_in_proj_w"].T, "a_out_w": i["L3_attn_out_proj_w"].T,
        "e_gw": i["L3_ffn_gate_w"].T.reshape(KD, P, E).transpose(1, 0, 2),
        "e_b1": i["L3_ffn_b1"].reshape(E, EX_FB, P).transpose(2, 0, 1), "e_b2": i["L3_ffn_b2"],
        "e_w": np.concatenate([w1, w2], 1).reshape(-1, EX_F)}


def kernel(**inputs):
    import concourse.bacc as bacc
    from concourse.bass_utils import run_bass_kernel_spmd

    arrays = {**shape_constants(), **laid_out({k: np.asarray(v) for k, v in inputs.items()})}
    arrays = {k: np.ascontiguousarray(v) for k, v in arrays.items()}
    nc = bacc.Bacc("TRN2", target_bir_lowering=False, num_devices=1)
    ins = {k: nc.dram_tensor(k, v.shape, mybir.dt.from_np(v.dtype), kind="ExternalInput").ap() for k, v in arrays.items()}
    out = nc.dram_tensor("out", [TOK, D], F32, kind="ExternalOutput").ap()
    program(nc, ins, out)
    result = run_bass_kernel_spmd(nc, [arrays], core_ids=[0]).results[0]["out"]
    return np.ascontiguousarray(np.asarray(result).T).reshape(1, SEQ, SIDE, SIDE)
```
